# Optimizing a Trainium2 kernel written in Bass

```python
import numpy as np
import jax
import jax.numpy as jnp

def _softmax(x, axis=-1):
    return jax.nn.softmax(x, axis=axis)

def _gelu(x):
    return jax.nn.gelu(x, approximate=True)

def _silu(x):
    return jax.nn.silu(x)

def _sigmoid(x):
    return jax.nn.sigmoid(x)

def _layernorm(x, axis=-1, eps=1e-05):
    m = jnp.mean(x, axis=axis, keepdims=True)
    v = jnp.var(x, axis=axis, keepdims=True)
    return (x - m) / jnp.sqrt(v + eps)

def _scatter_add(tgt, idx, src, axis=0):
    return tgt.at[idx].add(src)

def _segment_sum(src, seg, n):
    return jax.ops.segment_sum(src, seg, n)
kernel_name = 'mk_decoder_postln_d2_seqx_r8_a9986c'

def setup_inputs(seed: int=0):
    np.random.seed(seed)
    _w = jnp.asarray

    def _rec_inputs():
        import jax
        import jax.numpy as jnp
        _rk = jax.random.key(seed)
        x = -9.806e-05 + 1 * jax.random.normal(jax.random.fold_in(_rk, 1), (16, 256, 128), jnp.float32)
        _lenS = 256 - jax.random.randint(jax.random.fold_in(_rk, 7), (16,), 0, max(1, 256 // 4) + 1, jnp.int32)
        _lenS2 = 1601 - jax.random.randint(jax.random.fold_in(_rk, 8), (16,), 0, max(1, 1601 // 4) + 1, jnp.int32)
        _ctx_1024P = jax.random.normal(jax.random.fold_in(_rk, 11), (16, 16, 128), jnp.float32)
        _ctx_1024c = jax.random.dirichlet(jax.random.fold_in(_rk, 511), 0.3 * jnp.ones((16,), jnp.float32), (16, 1601))
        _ctx_1024t = jnp.einsum('bsk,bkd->bsd', _ctx_1024c, _ctx_1024P)
        _ctx_1024t = _ctx_1024t * jax.lax.rsqrt(jnp.mean(jnp.square(_ctx_1024t)) + 1e-12) * 0.953939
        ctx_1024 = -1.52775e-05 + 0.999936 * (_ctx_1024t + 0.3 * jax.random.normal(jax.random.fold_in(_rk, 611), (16, 1601, 128), jnp.float32))
        _validS = jnp.arange(256)[None, :] < _lenS[:, None]
        _validS2 = jnp.arange(1601)[None, :] < _lenS2[:, None]
        _causal = jnp.tril(jnp.ones((256, 256), dtype=bool))
        mask_BxS2_bf1 = jnp.ones((16, 1601), dtype=bool)
        return (x, ctx_1024, mask_BxS2_bf1)
    x, ctx_1024, mask_BxS2_bf1 = _rec_inputs()

    def _L0_attn_setup():
        import jax, jax.numpy as jnp
        import numpy as np
        D_MODEL = 128
        N_HEADS = 16
        LATENT_HEADS = 8
        LATENT_DIM = 64
        N_LATENTS = 64
        WINDOW = 32
        HEAD_DIM = D_MODEL // N_HEADS
        LAT_HD = LATENT_DIM // LATENT_HEADS
        B, S = (2, 512)

        def _pool_to_latents(x):
            Bx, Sx, C = x.shape
            chunk = max(1, Sx // N_LATENTS)
            return x.reshape(Bx, N_LATENTS, chunk, C).mean(axis=2)

        def _local_window_attn(Q, K, V):
            Bx, H, Sx, D = Q.shape
            W = WINDOW
            nb = Sx // W
            Qb = Q.reshape(Bx, H, nb, W, D)
            Kp = jnp.pad(K, ((0, 0), (0, 0), (W, 0), (0, 0))).reshape(Bx, H, nb + 1, W, D)
            Vp = jnp.pad(V, ((0, 0), (0, 0), (W, 0), (0, 0))).reshape(Bx, H, nb + 1, W, D)
            Kw = jnp.concatenate([Kp[:, :, :-1], Kp[:, :, 1:]], axis=3)
            Vw = jnp.concatenate([Vp[:, :, :-1], Vp[:, :, 1:]], axis=3)
            i = jnp.arange(W)[:, None]
            j = jnp.arange(2 * W)[None, :]
            base = (j > i) & (j <= i + W)
            blk0 = (jnp.arange(nb) > 0)[:, None, None] | (j >= W)[None, :, :]
            mask = base[None, :, :] & blk0
            sc = jnp.einsum('bhnid,bhnjd->bhnij', Qb, Kw) / np.sqrt(D).astype(np.float32)
            sc = jnp.where(mask[None, None], sc, -jnp.inf)
            p = jax.nn.softmax(sc, axis=-1)
            out = jnp.einsum('bhnij,bhnjd->bhnid', p, Vw)
            return out.reshape(Bx, H, Sx, D)
        key = jax.random.key(seed)
        ks = jax.random.split(key, 11)
        std = 0.02
        w = lambda k, shp: jax.random.normal(k, shp, jnp.float32) * std
        return {'x': jax.random.normal(ks[0], (B, S, D_MODEL), jnp.float32), 'wq': w(ks[1], (D_MODEL, D_MODEL)), 'wk': w(ks[2], (D_MODEL, D_MODEL)), 'wv': w(ks[3], (D_MODEL, D_MODEL)), 'wgq': w(ks[4], (D_MODEL, LATENT_DIM)), 'wgk': w(ks[5], (D_MODEL, LATENT_DIM)), 'wgv': w(ks[6], (D_MODEL, LATENT_DIM)), 'r_out_w': w(ks[7], (LATENT_DIM, D_MODEL)), 'gate_local_w': w(ks[8], (N_HEADS, HEAD_DIM)), 'gate_remote_w': w(ks[9], (N_HEADS, HEAD_DIM)), 'w_out': w(ks[10], (D_MODEL, D_MODEL))}
    _L0_attn_all = _L0_attn_setup()
    _L0_attn_in = {k: v for k, v in _L0_attn_all.items() if k in ('wq', 'wk', 'wv', 'wgq', 'wgk', 'wgv', 'r_out_w', 'gate_local_w', 'gate_remote_w', 'w_out')}
    del _L0_attn_all

    def _L0_xattn_setup():
        import jax, jax.numpy as jnp
        import numpy as np
        D = 128
        NUM_ITERS = 3
        EPS = 1e-06
        SCALE = D ** (-0.5)

        def rmsnorm(x, w, eps=EPS):
            return x * jax.lax.rsqrt(jnp.mean(x * x, axis=-1, keepdims=True) + eps) * w

        def gru_cell(x, h, wih, whh, bih, bhh):
            gx = x @ wih.T + bih
            gh = h @ whh.T + bhh
            xr, xz, xn = jnp.split(gx, 3, axis=-1)
            hr, hz, hn = jnp.split(gh, 3, axis=-1)
            r = jax.nn.sigmoid(xr + hr)
            z = jax.nn.sigmoid(xz + hz)
            n = jnp.tanh(xn + r * hn)
            return (1.0 - z) * n + z * h
        key = jax.random.key(seed)
        ks = jax.random.split(key, 8)
        B, K, M, d = (8, 64, 512, D)
        w_std = d ** (-0.5)
        return {'slots': jax.random.normal(ks[0], (B, K, d), jnp.float32), 'P': jax.random.normal(ks[1], (B, M, d), jnp.float32), 'Wq': jax.random.normal(ks[2], (d, d), jnp.float32) * w_std, 'Wk': jax.random.normal(ks[3], (d, d), jnp.float32) * w_std, 'Wv': jax.random.normal(ks[4], (d, d), jnp.float32) * w_std, 'gru_wih': jax.random.normal(ks[5], (3 * d, d), jnp.float32) * w_std, 'gru_whh': jax.random.normal(ks[6], (3 * d, d), jnp.float32) * w_std, 'gru_bih': jnp.zeros((3 * d,), jnp.float32), 'gru_bhh': jnp.zeros((3 * d,), jnp.float32), 'slot_norm_w': jnp.ones((d,), jnp.float32), 'input_norm_w': jnp.ones((d,), jnp.float32)}
    _L0_xattn_all = _L0_xattn_setup()
    _L0_xattn_in = {k: v for k, v in _L0_xattn_all.items() if k in ('Wq', 'Wk', 'Wv', 'gru_wih', 'gru_whh', 'gru_bih', 'gru_bhh', 'slot_norm_w', 'input_norm_w')}
    del _L0_xattn_all

    def _L0_ffn_setup():
        import jax, jax.numpy as jnp
        import numpy as np
        B, T, DIM = (2, 256, 128)
        H, DH, E, K = (16, 64, 8, 2)
        key = jax.random.key(seed)
        ks = jax.random.split(key, 7)
        s = 0.02
        return {'x': jax.random.normal(ks[0], (B, T, DIM), jnp.float32), 'Wq': jax.random.normal(ks[1], (H, DH, DIM), jnp.float32) * s, 'Wk': jax.random.normal(ks[2], (H, DH, DIM), jnp.float32) * s, 'Wv': jax.random.normal(ks[3], (E, DH, DIM), jnp.float32) * s, 'Ws': jax.random.normal(ks[4], (H, E, DIM), jnp.float32) * s, 'Wd': jax.random.normal(ks[5], (H, E, DIM), jnp.float32) * s, 'Wo': jax.random.normal(ks[6], (E, DIM, DH), jnp.float32) * s}
    _L0_ffn_all = _L0_ffn_setup()
    _L0_ffn_in = {k: v for k, v in _L0_ffn_all.items() if k in ('Wq', 'Wk', 'Wv', 'Ws', 'Wd', 'Wo')}
    del _L0_ffn_all

    def _L1_attn_setup():
        import jax, jax.numpy as jnp
        import numpy as np
        D_MODEL, D_STATE, EXPAND = (128, 16, 2)
        D_INNER = D_MODEL * EXPAND
        BATCH, SEQ = (2, 256)

        def _block_fwd(x, W_in, b_in, A_log, W_B, b_B, W_C, b_C, W_delta, b_delta, D_param, W_out, b_out):
            h = jax.nn.selu(jnp.einsum('bld,di->bli', x, W_in) + b_in)
            delta = jax.nn.softplus(jnp.einsum('bli,ij->blj', h, W_delta) + b_delta)
            Bm = jnp.einsum('bli,in->bln', h, W_B) + b_B
            Cm = jnp.einsum('bli,in->bln', h, W_C) + b_C
            A = -jnp.exp(A_log)

            def step(s, inp):
                dt, bt, ct, ht = inp
                dA = jnp.exp(dt[:, :, None] * A)
                dB = dt[:, :, None] * bt[:, None, :]
                s = dA * s + dB * ht[:, :, None]
                y = jnp.einsum('bdn,bn->bd', s, ct)
                return (s, y)
            s0 = jnp.zeros((h.shape[0], h.shape[2], A.shape[1]), dtype=h.dtype)
            xs = (jnp.swapaxes(delta, 0, 1), jnp.swapaxes(Bm, 0, 1), jnp.swapaxes(Cm, 0, 1), jnp.swapaxes(h, 0, 1))
            _, ys = jax.lax.scan(step, s0, xs)
            y = jnp.swapaxes(ys, 0, 1) + h * D_param
            return jnp.einsum('bli,id->bld', y, W_out) + b_out
        key = jax.random.key(seed)
        ks = jax.random.split(key, 13)
        s = 0.02
        return {'x': jax.random.normal(ks[0], (BATCH, SEQ, D_MODEL), dtype=jnp.float32), 'W_in': jax.random.normal(ks[1], (D_MODEL, D_INNER), dtype=jnp.float32) * s, 'b_in': jnp.zeros((D_INNER,), dtype=jnp.float32), 'A_log': jax.random.normal(ks[2], (D_INNER, D_STATE), dtype=jnp.float32) * 0.1, 'W_B': jax.random.normal(ks[3], (D_INNER, D_STATE), dtype=jnp.float32) * s, 'b_B': jnp.zeros((D_STATE,), dtype=jnp.float32), 'W_C': jax.random.normal(ks[4], (D_INNER, D_STATE), dtype=jnp.float32) * s, 'b_C': jnp.zeros((D_STATE,), dtype=jnp.float32), 'W_delta': jax.random.normal(ks[5], (D_INNER, D_INNER), dtype=jnp.float32) * s, 'b_delta': jnp.zeros((D_INNER,), dtype=jnp.float32), 'D_param': jnp.ones((D_INNER,), dtype=jnp.float32), 'W_out': jax.random.normal(ks[6], (D_INNER, D_MODEL), dtype=jnp.float32) * s, 'b_out': jnp.zeros((D_MODEL,), dtype=jnp.float32)}
    _L1_attn_all = _L1_attn_setup()
    _L1_attn_in = {k: v for k, v in _L1_attn_all.items() if k in ('W_in', 'b_in', 'A_log', 'W_B', 'b_B', 'W_C', 'b_C', 'W_delta', 'b_delta', 'D_param', 'W_out', 'b_out')}
    del _L1_attn_all

    def _L1_xattn_setup():
        import jax, jax.numpy as jnp
        import numpy as np
        H, DH = (8, 64)
        EPS = 1e-05

        def _ln(x, g, b):
            m = x.mean(-1, keepdims=True)
            v = ((x - m) ** 2).mean(-1, keepdims=True)
            return (x - m) / jnp.sqrt(v + EPS) * g + b
        key = jax.random.key(seed)
        ks = jax.random.split(key, 5)
        B, N, L, D = (4, 1024, 64, 128)
        inner = H * DH
        return {'x': jax.random.normal(ks[0], (B, N, D), jnp.float32), 'latents': jax.random.normal(ks[1], (B, L, D), jnp.float32), 'mask': jnp.ones((B, N), dtype=bool), 'g_x': jnp.ones((D,), jnp.float32), 'b_x': jnp.zeros((D,), jnp.float32), 'g_l': jnp.ones((D,), jnp.float32), 'b_l': jnp.zeros((D,), jnp.float32), 'w_q': jax.random.normal(ks[2], (D, inner), jnp.float32) * D ** (-0.5), 'w_kv': jax.random.normal(ks[3], (D, 2 * inner), jnp.float32) * D ** (-0.5), 'w_out': jax.random.normal(ks[4], (inner, D), jnp.float32) * inner ** (-0.5), 'g_o': jnp.ones((D,), jnp.float32), 'b_o': jnp.zeros((D,), jnp.float32)}
    _L1_xattn_all = _L1_xattn_setup()
    _L1_xattn_in = {k: v for k, v in _L1_xattn_all.items() if k in ('g_x', 'b_x', 'g_l', 'b_l', 'w_q', 'w_kv', 'w_out', 'g_o', 'b_o')}
    del _L1_xattn_all

    def _L1_ffn_setup():
        import jax, jax.numpy as jnp
        import numpy as np
        B, S, D, E = (4, 512, 128, 8)
        key = jax.random.key(seed)
        k1, k2, k3, k4, k5 = jax.random.split(key, 5)
        scale = 1.0 / np.sqrt(D)
        return {'x': jax.random.normal(k1, (B, S, D), dtype=jnp.float32), 'Wg': jax.random.normal(k2, (D, D), dtype=jnp.float32) * scale, 'bg': jnp.zeros((D,), dtype=jnp.float32), 'We': jax.random.normal(k3, (E, D, D), dtype=jnp.float32) * scale, 'be': jnp.zeros((E, D), dtype=jnp.float32)}
    _L1_ffn_all = _L1_ffn_setup()
    _L1_ffn_in = {k: v for k, v in _L1_ffn_all.items() if k in ('Wg', 'bg', 'We', 'be')}
    del _L1_ffn_all
    return {'x': x, 'ctx_1024': ctx_1024, 'mask_BxS2_bf1': mask_BxS2_bf1, 'L0_attn_wq': _L0_attn_in['wq'], 'L0_attn_wk': _L0_attn_in['wk'], 'L0_attn_wv': _L0_attn_in['wv'], 'L0_attn_wgq': _L0_attn_in['wgq'], 'L0_attn_wgk': _L0_attn_in['wgk'], 'L0_attn_wgv': _L0_attn_in['wgv'], 'L0_attn_r_out_w': _L0_attn_in['r_out_w'], 'L0_attn_gate_local_w': _L0_attn_in['gate_local_w'], 'L0_attn_gate_remote_w': _L0_attn_in['gate_remote_w'], 'L0_attn_w_out': _L0_attn_in['w_out'], 'L0_xattn_Wq': _L0_xattn_in['Wq'], 'L0_xattn_Wk': _L0_xattn_in['Wk'], 'L0_xattn_Wv': _L0_xattn_in['Wv'], 'L0_xattn_gru_wih': _L0_xattn_in['gru_wih'], 'L0_xattn_gru_whh': _L0_xattn_in['gru_whh'], 'L0_xattn_gru_bih': _L0_xattn_in['gru_bih'], 'L0_xattn_gru_bhh': _L0_xattn_in['gru_bhh'], 'L0_xattn_slot_norm_w': _L0_xattn_in['slot_norm_w'], 'L0_xattn_input_norm_w': _L0_xattn_in['input_norm_w'], 'L0_ffn_Wq': _L0_ffn_in['Wq'], 'L0_ffn_Wk': _L0_ffn_in['Wk'], 'L0_ffn_Wv': _L0_ffn_in['Wv'], 'L0_ffn_Ws': _L0_ffn_in['Ws'], 'L0_ffn_Wd': _L0_ffn_in['Wd'], 'L0_ffn_Wo': _L0_ffn_in['Wo'], 'L1_attn_W_in': _L1_attn_in['W_in'], 'L1_attn_b_in': _L1_attn_in['b_in'], 'L1_attn_A_log': _L1_attn_in['A_log'], 'L1_attn_W_B': _L1_attn_in['W_B'], 'L1_attn_b_B': _L1_attn_in['b_B'], 'L1_attn_W_C': _L1_attn_in['W_C'], 'L1_attn_b_C': _L1_attn_in['b_C'], 'L1_attn_W_delta': _L1_attn_in['W_delta'], 'L1_attn_b_delta': _L1_attn_in['b_delta'], 'L1_attn_D_param': _L1_attn_in['D_param'], 'L1_attn_W_out': _L1_attn_in['W_out'], 'L1_attn_b_out': _L1_attn_in['b_out'], 'L1_xattn_g_x': _L1_xattn_in['g_x'], 'L1_xattn_b_x': _L1_xattn_in['b_x'], 'L1_xattn_g_l': _L1_xattn_in['g_l'], 'L1_xattn_b_l': _L1_xattn_in['b_l'], 'L1_xattn_w_q': _L1_xattn_in['w_q'], 'L1_xattn_w_kv': _L1_xattn_in['w_kv'], 'L1_xattn_w_out': _L1_xattn_in['w_out'], 'L1_xattn_g_o': _L1_xattn_in['g_o'], 'L1_xattn_b_o': _L1_xattn_in['b_o'], 'L1_ffn_Wg': _L1_ffn_in['Wg'], 'L1_ffn_bg': _L1_ffn_in['bg'], 'L1_ffn_We': _L1_ffn_in['We'], 'L1_ffn_be': _L1_ffn_in['be']}

def reference(x, ctx_1024, mask_BxS2_bf1, L0_attn_wq, L0_attn_wk, L0_attn_wv, L0_attn_wgq, L0_attn_wgk, L0_attn_wgv, L0_attn_r_out_w, L0_attn_gate_local_w, L0_attn_gate_remote_w, L0_attn_w_out, L0_xattn_Wq, L0_xattn_Wk, L0_xattn_Wv, L0_xattn_gru_wih, L0_xattn_gru_whh, L0_xattn_gru_bih, L0_xattn_gru_bhh, L0_xattn_slot_norm_w, L0_xattn_input_norm_w, L0_ffn_Wq, L0_ffn_Wk, L0_ffn_Wv, L0_ffn_Ws, L0_ffn_Wd, L0_ffn_Wo, L1_attn_W_in, L1_attn_b_in, L1_attn_A_log, L1_attn_W_B, L1_attn_b_B, L1_attn_W_C, L1_attn_b_C, L1_attn_W_delta, L1_attn_b_delta, L1_attn_D_param, L1_attn_W_out, L1_attn_b_out, L1_xattn_g_x, L1_xattn_b_x, L1_xattn_g_l, L1_xattn_b_l, L1_xattn_w_q, L1_xattn_w_kv, L1_xattn_w_out, L1_xattn_g_o, L1_xattn_b_o, L1_ffn_Wg, L1_ffn_bg, L1_ffn_We, L1_ffn_be):
    import jax
    import jax.numpy as jnp

    def _L0_attn_ref(x, wq, wk, wv, wgq, wgk, wgv, r_out_w, gate_local_w, gate_remote_w, w_out):
        import jax, jax.numpy as jnp
        import numpy as np
        D_MODEL = 128
        N_HEADS = 16
        LATENT_HEADS = 8
        LATENT_DIM = 64
        N_LATENTS = 64
        WINDOW = 32
        HEAD_DIM = D_MODEL // N_HEADS
        LAT_HD = LATENT_DIM // LATENT_HEADS
        B, S = (2, 512)

        def _pool_to_latents(x):
            Bx, Sx, C = x.shape
            chunk = max(1, Sx // N_LATENTS)
            return x.reshape(Bx, N_LATENTS, chunk, C).mean(axis=2)

        def _local_window_attn(Q, K, V):
            Bx, H, Sx, D = Q.shape
            W = WINDOW
            nb = Sx // W
            Qb = Q.reshape(Bx, H, nb, W, D)
            Kp = jnp.pad(K, ((0, 0), (0, 0), (W, 0), (0, 0))).reshape(Bx, H, nb + 1, W, D)
            Vp = jnp.pad(V, ((0, 0), (0, 0), (W, 0), (0, 0))).reshape(Bx, H, nb + 1, W, D)
            Kw = jnp.concatenate([Kp[:, :, :-1], Kp[:, :, 1:]], axis=3)
            Vw = jnp.concatenate([Vp[:, :, :-1], Vp[:, :, 1:]], axis=3)
            i = jnp.arange(W)[:, None]
            j = jnp.arange(2 * W)[None, :]
            base = (j > i) & (j <= i + W)
            blk0 = (jnp.arange(nb) > 0)[:, None, None] | (j >= W)[None, :, :]
            mask = base[None, :, :] & blk0
            sc = jnp.einsum('bhnid,bhnjd->bhnij', Qb, Kw) / np.sqrt(D).astype(np.float32)
            sc = jnp.where(mask[None, None], sc, -jnp.inf)
            p = jax.nn.softmax(sc, axis=-1)
            out = jnp.einsum('bhnij,bhnjd->bhnid', p, Vw)
            return out.reshape(Bx, H, Sx, D)
        Bx, Sx, _ = x.shape
        chunk = max(1, Sx // N_LATENTS)
        Q = (x @ wq).reshape(Bx, Sx, N_HEADS, HEAD_DIM).transpose(0, 2, 1, 3)
        K = (x @ wk).reshape(Bx, Sx, N_HEADS, HEAD_DIM).transpose(0, 2, 1, 3)
        V = (x @ wv).reshape(Bx, Sx, N_HEADS, HEAD_DIM).transpose(0, 2, 1, 3)
        local = _local_window_attn(Q, K, V)
        GQ = (x @ wgq).reshape(Bx, Sx, LATENT_HEADS, LAT_HD).transpose(0, 2, 1, 3)
        GK = _pool_to_latents(x @ wgk).reshape(Bx, N_LATENTS, LATENT_HEADS, LAT_HD).transpose(0, 2, 1, 3)
        GV = _pool_to_latents(x @ wgv).reshape(Bx, N_LATENTS, LATENT_HEADS, LAT_HD).transpose(0, 2, 1, 3)
        lsc = jnp.einsum('bhsd,bhnd->bhsn', GQ, GK) / np.sqrt(LAT_HD).astype(np.float32)
        lmask = jnp.arange(N_LATENTS)[None, :] <= (jnp.arange(Sx) // chunk)[:, None]
        lsc = jnp.where(lmask[None, None], lsc, -jnp.inf)
        lp = jax.nn.softmax(lsc, axis=-1)
        rem = jnp.einsum('bhsn,bhnd->bhsd', lp, GV)
        rem = rem.transpose(0, 2, 1, 3).reshape(Bx, Sx, LATENT_DIM) @ r_out_w
        rem = rem.reshape(Bx, Sx, N_HEADS, HEAD_DIM).transpose(0, 2, 1, 3)
        gl = jax.nn.sigmoid(jnp.einsum('bhsd,hd->bhs', Q, gate_local_w))[..., None]
        gr = jax.nn.sigmoid(jnp.einsum('bhsd,hd->bhs', Q, gate_remote_w))[..., None]
        out = gl * local + gr * rem
        out = out.transpose(0, 2, 1, 3).reshape(Bx, Sx, D_MODEL)
        return out @ w_out

    def _L0_xattn_ref(slots, P, Wq, Wk, Wv, gru_wih, gru_whh, gru_bih, gru_bhh, slot_norm_w, input_norm_w):
        import jax, jax.numpy as jnp
        import numpy as np
        D = 128
        NUM_ITERS = 3
        EPS = 1e-06
        SCALE = D ** (-0.5)

        def rmsnorm(x, w, eps=EPS):
            return x * jax.lax.rsqrt(jnp.mean(x * x, axis=-1, keepdims=True) + eps) * w

        def gru_cell(x, h, wih, whh, bih, bhh):
            gx = x @ wih.T + bih
            gh = h @ whh.T + bhh
            xr, xz, xn = jnp.split(gx, 3, axis=-1)
            hr, hz, hn = jnp.split(gh, 3, axis=-1)
            r = jax.nn.sigmoid(xr + hr)
            z = jax.nn.sigmoid(xz + hz)
            n = jnp.tanh(xn + r * hn)
            return (1.0 - z) * n + z * h
        Pn = rmsnorm(P, input_norm_w)
        k_proj = Pn @ Wk.T
        v_proj = Pn @ Wv.T
        for _ in range(NUM_ITERS):
            sn = rmsnorm(slots, slot_norm_w)
            q_proj = sn @ Wq.T
            scores = jnp.einsum('bkd,bmd->bkm', q_proj, k_proj) * SCALE
            attn = jax.nn.softmax(scores, axis=-2)
            attn = attn / (jnp.sum(attn, axis=-1, keepdims=True) + EPS)
            updates = jnp.einsum('bkm,bmd->bkd', attn, v_proj)
            slots = gru_cell(updates, slots, gru_wih, gru_whh, gru_bih, gru_bhh)
        return slots

    def _L0_ffn_ref(x, Wq, Wk, Wv, Ws, Wd, Wo):
        import jax, jax.numpy as jnp
        import numpy as np
        B, T, DIM = (2, 256, 128)
        H, DH, E, K = (16, 64, 8, 2)
        scale = DH ** (-0.5)
        q = jnp.einsum('btc,hdc->bhtd', x, Wq)
        k = jnp.einsum('btc,hdc->bhtd', x, Wk)
        gate_v = jnp.einsum('btc,hec->bthe', x, Ws)
        w, sel = jax.lax.top_k(gate_v, K)
        wsig = jax.nn.sigmoid(w)
        oh = jax.nn.one_hot(sel, E, dtype=x.dtype)
        mix_v = jnp.einsum('bthk,bthke->bthe', wsig, oh)
        proj_v = jnp.einsum('btc,edc->bted', x, Wv)
        v = jnp.einsum('bthe,bted->bhtd', mix_v, proj_v)
        scores = jnp.einsum('bhid,bhjd->bhij', q * scale, k)
        probs = jax.nn.softmax(scores, axis=-1)
        attn = jnp.einsum('bhij,bhjd->bihd', probs, v)
        gate_o = jnp.einsum('btc,hec->bthe', x, Wd)
        _, sel_o = jax.lax.top_k(gate_o, K)
        mask_o = jax.nn.one_hot(sel_o, E, dtype=x.dtype).sum(axis=3)
        res = jnp.einsum('bthe,bthd,efd->bthf', mask_o, attn, Wo)
        return res.sum(axis=2)

    def _L1_attn_ref(x, W_in, b_in, A_log, W_B, b_B, W_C, b_C, W_delta, b_delta, D_param, W_out, b_out):
        import jax, jax.numpy as jnp
        import numpy as np
        D_MODEL, D_STATE, EXPAND = (128, 16, 2)
        D_INNER = D_MODEL * EXPAND
        BATCH, SEQ = (2, 256)

        def _block_fwd(x, W_in, b_in, A_log, W_B, b_B, W_C, b_C, W_delta, b_delta, D_param, W_out, b_out):
            h = jax.nn.selu(jnp.einsum('bld,di->bli', x, W_in) + b_in)
            delta = jax.nn.softplus(jnp.einsum('bli,ij->blj', h, W_delta) + b_delta)
            Bm = jnp.einsum('bli,in->bln', h, W_B) + b_B
            Cm = jnp.einsum('bli,in->bln', h, W_C) + b_C
            A = -jnp.exp(A_log)

            def step(s, inp):
                dt, bt, ct, ht = inp
                dA = jnp.exp(dt[:, :, None] * A)
                dB = dt[:, :, None] * bt[:, None, :]
                s = dA * s + dB * ht[:, :, None]
                y = jnp.einsum('bdn,bn->bd', s, ct)
                return (s, y)
            s0 = jnp.zeros((h.shape[0], h.shape[2], A.shape[1]), dtype=h.dtype)
            xs = (jnp.swapaxes(delta, 0, 1), jnp.swapaxes(Bm, 0, 1), jnp.swapaxes(Cm, 0, 1), jnp.swapaxes(h, 0, 1))
            _, ys = jax.lax.scan(step, s0, xs)
            y = jnp.swapaxes(ys, 0, 1) + h * D_param
            return jnp.einsum('bli,id->bld', y, W_out) + b_out
        return _block_fwd(x, W_in, b_in, A_log, W_B, b_B, W_C, b_C, W_delta, b_delta, D_param, W_out, b_out)

    def _L1_xattn_ref(x, latents, mask, g_x, b_x, g_l, b_l, w_q, w_kv, w_out, g_o, b_o):
        import jax, jax.numpy as jnp
        import numpy as np
        H, DH = (8, 64)
        EPS = 1e-05

        def _ln(x, g, b):
            m = x.mean(-1, keepdims=True)
            v = ((x - m) ** 2).mean(-1, keepdims=True)
            return (x - m) / jnp.sqrt(v + EPS) * g + b
        B, Lq = (latents.shape[0], latents.shape[1])
        scale = DH ** (-0.5)
        xn = _ln(x, g_x, b_x)
        ln = _ln(latents, g_l, b_l)
        q = ln @ w_q
        kv_in = jnp.concatenate([xn, ln], axis=1)
        k, v = jnp.split(kv_in @ w_kv, 2, axis=-1)
        split = lambda t: t.reshape(t.shape[0], t.shape[1], H, DH).transpose(0, 2, 1, 3)
        q, k, v = (split(q) * scale, split(k), split(v))
        sim = jnp.einsum('bhid,bhjd->bhij', q, k)
        m = jnp.concatenate([mask, jnp.ones((B, Lq), dtype=bool)], axis=1)[:, None, None, :]
        sim = jnp.where(m, sim, -jnp.finfo(sim.dtype).max)
        attn = jax.nn.softmax(sim, axis=-1)
        out = jnp.einsum('bhij,bhjd->bhid', attn, v)
        out = out.transpose(0, 2, 1, 3).reshape(B, Lq, H * DH)
        return _ln(out @ w_out, g_o, b_o)

    def _L1_ffn_ref(x, Wg, bg, We, be):
        import jax, jax.numpy as jnp
        import numpy as np
        B, S, D, E = (4, 512, 128, 8)
        probs = jax.nn.softmax(x @ Wg + bg, axis=-1)
        idx = jnp.argmax(probs, axis=-1)
        p = jnp.take_along_axis(probs, idx[..., None], axis=-1)[..., 0]
        e_idx = idx % We.shape[0]
        h = jax.nn.relu(jnp.einsum('bsd,edf->besf', x, We) + be[None, :, None, :])
        onehot = jax.nn.one_hot(e_idx, We.shape[0], dtype=x.dtype)
        out = jnp.einsum('besf,bse->bsf', h, onehot) * p[..., None]
        return out
    x = _layernorm(x + _L0_attn_ref(x, L0_attn_wq, L0_attn_wk, L0_attn_wv, L0_attn_wgq, L0_attn_wgk, L0_attn_wgv, L0_attn_r_out_w, L0_attn_gate_local_w, L0_attn_gate_remote_w, L0_attn_w_out), axis=-1)
    x = _layernorm(x + _L0_xattn_ref(x, ctx_1024, L0_xattn_Wq, L0_xattn_Wk, L0_xattn_Wv, L0_xattn_gru_wih, L0_xattn_gru_whh, L0_xattn_gru_bih, L0_xattn_gru_bhh, L0_xattn_slot_norm_w, L0_xattn_input_norm_w), axis=-1)
    x = _layernorm(x + _L0_ffn_ref(x, L0_ffn_Wq, L0_ffn_Wk, L0_ffn_Wv, L0_ffn_Ws, L0_ffn_Wd, L0_ffn_Wo), axis=-1)
    x = _layernorm(x + _L1_attn_ref(x, L1_attn_W_in, L1_attn_b_in, L1_attn_A_log, L1_attn_W_B, L1_attn_b_B, L1_attn_W_C, L1_attn_b_C, L1_attn_W_delta, L1_attn_b_delta, L1_attn_D_param, L1_attn_W_out, L1_attn_b_out), axis=-1)
    x = _layernorm(x + _L1_xattn_ref(ctx_1024, x, mask_BxS2_bf1, L1_xattn_g_x, L1_xattn_b_x, L1_xattn_g_l, L1_xattn_b_l, L1_xattn_w_q, L1_xattn_w_kv, L1_xattn_w_out, L1_xattn_g_o, L1_xattn_b_o), axis=-1)
    x = _layernorm(x + _L1_ffn_ref(x, L1_ffn_Wg, L1_ffn_bg, L1_ffn_We, L1_ffn_be), axis=-1)
    return x

_drawn_inputs = setup_inputs


def setup_inputs(seed=0):
    import zlib

    import numpy as np

    out = dict(_drawn_inputs(seed))
    spreads = {'L0_xattn_gru_bih': (0.0, 0.1),
     'L0_xattn_gru_bhh': (0.0, 0.293),
     'L0_xattn_slot_norm_w': (1.0, 0.6),
     'L0_xattn_input_norm_w': (1.0, 0.2),
     'L1_attn_b_in': (0.0, 0.1),
     'L1_attn_b_B': (0.0, 0.8),
     'L1_attn_b_C': (0.0, 0.8),
     'L1_attn_b_delta': (0.0, 0.8),
     'L1_attn_D_param': (1.0, 0.6),
     'L1_attn_b_out': (0.0, 0.1),
     'L1_xattn_g_x': (1.0, 0.2),
     'L1_xattn_b_x': (0.0, 0.1),
     'L1_xattn_g_l': (1.0, 0.2),
     'L1_xattn_b_l': (0.0, 0.1),
     'L1_xattn_g_o': (1.0, 0.2),
     'L1_xattn_b_o': (0.0, 0.1),
     'L1_ffn_bg': (0.0, 0.514),
     'L1_ffn_be': (0.0, 0.8)}
    factors = {'L0_attn_wq': 8.0,
     'L0_attn_wk': 8.0,
     'L0_attn_wv': 8.0,
     'L0_attn_wgq': 8.0,
     'L0_attn_wgk': 8.0,
     'L0_attn_wgv': 8.0,
     'L0_attn_r_out_w': 8.0,
     'L0_attn_gate_local_w': 8.0,
     'L0_attn_gate_remote_w': 8.0,
     'L0_attn_w_out': 8.0,
     'L0_ffn_Wq': 8.0,
     'L0_ffn_Wk': 8.0,
     'L0_ffn_Ws': 4.481,
     'L0_ffn_Wd': 2.908,
     'L1_attn_A_log': 8.0,
     'L1_attn_W_B': 8.0,
     'L1_attn_W_C': 8.0,
     'L1_attn_W_delta': 8.0}
    for name, (base, spread) in spreads.items():
        noise = np.random.default_rng([zlib.crc32(name.encode()), seed]).standard_normal(out[name].shape)
        drawn = base * np.exp(spread * noise) if base else spread * noise
        out[name] = jnp.asarray(drawn.astype(out[name].dtype))
    for name, factor in factors.items():
        out[name] = (out[name] * factor).astype(out[name].dtype)
    return out
```

```python
import concourse.bass as bass
from concourse import mybir
from contextlib import ExitStack

F32 = mybir.dt.float32
BF16 = mybir.dt.bfloat16
U8 = mybir.dt.uint8
ACT = mybir.ActivationFunctionType
ALU = mybir.AluOpType
AX = mybir.AxisListType

B, S, D = 16, 256, 128
SC = 1601
P = 128
LANES = (0, 1)
TT = S // P
NEG = -1e30
BANK = 512


class Marks:

    def __init__(self, make, known):
        self.known = known
        self.count, self.place = {}, {}
        keys = sorted(known.count) if known else []
        self.make = make
        self.sems = {key: make("_".join(map(str, key))) for key in keys if key[0] != "setup"}
        self.round_sems = list(self.sems.values())
        self.sems.update({key: make("_".join(map(str, key))) for key in keys if key[0] == "setup"})
        self.dry = None if known else make("dry")

    def done(self, engine, name, lane=0):
        key = (name.split(".")[0], engine, lane)
        self.count[key] = self.count.get(key, 0) + 1
        assert (name, lane) not in self.place, name
        self.place[name, lane] = (key, self.count[key])
        return self.sems.get(key, self.dry), 1

    def at(self, name, lane=0):
        if self.known is None:
            return self.dry, 1
        key, value = self.known.place[name, lane]
        return self.sems[key], value


def build(nc, w, out, known, rounds):
    ctx = ExitStack()
    with ctx:
        def sb(name, shape, dt=F32):
            return ctx.enter_context(nc.sbuf_tensor(name, shape, dt))

        def sem(name):
            return ctx.enter_context(nc.semaphore(name))

        s_x = [sem(f"x_loaded{u}") for u in LANES]
        s_ctx = [sem(f"context_loaded{u}") for u in LANES]
        s_mask = [sem(f"mask_loaded{u}") for u in LANES]
        s_out = sem("x_stored")
        s_round_done = sem("round_done")
        marks = Marks(sem, known)
        round_sems = [*s_x, *s_ctx, *s_mask, s_out, s_round_done, *marks.round_sems]
        cleared = range(round_sems[0].num, round_sems[-1].num + 1)
        assert [s.num for s in round_sems] == list(cleared)
        at, done = marks.at, marks.done

        ps = [ctx.enter_context(nc.psum_tensor(f"ps{u}", [P, 4, BANK], F32)) for u in LANES]

        ident = sb("ident", [P, P])
        ones_row = sb("ones_row", [1, P])
        eps6 = sb("eps6", [P, 1])
        head_of = sb("head_of", [P, 16])
        head_mod = sb("head_mod", [P, 4])
        X = [sb(f"X{u}", [P, TT, P]) for u in LANES]
        XT = [sb(f"XT{u}", [P, S]) for u in LANES]
        lnt = [sb(f"lnt{u}", [P, 32]) for u in LANES]
        res = [sb(f"res{u}", [P, TT, P]) for u in LANES]
        AREA = 15760
        area = [sb(f"area{u}", [P, AREA]) for u in LANES]

        class Carve:

            def __init__(self, u, start=0):
                self.u, self.at = u, start

            def __call__(self, *shape):
                n = 1
                for s in shape:
                    n *= s
                a = area[self.u][:, self.at:self.at + n]
                self.at += n
                assert self.at <= AREA, self.at
                if len(shape) == 1:
                    return a
                names = " ".join("abcde"[:len(shape)])
                return a.rearrange(f"p ({names}) -> p {names}", **dict(zip("abcde", shape)))

        def over(ap, shape):
            return ap.to_broadcast(shape)

        s_weights = sem("weights_loaded")
        s_pool = sem("positions_made")
        s_id = sem("identity_made")
        ENGINES = ("tensor", "vector", "scalar", "pool")
        s_open = {engine: sem(f"round_open_{engine}") for engine in ENGINES}
        x_in = w["x"].rearrange("b (t p) d -> b p t d", p=P)
        x_out = out.rearrange("b (t p) d -> b p t d", p=P)

        def step(eng, engine, instruction, name, u=0):
            instruction.then_inc(*done(engine, name, u))
            eng.wait_ge(*at(name, u))

        def mark(eng, engine, instruction, name, u=0):
            instruction.then_inc(*done(engine, name, u))

        def rsqrt_newton(v, tag, u, y, x, t):
            step(v, "vector", v.tensor_tensor(t, y, y, ALU.mult), f"{tag}.nt0", u)
            step(v, "vector", v.tensor_tensor(t, t, x, ALU.mult), f"{tag}.nt1", u)
            step(v, "vector", v.tensor_scalar(t, t, -0.5, 1.5, ALU.mult, ALU.add), f"{tag}.nt2", u)
            step(v, "vector", v.tensor_tensor(y, y, t, ALU.mult), f"{tag}.rstd", u)

        def moments(v, tag, u, src, eps):
            st = lnt[u]
            for i in range(TT):
                step(v, "vector", v.bn_stats(st[:, 16 + 6 * i:22 + 6 * i], src[:, i, :]), f"{tag}.st{i}", u)
            v.memset(st[:, 12:14], 0.0).then_inc(*done("vector", f"{tag}.clear", u))
            for i in range(TT):
                mark(v, "vector", v.bn_aggr(st[:, 2 * i:2 * i + 2], st[:, 16 + 6 * i:22 + 6 * i]), f"{tag}.mv{i}", u)
            v.wait_ge(*at(f"{tag}.mv{TT - 1}", u))
            step(v, "vector", v.tensor_scalar(st[:, 4:6], st[:, 0:4].rearrange("p (i c) -> p c i", c=2)[:, 1, :], eps, None, ALU.add), f"{tag}.var", u)

        def norm_vector_1(v, tag, u, y):
            step(v, "vector", v.tensor_tensor(res[u][:, :, :], y, X[u][:, :, :], ALU.add), f"{tag}.res", u)
            moments(v, tag, u, res[u], 1e-5)

        def norm_scalar(a, tag, u):
            st = lnt[u]
            a.wait_ge(*at(f"{tag}.var", u))
            step(a, "scalar", a.activation(st[:, 6:8], st[:, 4:6], ACT.Ln), f"{tag}.ln", u)
            step(a, "scalar", a.activation(st[:, 8:10], st[:, 6:8], ACT.Exp, scale=-0.5), f"{tag}.power", u)

        def norm_vector_2(v, tag, u, src=None, dst=None):
            st = lnt[u]
            src = res[u] if src is None else src
            dst = X[u] if dst is None else dst
            v.wait_ge(*at(f"{tag}.power", u))
            rsqrt_newton(v, tag, u, st[:, 8:10], st[:, 4:6], st[:, 10:12])
            for i in range(TT):
                step(v, "vector", v.tensor_scalar(dst[:, i, :], src[:, i, :], st[:, 2 * i:2 * i + 1], st[:, 8 + i:9 + i], ALU.subtract, ALU.mult),
                     f"{tag}.x{i}", u)

        AH, AHD, AW = 16, 8, 32
        LH, LN = 8, 64
        POOL = S // LN
        QT = [(0, 96, 0, 96), (96, 96, 64, 128), (160, 96, 128, 128)]
        A_SCALE = float(AHD) ** -0.5
        a_w = sb("a_w", [P, 3, P])
        a_wg = sb("a_wg", [P, 3, 64])
        a_wo = sb("a_wo", [P, P])
        a_ro = sb("a_ro", [64, P])
        a_gate = sb("a_gate", [P, 2])
        a_gates = sb("a_gates", [P, 32])
        a_mask = [sb(f"a_mask{t}", [P, P]) for t in range(3)]
        a_lmask = sb("a_lmask", [P, TT, LN])

        class StageA:
            def __init__(self, u):
                c = Carve(u)
                self.qT = c(S)
                self.kT = c(4, S)
                self.gqT = c(S)
                self.gkT = c(4, LN)
                self.xp = c(2, LN)
                self.gv = c(4, 2, 9)
                self.v = c(3, AH, 9)
                self.s = c(AH, P)
                self.pT = c(AH, P)
                self.ls = c(TT, LH, LN)
                self.lpT = c(TT * 4, P)
                self.mx = c(16)
                self.rs = c(32)
                self.rem = c(TT, 64)
                self.remT = c(S)
                self.g = c(32)
                self.loc = c(AH, AHD)
                self.o = c(AH, AHD)
                self.oT = c(S)

        SA = [StageA(u) for u in LANES]

        def a_load(sp):
            for i, n in enumerate(("wq", "wk", "wv")):
                sp.dma_start(a_w[:, i, :], w[f"L0_attn_{n}"]).then_inc(s_weights, 16)
            for i, n in enumerate(("wgq", "wgk", "wgv")):
                sp.dma_start(a_wg[:, i, :], w[f"L0_attn_{n}"]).then_inc(s_weights, 16)
            sp.dma_start(a_wo[:, :], w["L0_attn_w_out"]).then_inc(s_weights, 16)
            sp.dma_start(a_ro[:, :], w["L0_attn_r_out_w"]).then_inc(s_weights, 16)
            sp.dma_start(a_gate[:, 0:1], w["L0_attn_gate_local_w"].rearrange("h (d a) -> (h d) a", a=1)).then_inc(s_weights, 16)
            sp.dma_start(a_gate[:, 1:2], w["L0_attn_gate_remote_w"].rearrange("h (d a) -> (h d) a", a=1)).then_inc(s_weights, 16)
            return 10

        def a_setup_pool(g):
            for t, (qs, qn, ks, kn) in enumerate(QT):
                g.memset(a_mask[t][:, :], 0.0).then_inc(s_pool, 1)
            g.memset(a_lmask[:, :, :], 0.0).then_inc(s_pool, 1)
            g.wait_ge(s_pool, 4)
            for t, (qs, qn, ks, kn) in enumerate(QT):
                m = a_mask[t][:, :]
                g.affine_select(out=m, in_=m, compare_op=ALU.is_ge, fill=NEG, base=qs - ks,
                                pattern=[[-1, P]], channel_multiplier=1).then_inc(s_pool, 1)
            g.affine_select(out=a_lmask[:, :, :], in_=a_lmask[:, :, :], compare_op=ALU.is_ge, fill=NEG, base=0,
                            pattern=[[P, TT], [-POOL, LN]], channel_multiplier=1).then_inc(s_pool, 1)
            g.wait_ge(s_pool, 8)
            for t, (qs, qn, ks, kn) in enumerate(QT):
                m = a_mask[t][:, :]
                g.affine_select(out=m, in_=m, compare_op=ALU.is_ge, fill=NEG, base=AW - 1 + ks - qs,
                                pattern=[[1, P]], channel_multiplier=-1).then_inc(s_pool, 1)

        def a_setup_vector(v):
            for i in range(2):
                step(v, "vector", v.tensor_scalar(a_gates[:, 16 * i:16 * i + 16], head_of[:, :], a_gate[:, i:i + 1], None, ALU.mult), "setup.gates%d" % i)

        def a_tensor(pe):
            for u in LANES:
                pe.wait_ge(s_x[u], 16)
                for t in range(TT):
                    m = pe.transpose(ps[u][:, 0, P * t:P * t + P], X[u][:, t, :], ident[:, :])
                m.then_inc(*done("tensor", "A.xT_p", u))
            for u in LANES:
                z = SA[u]
                pe.wait_ge(*at("A.xp", u))
                for i in range(2):
                    pe.matmul(ps[u][:, 1, S * i:S * i + S], a_w[:, i, :], XT[u][:, :], start=True, stop=True)
                pe.matmul(ps[u][0:64, 2, 0:S], a_wg[:, 0, :], XT[u][:, :], start=True, stop=True)
                pe.matmul(ps[u][0:64, 2, 256:256 + LN], a_wg[:, 1, :], z.xp[:, 0, :], start=True, stop=True)
                pe.matmul(ps[u][:, 2, 320:384], z.xp, a_wg[:, 2, :], start=True, stop=True)
                for t, (qs, qn, ks, kn) in enumerate(QT):
                    m = pe.matmul(ps[u][0:kn, 3, P * t:P * t + P], XT[u][:, ks:ks + kn], a_w[:, 2, :], start=True, stop=True)
                m.then_inc(*done("tensor", "A.proj_p", u))
            for u in LANES:
                z = SA[u]
                pe.wait_ge(*at("A.proj", u))
                pe.wait_ge(*at("A.proj_a", u))
                for i in range(TT):
                    for g in range(2):
                        for r in range(4):
                            m = pe.matmul(ps[u][:, g, 256 * i + 64 * r:256 * i + 64 * r + 64],
                                          z.gqT[32 * g:32 * g + 32, P * i:P * i + P],
                                          z.gkT[32 * g:32 * g + 32, r, :], start=True, stop=True)
                m.then_inc(*done("tensor", "A.ls_p", u))
            for u in LANES:
                z = SA[u]
                pe.wait_ge(*at("A.lprob", u))
                for i in range(TT):
                    for c in range(4):
                        m = pe.transpose(ps[u][:, 2 + i, P * c:P * c + P], z.ls[:, i, 2 * c:2 * c + 2, :], ident[:, :])
                m.then_inc(*done("tensor", "A.lpT_p", u))
            for u in LANES:
                z = SA[u]
                pe.wait_ge(*at("A.lpT", u))
                for i in range(TT):
                    for c in range(4):
                        m = pe.matmul(ps[u][:, 0, P * i + 18 * c:P * i + 18 * c + 18], z.lpT[:, 4 * i + c, :],
                                      z.gv[:, c, :, :], start=True, stop=True)
                m.then_inc(*done("tensor", "A.rem_p", u))
            for u in LANES:
                z = SA[u]
                pe.wait_ge(*at("A.rem", u))
                m = pe.transpose(ps[u][:, 1, 0:P], z.rem, ident[:, :])
                m.then_inc(*done("tensor", "A.remT_p", u))
            for t, (qs, qn, ks, kn) in enumerate(QT):
                for u in LANES:
                    z = SA[u]
                    pe.wait_ge(*at(f"A.o{t - 1}" if t else "A.remT", u))
                    for g in range(4):
                        for r in range(4):
                            m = pe.matmul(ps[u][0:qn, g, P * r:P * r + kn], z.qT[32 * g:32 * g + 32, qs:qs + qn],
                                          z.kT[32 * g:32 * g + 32, r, ks:ks + kn], start=True, stop=True)
                    m.then_inc(*done("tensor", f"A.s_p{t}", u))
                for u in LANES:
                    z = SA[u]
                    pe.wait_ge(*at(f"A.prob{t}", u))
                    for h in range(AH):
                        m = pe.transpose(ps[u][0:kn, h // 4, P * (h % 4):P * (h % 4) + qn], z.s[0:qn, h, 0:kn], ident[0:qn, 0:qn])
                    m.then_inc(*done("tensor", f"A.pT_p{t}", u))
                for u in LANES:
                    z = SA[u]
                    pe.wait_ge(*at(f"A.pT{t}", u))
                    for h in range(AH):
                        pe.matmul(ps[u][0:qn, 0, 9 * h:9 * h + 9], z.pT[0:kn, h, 0:qn], z.v[0:kn, t, h, :], start=True, stop=True)
                    pe.matmul(ps[u][0:qn, 0, 160:192], z.qT[:, qs:qs + qn], a_gates[:, :], start=True, stop=True)
                    pe.matmul(ps[u][0:qn, 0, 256:384], z.remT[0:64, qs:qs + qn], a_ro[:, :], start=True, stop=True)\
                        .then_inc(*done("tensor", f"A.o_p{t}", u))
                for u in LANES:
                    z = SA[u]
                    pe.wait_ge(*at(f"A.o{t}", u))
                    pe.transpose(ps[u][:, 1, 0:qn], z.o[0:qn, :, :], ident[0:qn, 0:qn])\
                        .then_inc(*done("tensor", f"A.oT_p{t}", u))
                for u in LANES:
                    pe.wait_ge(*at(f"A.oT{t}", u))
            for u in LANES:
                z = SA[u]
                for i in range(TT):
                    m = pe.matmul(ps[u][:, 0, P * i:P * i + P], z.oT[:, P * i:P * i + P], a_wo[:, :], start=True, stop=True)
                m.then_inc(*done("tensor", "A.y_p", u))

        def a_vector(v):
            for u in LANES:
                z = SA[u]
                v.wait_ge(*at("A.xT_p", u))
                step(v, "vector", v.tensor_copy(XT[u][:, :], ps[u][:, 0, 0:S]), "A.xT", u)
                step(v, "vector", v.tensor_reduce(z.xp[:, 0, :], XT[u][:, :].rearrange("p (n c) -> p n c", c=POOL), AX.X, ALU.add), "A.xp0", u)
                step(v, "vector", v.tensor_scalar(z.xp[:, 0, :], z.xp[:, 0, :], 1.0 / POOL, None, ALU.mult), "A.xp1", u)
                step(v, "vector", v.tensor_copy(z.xp[:, 1, :], z.xp[:, 0, :]), "A.xp", u)
            for u in LANES:
                z = SA[u]
                v.wait_ge(*at("A.proj_p", u))
                step(v, "vector", v.tensor_tensor(z.kT, over(ps[u][:, 1, S:2 * S].unsqueeze(1), [P, 4, S]),
                                                  over(head_mod[:, :].unsqueeze(2), [P, 4, S]), ALU.mult), "A.kT", u)
                step(v, "vector", v.tensor_tensor(z.gkT[0:64, :, :], over(ps[u][0:64, 2, 256:256 + LN].unsqueeze(1), [64, 4, LN]),
                                                  over(head_mod[0:64, :].unsqueeze(2), [64, 4, LN]), ALU.mult), "A.gkT", u)
                for k in range(2):
                    src = ps[u][64 * k:64 * k + 64, 2, 320:384].rearrange("p (c e d) -> p c e d", c=4, e=2)
                    step(v, "vector", v.tensor_copy(z.gv[64 * k:64 * k + 64, :, k, 0:8], src[:, :, k, :]), f"A.gv{k}", u)
                    step(v, "vector", v.memset(z.gv[64 * k:64 * k + 64, :, k, 8:9], 1.0), f"A.gvone{k}", u)
                    step(v, "vector", v.memset(z.gv[64 * k:64 * k + 64, :, 1 - k, :], 0.0), f"A.gvnil{k}", u)
                step(v, "vector", v.memset(z.v[:, :, :, 8:9], 1.0), "A.vone", u)
                for t, (qs, qn, ks, kn) in enumerate(QT):
                    step(v, "vector", v.tensor_copy(z.v[0:kn, t, :, 0:8], ps[u][0:kn, 3, P * t:P * t + P].rearrange("p (h d) -> p h d", d=AHD)),
                         f"A.v{t}" if t < 2 else "A.proj", u)
            for u in LANES:
                z = SA[u]
                v.wait_ge(*at("A.ls_p", u))
                for i in range(TT):
                    step(v, "vector", v.tensor_tensor(
                        z.ls[:, i, :, :].rearrange("p (g r) n -> p g r n", g=2),
                        ps[u][:, 0:2, 256 * i:256 * i + 256].rearrange("p g (r n) -> p g r n", r=4),
                        over(a_lmask[:, i:i + 1, :].unsqueeze(1), [P, 2, 4, LN]), ALU.add), f"A.lsm{i}", u)
                step(v, "vector", v.tensor_reduce(z.mx, z.ls, AX.X, ALU.max), "A.lmx", u)
                step(v, "vector", v.tensor_tensor(z.ls, z.ls, over(z.mx.rearrange("p (i h) -> p i h", i=TT).unsqueeze(3), [P, TT, LH, LN]), ALU.subtract), "A.lsub", u)
            for u in LANES:
                z = SA[u]
                v.wait_ge(*at("A.rem_p", u))
                o = ps[u][:, 0, 0:2 * P].rearrange("p (i c) -> p i c", i=TT)[:, :, 0:72].rearrange("p i (h d) -> p i h d", d=9)
                rs = z.rs[:, 0:16].rearrange("p (i h) -> p i h", i=TT)
                step(v, "vector", v.reciprocal(rs.unsqueeze(3), o[:, :, :, 8:9]), "A.rrs", u)
                step(v, "vector", v.tensor_tensor(z.rem.rearrange("p i (h d) -> p i h d", d=8), o[:, :, :, 0:8],
                                                  over(rs.unsqueeze(3), [P, TT, LH, 8]), ALU.mult), "A.rem", u)
            for u in LANES:
                z = SA[u]
                v.wait_ge(*at("A.remT_p", u))
                step(v, "vector", v.tensor_copy(z.remT[0:64, 0:P], ps[u][0:64, 1, 0:P]), "A.remT0", u)
                step(v, "vector", v.tensor_copy(z.remT[0:64, P:S], ps[u][64:P, 1, 0:P]), "A.remT", u)
            for t, (qs, qn, ks, kn) in enumerate(QT):
                for u in LANES:
                    z = SA[u]
                    v.wait_ge(*at(f"A.s_p{t}", u))
                    sc = ps[u][0:qn, :, :].rearrange("p g (r k) -> p (g r) k", k=P)[:, :, 0:kn]
                    step(v, "vector", v.tensor_tensor(z.s[0:qn, :, 0:kn], sc, over(a_mask[t][0:qn, 0:kn].unsqueeze(1), [qn, AH, kn]), ALU.add), f"A.sm{t}", u)
                    step(v, "vector", v.tensor_reduce(z.mx[0:qn, :], z.s[0:qn, :, 0:kn], AX.X, ALU.max), f"A.mx{t}", u)
                for u in LANES:
                    z = SA[u]
                    v.wait_ge(*at(f"A.o_p{t}", u))
                    v.wait_ge(*at(f"A.gexp{t}", u))
                    o = ps[u][0:qn, 0, 0:144].rearrange("p (h d) -> p h d", d=9)
                    step(v, "vector", v.tensor_scalar(z.g[0:qn, :], z.g[0:qn, :], 1.0, None, ALU.add), f"A.g1{t}", u)
                    step(v, "vector", v.reciprocal(z.g[0:qn, :], z.g[0:qn, :]), f"A.g{t}", u)
                    step(v, "vector", v.reciprocal(z.rs[0:qn, 0:16].unsqueeze(2), o[:, :, 8:9]), f"A.rs{t}", u)
                    step(v, "vector", v.tensor_tensor(z.rs[0:qn, 0:16], z.rs[0:qn, 0:16], z.g[0:qn, 0:16], ALU.mult), f"A.grs{t}", u)
                    step(v, "vector", v.tensor_tensor(z.loc[0:qn, :, :], o[:, :, 0:8], over(z.rs[0:qn, 0:16].unsqueeze(2), [qn, AH, 8]), ALU.mult), f"A.loc{t}", u)
                    step(v, "vector", v.tensor_tensor(z.o[0:qn, :, :], ps[u][0:qn, 0, 256:384].rearrange("p (h d) -> p h d", d=8),
                                                      over(z.g[0:qn, 16:32].unsqueeze(2), [qn, AH, 8]), ALU.mult), f"A.orem{t}", u)
                    step(v, "vector", v.tensor_tensor(z.o[0:qn, :, :], z.o[0:qn, :, :], z.loc[0:qn, :, :], ALU.add), f"A.o{t}", u)
                for u in LANES:
                    z = SA[u]
                    v.wait_ge(*at(f"A.oT_p{t}", u))
                    step(v, "vector", v.tensor_copy(z.oT[:, qs:qs + qn], ps[u][:, 1, 0:qn]), f"A.oT{t}", u)
            for u in LANES:
                v.wait_ge(*at("A.y_p", u))
                norm_vector_1(v, "A", u, ps[u][:, 0, 0:S].rearrange("p (i d) -> p i d", i=TT))
            for u in LANES:
                norm_vector_2(v, "A", u)

        def a_scalar(a):
            for u in LANES:
                z = SA[u]
                a.wait_ge(*at("A.proj_p", u))
                a.wait_ge(*at("A.kT", u))
                step(a, "scalar", a.activation(z.qT, ps[u][:, 1, 0:S], ACT.Copy), "A.qT", u)
                a.wait_ge(*at("A.proj", u))
                step(a, "scalar", a.activation(z.gqT[0:64, :], ps[u][0:64, 2, 0:S], ACT.Copy), "A.proj_a", u)
            for u in LANES:
                z = SA[u]
                a.wait_ge(*at("A.lsub", u))
                step(a, "scalar", a.activation(z.ls, z.ls, ACT.Exp, scale=A_SCALE), "A.lprob", u)
            for u in LANES:
                z = SA[u]
                a.wait_ge(*at("A.lpT_p", u))
                step(a, "scalar", a.activation(z.lpT, ps[u][:, 2:4, :].rearrange("p b (c q) -> p (b c) q", c=4), ACT.Copy), "A.lpT", u)
            for t, (qs, qn, ks, kn) in enumerate(QT):
                for u in LANES:
                    z = SA[u]
                    a.wait_ge(*at(f"A.ssub{t}", u))
                    step(a, "scalar", a.activation(z.s[0:qn, :, 0:kn], z.s[0:qn, :, 0:kn], ACT.Exp, scale=A_SCALE), f"A.prob{t}", u)
                for u in LANES:
                    z = SA[u]
                    a.wait_ge(*at(f"A.pT_p{t}", u))
                    src = ps[u][0:kn, :, :].rearrange("p g (r k) -> p (g r) k", k=P)[:, :, 0:qn]
                    step(a, "scalar", a.activation(z.pT[0:kn, :, 0:qn], src, ACT.Copy), f"A.pT{t}", u)
                for u in LANES:
                    z = SA[u]
                    a.wait_ge(*at(f"A.o_p{t}", u))
                    step(a, "scalar", a.activation(z.g[0:qn, :], ps[u][0:qn, 0, 160:192], ACT.Exp, scale=-1.0), f"A.gexp{t}", u)
            for u in LANES:
                norm_scalar(a, "A", u)

        def a_pool(g):
            for t, (qs, qn, ks, kn) in enumerate(QT):
                for u in LANES:
                    z = SA[u]
                    g.wait_ge(*at(f"A.mx{t}", u))
                    step(g, "pool", g.tensor_tensor(z.s[0:qn, :, 0:kn], z.s[0:qn, :, 0:kn], over(z.mx[0:qn, :].unsqueeze(2), [qn, AH, kn]), ALU.subtract), f"A.ssub{t}", u)

        MT = (SC + P - 1) // P
        ML = SC - (MT - 1) * P
        MP = (MT + 1) // 2
        ITERS = 3
        b_w = [XT[0][:, 0:P], XT[0][:, P:S], XT[1][:, 0:P]]
        b_gw = [[X[0][:, 0, :], X[0][:, 1, :], X[1][:, 0, :]],
                [X[1][:, 1, :], res[0][:, 0, :], res[0][:, 1, :]]]
        b_hhT = sb("b_hhT", [P, 3 * P])
        c_wqT = sb("c_wqT", [P, 1024])
        b_ihT = c_wqT[:, 0:3 * P]
        b_A = sb("b_A", [P, P])
        b_C = sb("b_C", [P, 3 * P])
        b_bias = sb("b_bias", [P, 2, 3])
        b_nw = sb("b_nw", [P, 2])
        b_small = sb("b_small", [P, 8])
        b_mean = sb("b_mean", [P, P])
        e_ln = sb("e_ln", [P, 4])
        KV = SC + S
        kvT = [sb(f"kvT{u}", [P, KV]) for u in LANES]

        class StageB:
            def __init__(self, u):
                c = Carve(u, AREA - MT * P)
                self.ctx = c(MT, P)
                c = Carve(u)
                self.p = c(MT, P + 1)
                self.pT = c(SC)
                self.att = c(MT, S)
                c2 = Carve(u, c.at - MT * S)
                self.xn = c2(MT, P)
                self.pw = c(MT, P + 1)
                self.st = c(MT, 6)
                self.vv = c(2, MT)
                self.rr = c(2, MT)
                self.t1 = c(2, MT)
                self.mean = c(MT)
                self.df = c(MT)
                self.sl = c(S)
                self.sq = c(S)
                self.qk = c(S)
                self.mx = c(2 * MP)
                self.rs = c(2 * MP)
                self.rd = c(2)
                self.un = c(2, P)
                self.uT = c(S)
                self.rz = c(2 * S)
                self.n = c(S)
                self.t = c(S)
                assert c.at <= AREA - MT * P

        SB = [StageB(u) for u in LANES]

        def col(name, a=1):
            return w[name].rearrange("(g p) -> p g", p=P)

        def b_load(sp):
            for i, n in enumerate(("Wq", "Wk", "Wv")):
                sp.dma_start(b_w[i], w[f"L0_xattn_{n}"]).then_inc(s_weights, 16)
            for i, n in enumerate(("gru_wih", "gru_whh")):
                for g in range(3):
                    sp.dma_start(b_gw[i][g], w[f"L0_xattn_{n}"][P * g:P * g + P, :]).then_inc(s_weights, 16)
            for i, n in enumerate(("gru_bih", "gru_bhh")):
                sp.dma_start(b_bias[:, i, :], col(f"L0_xattn_{n}"), allow_slow_non_contiguous=True).then_inc(s_weights, 16)
            for i, n in enumerate(("slot_norm_w", "input_norm_w")):
                sp.dma_start(b_nw[:, i:i + 1], col(f"L0_xattn_{n}"), allow_slow_non_contiguous=True).then_inc(s_weights, 16)
            for i, n in enumerate(("g_x", "b_x", "g_l", "b_l")):
                sp.dma_start(e_ln[:, i:i + 1], col(f"L1_xattn_{n}"), allow_slow_non_contiguous=True).then_inc(s_weights, 16)

        def b_setup_pool(g):
            for u in LANES:
                g.memset(area[u][:, :], 0.0).then_inc(s_pool, 1)
            g.memset(b_mean[:, :], 1.0 / P).then_inc(s_pool, 1)

        def b_setup_tensor(pe):
            pe.matmul(ps[0][:, 0, 0:P], b_w[0], b_w[1], start=True, stop=True)
            for i in range(3):
                pe.transpose(ps[0][:, 1, P * i:P * i + P], b_gw[0][i], ident[:, :])
            for i in range(3):
                m = pe.transpose(ps[0][:, 2, P * i:P * i + P], b_gw[1][i], ident[:, :])
            m.then_inc(*done("tensor", "setup.b1_p"))
            pe.wait_ge(*at("setup.b_ihT"))
            pe.matmul(ps[0][:, 3, 0:3 * P], b_w[2], b_ihT, start=True, stop=True).then_inc(*done("tensor", "setup.b2_p"))

        def b_setup_vector(v):
            v.wait_ge(*at("setup.b1_p"))
            step(v, "vector", v.tensor_scalar(b_A[:, :], ps[0][:, 0, 0:P], b_nw[:, 0:1], None, ALU.mult), "setup.b_A")
            step(v, "vector", v.tensor_copy(b_hhT[:, :], ps[0][:, 2, 0:3 * P]), "setup.b_hhT")
            step(v, "vector", v.tensor_copy(b_ihT, ps[0][:, 1, 0:3 * P]), "setup.b_ihT")
            v.wait_ge(*at("setup.b2_p"))
            step(v, "vector", v.tensor_scalar(b_C[:, :], ps[0][:, 3, 0:3 * P], b_nw[:, 1:2], None, ALU.mult), "setup.b_C")
            step(v, "vector", v.tensor_tensor(b_small[:, 0:2], b_bias[:, 0, 0:2], b_bias[:, 1, 0:2], ALU.add), "setup.b_s0")
            step(v, "vector", v.tensor_scalar(b_small[:, 0:2], b_small[:, 0:2], -1.0, None, ALU.mult), "setup.b_s1")
            step(v, "vector", v.tensor_scalar(b_small[:, 2:3], b_bias[:, 0, 2:3], 2.0, None, ALU.mult), "setup.b_s2")
            step(v, "vector", v.tensor_scalar(b_small[:, 3:4], b_nw[:, 1:2], float(D) ** -0.5, None, ALU.mult), "setup.b_s3")

        def b_sync(sp, it):
            for u in LANES:
                src = w["ctx_1024"][it * 2 + u]
                sp.dma_start(SB[u].ctx[:, 0:MT - 1, :], src[0:P * (MT - 1), :].rearrange("(t p) d -> p t d", p=P)).then_inc(s_ctx[u], 16)
                sp.dma_start(SB[u].ctx[0:ML, MT - 1, :], src[P * (MT - 1):SC, :]).then_inc(s_ctx[u], 16)

        def rows(m):
            return ML if m == MT - 1 else P

        def b_tensor(pe):
            for u in LANES:
                pe.wait_ge(*at("B.p", u))
                for m in range(MT):
                    o = pe.transpose(ps[u][:, m // 4, P * (m % 4):P * (m % 4) + rows(m)], SB[u].p[0:rows(m), m, 0:P], ident[0:rows(m), 0:rows(m)])
                o.then_inc(*done("tensor", "B.pT_p", u))
            for u in LANES:
                pe.wait_ge(*at("B.pT", u))
                pe.wait_ge(*at("B.xn", u))
                for m in range(MT):
                    o = pe.transpose(ps[u][:, m // 4, P * (m % 4):P * (m % 4) + rows(m)], SB[u].xn[0:rows(m), m, :], ident[0:rows(m), 0:rows(m)])
                o.then_inc(*done("tensor", "B.xnT_p", u))
            for u in LANES:
                pe.wait_ge(*at("B.xnT", u))
                for i in range(TT):
                    o = pe.transpose(ps[u][:, 0, P * i:P * i + P], X[u][:, i, :], ident[:, :])
                o.then_inc(*done("tensor", "B.slT_p", u))
            for r in range(ITERS):
                k = f"B.{r}"
                for u in LANES:
                    pe.wait_ge(*at(f"{k}.sq", u))
                    pe.matmul(ps[u][:, 3, 0:S], b_mean[:, :], SB[u].sq, start=True, stop=True).then_inc(*done("tensor", f"{k}.ms_p", u))
                for u in LANES:
                    pe.wait_ge(*at(f"{k}.sn", u))
                    pe.matmul(ps[u][:, 3, 0:S], b_A[:, :], SB[u].sq, start=True, stop=True).then_inc(*done("tensor", f"{k}.qk_p", u))
                for g in range(MP + 1):
                    for u in LANES:
                        z = SB[u]
                        if g < MP:
                            if g == 0:
                                pe.wait_ge(*at(f"{k}.qk", u))
                            if g >= 2:
                                pe.wait_ge(*at(f"{k}.att{2 * g - 3}", u))
                            for m in range(2 * g, min(2 * g + 2, MT)):
                                o = pe.matmul(ps[u][0:rows(m), g % 2, S * (m % 2):S * (m % 2) + S], z.pT[:, P * m:P * m + rows(m)], z.qk, start=True, stop=True)
                            o.then_inc(*done("tensor", f"{k}.s_p{g}", u))
                    for u in LANES if g >= 1 else ():
                        z = SB[u]
                        pe.wait_ge(*at(f"{k}.pw{g - 1}", u))
                        for m in range(2 * g - 2, min(2 * g, MT)):
                            for j in range(2):
                                o = pe.matmul(ps[u][:, 2 + j, 0:P + 1], z.att[0:rows(m), m, P * j:P * j + P], z.pw[0:rows(m), m, :],
                                              start=m == 0, stop=m == MT - 1)
                        if g == MP:
                            o.then_inc(*done("tensor", f"{k}.u_p", u))
                for u in LANES:
                    pe.wait_ge(*at(f"{k}.un", u))
                    for j in range(2):
                        o = pe.transpose(ps[u][:, 0, P * j:P * j + P], SB[u].un[:, j, :], ident[:, :])
                    o.then_inc(*done("tensor", f"{k}.uT_p", u))
                for u in LANES:
                    z = SB[u]
                    pe.wait_ge(*at(f"{k}.uT", u))
                    for j in range(2):
                        pe.matmul(ps[u][:, 1, S * j:S * j + S], b_C[:, P * j:P * j + P], z.uT, start=True, stop=False)
                        pe.matmul(ps[u][:, 1, S * j:S * j + S], b_hhT[:, P * j:P * j + P], z.sl, start=False, stop=True)
                    pe.matmul(ps[u][:, 2, 0:S], b_C[:, 2 * P:3 * P], z.uT, start=True, stop=True)
                    pe.matmul(ps[u][:, 2, S:2 * S], b_hhT[:, 2 * P:3 * P], z.sl, start=True, stop=True).then_inc(*done("tensor", f"{k}.gru_p", u))
            for u in LANES:
                pe.wait_ge(*at(f"B.{ITERS - 1}.sl", u))
                for i in range(TT):
                    o = pe.transpose(ps[u][:, 0, P * i:P * i + P], SB[u].sl[:, P * i:P * i + P], ident[:, :])
                o.then_inc(*done("tensor", "B.y_p", u))

        def b_vector(v):
            for u in LANES:
                z = SB[u]
                v.wait_ge(s_ctx[u], 32)
                for m in range(MT):
                    mark(v, "vector", v.bn_stats(z.st[:, m, :], z.ctx[:, m, :]), f"B.cst{m}", u)
                v.wait_ge(*at(f"B.cst{MT - 1}", u))
                me, mo, ce, co = (z.st[:, :, i] for i in (1, 4, 2, 5))
                step(v, "vector", v.tensor_tensor(z.mean, me, mo, ALU.add), "B.cmean0", u)
                step(v, "vector", v.tensor_tensor(z.df, me, mo, ALU.subtract), "B.df", u)
                step(v, "vector", v.tensor_scalar(z.mean, z.mean, 0.5, None, ALU.mult), "B.cmean", u)
                step(v, "vector", v.tensor_tensor(z.df, z.df, z.df, ALU.mult), "B.df2", u)
                step(v, "vector", v.tensor_tensor(z.vv[:, 0, :], ce, co, ALU.add), "B.cv", u)
                step(v, "vector", v.tensor_scalar(z.vv[:, 0, :], z.vv[:, 0, :], 1.0 / D, None, ALU.mult), "B.cvd", u)
                step(v, "vector", v.scalar_tensor_tensor(out=z.vv[:, 0, :], in0=z.df, scalar=0.25, in1=z.vv[:, 0, :], op0=ALU.mult, op1=ALU.add), "B.cvar", u)
                step(v, "vector", v.tensor_tensor(z.vv[:, 1, :], z.mean, z.mean, ALU.mult), "B.msq", u)
                step(v, "vector", v.tensor_tensor(z.vv[:, 1, :], z.vv[:, 1, :], z.vv[:, 0, :], ALU.add), "B.ms", u)
                step(v, "vector", v.tensor_scalar(z.vv[:, 0, :], z.vv[:, 0, :], 1e-5, None, ALU.add), "B.vare", u)
                step(v, "vector", v.tensor_scalar(z.vv[:, 1, :], z.vv[:, 1, :], 1e-6, None, ALU.add), "B.vv", u)
            for u in LANES:
                z = SB[u]
                v.wait_ge(*at("B.cpower", u))
                rsqrt_newton(v, "B.c", u, z.rr, z.vv, z.t1)
                step(v, "vector", v.tensor_tensor(z.p[:, :, 0:P], z.ctx, over(z.rr[:, 1, :].unsqueeze(2), [P, MT, P]), ALU.mult), "B.p0", u)
                step(v, "vector", v.memset(z.p[:, :, P:P + 1], 1.0), "B.p", u)
            for u in LANES:
                v.wait_ge(*at("B.slT_p", u))
                step(v, "vector", v.tensor_copy(SB[u].sl, ps[u][:, 0, 0:S]), "B.sl", u)
            for r in range(ITERS):
                k = f"B.{r}"
                for u in LANES:
                    z = SB[u]
                    step(v, "vector", v.tensor_tensor(z.sq, z.sl, z.sl, ALU.mult), f"{k}.sq", u)
                for u in LANES:
                    z = SB[u]
                    v.wait_ge(*at(f"{k}.power", u))
                    step(v, "vector", v.tensor_tensor(z.sq, z.sl, z.t, ALU.mult), f"{k}.sn", u)
                for u in LANES:
                    v.wait_ge(*at(f"{k}.qk_p", u))
                    step(v, "vector", v.tensor_scalar(SB[u].qk, ps[u][:, 3, 0:S], b_small[:, 3:4], None, ALU.mult), f"{k}.qk", u)
                for g in range(MP):
                    n = min(2, MT - 2 * g)
                    q = rows(2 * g + n - 1)
                    for u in LANES:
                        z = SB[u]
                        v.wait_ge(*at(f"{k}.s_p{g}", u))
                        step(v, "vector", v.tensor_reduce(z.mx[0:q, 2 * g:2 * g + n], ps[u][0:q, g % 2, 0:S * n].rearrange("p (m k) -> p m k", m=n), AX.X, ALU.max), f"{k}.mx{g}", u)
                        mark(v, "vector", v.tensor_scalar(z.mx[0:q, 2 * g:2 * g + n], z.mx[0:q, 2 * g:2 * g + n], -1.0, None, ALU.mult), f"{k}.nmx{g}", u)
                    if g >= 1:
                        b_weigh(v, k, g - 1)
                b_weigh(v, k, MP - 1)
                for u in LANES:
                    z = SB[u]
                    v.wait_ge(*at(f"{k}.u_p", u))
                    step(v, "vector", v.tensor_scalar(z.rd, ps[u][:, 2:4, P], 1e-6, None, ALU.add), f"{k}.rd0", u)
                    step(v, "vector", v.reciprocal(z.rd, z.rd), f"{k}.rd", u)
                    step(v, "vector", v.tensor_tensor(z.un, ps[u][:, 2:4, 0:P], over(z.rd.unsqueeze(2), [P, 2, P]), ALU.mult), f"{k}.un", u)
                for u in LANES:
                    z = SB[u]
                    v.wait_ge(*at(f"{k}.ez", u))
                    step(v, "vector", v.tensor_scalar(z.rz, z.rz, 1.0, None, ALU.add), f"{k}.rz1", u)
                    step(v, "vector", v.reciprocal(z.rz, z.rz), f"{k}.rz", u)
                    step(v, "vector", v.scalar_tensor_tensor(out=z.t, in0=ps[u][:, 2, S:2 * S], scalar=b_bias[:, 1, 2:3], in1=z.rz[:, 0:S], op0=ALU.add, op1=ALU.mult), f"{k}.t0", u)
                    step(v, "vector", v.tensor_tensor(z.t, ps[u][:, 2, 0:S], z.t, ALU.add), f"{k}.t1", u)
                for u in LANES:
                    z = SB[u]
                    v.wait_ge(*at(f"{k}.en", u))
                    step(v, "vector", v.tensor_scalar(z.n, z.n, 1.0, None, ALU.add), f"{k}.n0", u)
                    step(v, "vector", v.reciprocal(z.n, z.n), f"{k}.n1", u)
                    step(v, "vector", v.tensor_scalar(z.n, z.n, -2.0, 1.0, ALU.mult, ALU.add), f"{k}.n", u)
                    step(v, "vector", v.tensor_tensor(z.t, z.sl, z.n, ALU.subtract), f"{k}.d0", u)
                    step(v, "vector", v.tensor_tensor(z.t, z.rz[:, S:2 * S], z.t, ALU.mult), f"{k}.d1", u)
                    step(v, "vector", v.tensor_tensor(z.sl, z.n, z.t, ALU.add), f"{k}.sl", u)
            for u in LANES:
                v.wait_ge(*at("B.y_p", u))
                norm_vector_1(v, "B", u, ps[u][:, 0, 0:S].rearrange("p (i d) -> p i d", i=TT))
            for u in LANES:
                norm_vector_2(v, "B", u)

        def b_weigh(v, k, g):
            n = min(2, MT - 2 * g)
            q = rows(2 * g + n - 1)
            for u in LANES:
                z = SB[u]
                v.wait_ge(*at(f"{k}.att{2 * g + n - 1}", u))
                step(v, "vector", v.reciprocal(z.rs[0:q, 2 * g:2 * g + n], z.rs[0:q, 2 * g:2 * g + n]), f"{k}.rs{g}", u)
                mark(v, "vector", v.tensor_tensor(z.pw[0:q, 2 * g:2 * g + n, :], z.p[0:q, 2 * g:2 * g + n, :],
                                                  over(z.rs[0:q, 2 * g:2 * g + n].unsqueeze(2), [q, n, P + 1]), ALU.mult), f"{k}.pw{g}", u)

        def b_scalar(a):
            for u in LANES:
                z = SB[u]
                a.wait_ge(*at("B.vv", u))
                step(a, "scalar", a.activation(z.t1, z.vv, ACT.Ln), "B.cln", u)
                step(a, "scalar", a.activation(z.rr, z.t1, ACT.Exp, scale=-0.5), "B.cpower", u)
            for u in LANES:
                a.wait_ge(*at("B.pT_p", u))
                step(a, "scalar", a.activation(SB[u].pT, ps[u][:, :, :].rearrange("p b c -> p (b c)")[:, 0:SC], ACT.Copy), "B.pT", u)
            for u in LANES:
                a.wait_ge(*at("B.xnT_p", u))
                step(a, "scalar", a.activation(kvT[u][:, 0:SC], ps[u][:, :, :].rearrange("p b c -> p (b c)")[:, 0:SC], ACT.Identity,
                                               scale=e_ln[:, 0:1], bias=e_ln[:, 1:2]), "B.xnT", u)
            for r in range(ITERS):
                k = f"B.{r}"
                for u in LANES:
                    z = SB[u]
                    a.wait_ge(*at(f"{k}.ms_p", u))
                    step(a, "scalar", a.activation(z.t, ps[u][:, 3, 0:S], ACT.Ln, bias=eps6[:, 0:1]), f"{k}.ln", u)
                    step(a, "scalar", a.activation(z.t, z.t, ACT.Exp, scale=-0.5), f"{k}.power", u)
                for g in range(MP):
                    for u in LANES:
                        z = SB[u]
                        a.wait_ge(*at(f"{k}.nmx{g}", u))
                        for m in range(2 * g, min(2 * g + 2, MT)):
                            q = rows(m)
                            mark(a, "scalar", a.activation(z.att[0:q, m, :], ps[u][0:q, g % 2, S * (m % 2):S * (m % 2) + S], ACT.Exp,
                                                           bias=z.mx[0:q, m:m + 1], accum_out=z.rs[0:q, m:m + 1]), f"{k}.att{m}", u)
                for u in LANES:
                    a.wait_ge(*at(f"{k}.uT_p", u))
                    step(a, "scalar", a.activation(SB[u].uT, ps[u][:, 0, 0:S], ACT.Copy), f"{k}.uT", u)
                for u in LANES:
                    z = SB[u]
                    a.wait_ge(*at(f"{k}.gru_p", u))
                    for j, name in enumerate(("er", "ez")):
                        mark(a, "scalar", a.activation(z.rz[:, S * j:S * j + S], ps[u][:, 1, S * j:S * j + S], ACT.Exp, scale=-1.0, bias=b_small[:, j:j + 1]), f"{k}.{name}", u)
                for u in LANES:
                    z = SB[u]
                    a.wait_ge(*at(f"{k}.t1", u))
                    step(a, "scalar", a.activation(z.n, z.t, ACT.Exp, scale=2.0, bias=b_small[:, 2:3]), f"{k}.en", u)
            for u in LANES:
                norm_scalar(a, "B", u)

        def b_pool(g):
            for u in LANES:
                z = SB[u]
                g.wait_ge(*at("B.c.rstd", u))
                step(g, "pool", g.tensor_tensor(z.xn, z.ctx, over(z.mean.unsqueeze(2), [P, MT, P]), ALU.subtract), "B.xn0", u)
                step(g, "pool", g.tensor_tensor(z.xn, z.xn, over(z.rr[:, 0, :].unsqueeze(2), [P, MT, P]), ALU.mult), "B.xn", u)

        CH, CD, CE = 16, 64, 8
        CP = CH // 2
        c_wkT = sb("c_wkT", [P, CH * CD])
        c_wvT = sb("c_wvT", [P, CE * CD])
        c_wgT = sb("c_wgT", [P, 2 * CH * CE])
        c_woT = sb("c_woT", [P, 4, P])
        c_order = sb("c_order", [P, CE])
        cp_ = [sb(f"c_prob{i}", [P, TT, S]) for i in range(2)]
        ct_ = [sb(f"c_probT{i}", [P, TT, S]) for i in range(2)]

        class StageC:
            def __init__(self, u):
                c = Carve(u)
                self.gT = c(TT, 4, P)
                c(CP * S - TT * 4 * P)
                self.k = c(CP, S)
                self.pv = c(TT, CE, CD)
                self.v = c(TT, CH, CD)
                self.att = c(TT, CH, CD)
                self.e1 = c(2048)
                self.gate = c(TT, 2, CH, CE)
                self.k1 = c(TT, 2, CH, CE)
                self.k2 = c(TT, 2, CH, CE)
                self.ix = c(TT, 2, CH, CE)
                self.m = c(TT * 2 * CH)
                self.mix = c(TT, CH, CE)
                self.mx = c(CH, TT)
                self.rs = c(CH, TT)
                self.e2 = c(2048)
                self.prod = [self.e1, self.e2]
                self.g = self.pv

        SC_ = [StageC(u) for u in LANES]
        c_q = [area[1][:, 1024 * i:1024 * i + 1024].rearrange("p (h q) -> p h q", h=4) for i in range(2)]
        C_UNITS = [(u, h) for u in LANES for h in range(CH)]

        def c_load(sp):
            def rows_of(t):
                return t.rearrange("a b c -> (a b) c").rearrange("(g p) c -> p g c", p=P)
            def part(u, a, g):
                return kvT[u][:, a:a + g * P].rearrange("p (g c) -> p g c", g=g)
            sp.dma_start(part(0, 0, 8), rows_of(w["L0_ffn_Wq"])).then_inc(s_weights, 16)
            sp.dma_start(part(1, 0, 8), rows_of(w["L0_ffn_Wk"])).then_inc(s_weights, 16)
            sp.dma_start(part(0, 1024, 4), rows_of(w["L0_ffn_Wv"])).then_inc(s_weights, 16)
            sp.dma_start(part(0, 1536, 1), rows_of(w["L0_ffn_Ws"])).then_inc(s_weights, 16)
            sp.dma_start(part(1, 1536, 1), rows_of(w["L0_ffn_Wd"])).then_inc(s_weights, 16)
            sp.dma_start(kvT[1][:, 1024:1536].rearrange("p (e d) -> p e d", e=CE), w["L0_ffn_Wo"].rearrange("e f d -> f e d")).then_inc(s_weights, 16)

        def c_setup_pool(g):
            for e in range(CE):
                g.memset(c_order[:, e:e + 1], float(CE - e)).then_inc(s_pool, 1)

        def c_setup_tensor(pe):
            for i in range(8):
                for u in LANES:
                    m = pe.transpose(ps[1][:, 2 * u + i // 4, P * (i % 4):P * (i % 4) + P], kvT[u][:, P * i:P * i + P], ident[:, :])
            m.then_inc(*done("tensor", "setup.c1_p"))
            pe.wait_ge(*at("setup.c_wk"))
            for i in range(4):
                pe.transpose(ps[1][:, 0, P * i:P * i + P], kvT[0][:, 1024 + P * i:1024 + P * i + P], ident[:, :])
                pe.transpose(ps[1][:, 1, P * i:P * i + P], kvT[1][:, 1024 + P * i:1024 + P * i + P], ident[:, :])
            for u in LANES:
                m = pe.transpose(ps[1][:, 2, P * u:P * u + P], kvT[u][:, 1536:1536 + P], ident[:, :])
            m.then_inc(*done("tensor", "setup.c2_p"))

        def c_setup_vector(v):
            v.wait_ge(*at("setup.c1_p"))
            step(v, "vector", v.tensor_scalar(c_wqT[:, :], ps[1][:, 0:2, :].rearrange("p a b -> p (a b)"), float(CD) ** -0.5, None, ALU.mult), "setup.c_wq")
            step(v, "vector", v.tensor_copy(c_wkT[:, :], ps[1][:, 2:4, :].rearrange("p a b -> p (a b)")), "setup.c_wk")
            v.wait_ge(*at("setup.c2_p"))
            step(v, "vector", v.tensor_copy(c_wvT[:, :], ps[1][:, 0, :]), "setup.c_wv")
            step(v, "vector", v.tensor_copy(c_woT[:, :, :], ps[1][:, 1, :].rearrange("p (a b) -> p a b", a=4)), "setup.c_wo")
            step(v, "vector", v.tensor_copy(c_wgT[:, :], ps[1][:, 2, 0:2 * P]), "setup.c_wg")

        def transposed_x(pe, tag):
            for u in LANES:
                for i in range(TT):
                    m = pe.transpose(ps[u][:, 0, P * i:P * i + P], X[u][:, i, :], ident[:, :])
                m.then_inc(*done("tensor", f"{tag}.xT_p", u))

        def copy_xT(v, tag):
            for u in LANES:
                v.wait_ge(*at(f"{tag}.xT_p", u))
                step(v, "vector", v.tensor_copy(XT[u][:, :], ps[u][:, 0, 0:S]), f"{tag}.xT", u)

        C_GROUPS = len(LANES) * 2 * (CH // 4)
        C_QK_AT = {4 * (m // 2 - 1) + m % 2: m for m in range(2, C_GROUPS)}

        def c_qk_tensor(pe, m):
            u, j = m // 8, m % 8 // 2
            weights = c_wqT if m % 2 == 0 else c_wkT
            if m >= 2:
                pe.wait_ge(*at(f"C.qk{m - 2}"))
            for c in range(2):
                q = pe.matmul(ps[1][:, 2 + m % 2, S * c:S * c + S], weights[:, P * (2 * j + c):P * (2 * j + c) + P], XT[u][:, :], start=True, stop=True)
            q.then_inc(*done("tensor", f"C.qk_p{m}"))

        def c_qk_scalar(a, m):
            u, j = m // 8, m % 8 // 2
            if m == 0:
                a.wait_ge(*at("C.zero"))
            a.wait_ge(*at(f"C.qk_p{m}"))
            if m % 2 == 0:
                if m >= 4:
                    a.wait_ge(*at(f"C.s_p{4 * (m // 2 - 2) + 3}"))
                for half in range(2):
                    r = CD * half
                    mark(a, "scalar", a.activation(c_q[m // 2 % 2][r:r + CD, half:4:2, :], ps[1][r:r + CD, 2, :].rearrange("p (c q) -> p c q", c=2), ACT.Copy),
                         f"C.qk{m}" if half else f"C.qka{m}")
            else:
                mark(a, "scalar", a.activation(SC_[u].k[:, 2 * j:2 * j + 2, :].rearrange("p a b -> p (a b)"), ps[1][:, 3, :], ACT.Copy), f"C.qk{m}")

        def c_pv_banks(u):
            return ps[0][:, 2:4, :] if u == 0 else ps[1][:, 0:2, :]

        def c_tensor(pe):
            for u in LANES:
                pe.wait_ge(*at("B.x1", u))
                for i in range(TT):
                    m = pe.transpose(ps[u][:, 0, P * i:P * i + P], X[u][:, i, :], ident[:, :])
                m.then_inc(*done("tensor", "C.xT_p", u))
            for u in LANES:
                pe.wait_ge(*at("C.xT", u))
                for i in range(TT):
                    m = pe.matmul(ps[0][:, u, S * i:S * i + S], XT[u][:, P * i:P * i + P], c_wgT[:, :], start=True, stop=True)
                m.then_inc(*done("tensor", "C.gate_p", u))
            for m in range(2):
                c_qk_tensor(pe, m)
            for u in LANES:
                for i in range(TT):
                    m = pe.matmul(c_pv_banks(u)[:, i, :], XT[u][:, P * i:P * i + P], c_wvT[:, :], start=True, stop=True)
                m.then_inc(*done("tensor", "C.pv_p", u))
            last = len(C_UNITS)
            for n in range(last + 2):
                if n < last:
                    u, h = C_UNITS[n]
                    z = SC_[u]
                    if n < 2:
                        pe.wait_ge(*at("C.gate", n))
                    if n >= 2:
                        pe.wait_ge(*at(f"C.exp{n - 2}"))
                    if h % 4 == 0:
                        pe.wait_ge(*at(f"C.qk{CH // 2 * u + 2 * (h // 4) + 1}"))
                    for i in range(TT):
                        m = pe.matmul(ps[0][:, n % 2, S * i:S * i + S], c_q[n // 4 % 2][:, h % 4, P * i:P * i + P], z.k[:, h // 2, :], start=True, stop=True)
                    m.then_inc(*done("tensor", f"C.s_p{n}"))
                if n in C_QK_AT:
                    c_qk_tensor(pe, C_QK_AT[n])
                if 1 <= n < last + 1:
                    o = n - 1
                    pe.wait_ge(*at(f"C.exp{o}"))
                    if o == 0:
                        pe.wait_ge(*at("C.pv", 0))
                    if o >= 2:
                        pe.wait_ge(*at(f"C.pT{o - 2}"))
                    for j in range(TT):
                        for i in range(TT):
                            m = pe.transpose(ps[0][:, 2 + o % 2, S * j + P * i:S * j + P * i + P], cp_[o % 2][:, i, P * j:P * j + P], ident[:, :])
                    m.then_inc(*done("tensor", f"C.pT_p{o}"))
                if n >= 2:
                    o = n - 2
                    u, h = C_UNITS[o]
                    z = SC_[u]
                    if o == 0:
                        pe.wait_ge(*at("C.pv", 1))
                    if h % 4 == 0:
                        pe.wait_ge(*at(f"C.v{2 * (h // 4) + 1}", u))
                    pe.wait_ge(*at(f"C.pT{o}"))
                    if o >= 2:
                        pe.wait_ge(*at(f"C.att{o - 2}"))
                    for i in range(TT):
                        for j in range(TT):
                            m = pe.matmul(ps[1][:, o % 2, CD * i:CD * i + CD], ct_[o % 2][:, j, P * i:P * i + P], z.v[:, j, h, :], start=j == 0, stop=j == TT - 1)
                    m.then_inc(*done("tensor", f"C.o_p{o}"))
            for u in LANES:
                z = SC_[u]
                pe.wait_ge(*at("C.g7", u))
                if u == 1:
                    pe.wait_ge(*at("C.res", 0))
                for i in range(TT):
                    for c in range(4):
                        m = pe.transpose(ps[1][:, 2 + i, P * c:P * c + P], z.g[:, i, 2 * c:2 * c + 2, :], ident[:, :])
                m.then_inc(*done("tensor", "C.gT_p", u))
                if u == 0:
                    pe.wait_ge(*at(f"C.att{last - 1}"))
                pe.wait_ge(*at("C.gT", u))
                for i in range(TT):
                    for c in range(4):
                        m = pe.matmul(ps[1][:, u, P * i:P * i + P], z.gT[:, i, c, :], c_woT[:, c, :], start=c == 0, stop=c == 3)
                m.then_inc(*done("tensor", "C.y_p", u))

        def c_pick(v, u, gate, k, ix, m, name):
            gr = gate.rearrange("p i k h e -> p (i k h) e")
            kr = k.rearrange("p i k h e -> p (i k h) e")
            ir = ix.rearrange("p i k h e -> p (i k h) e")
            mb = over(m.unsqueeze(2), [P, TT * 2 * CH, CE])
            step(v, "vector", v.tensor_reduce(m, gr, AX.X, ALU.max), f"C.{name}m", u)
            step(v, "vector", v.tensor_tensor(ir, gr, mb, ALU.is_equal), f"C.{name}e", u)
            step(v, "vector", v.tensor_tensor(ir, ir, over(c_order[:, :].unsqueeze(1), [P, TT * 2 * CH, CE]), ALU.mult), f"C.{name}i", u)
            step(v, "vector", v.tensor_reduce(m, ir, AX.X, ALU.max), f"C.{name}f", u)
            step(v, "vector", v.tensor_tensor(kr, ir, mb, ALU.is_equal), f"C.{name}", u)

        def c_gates_vector(v, u):
            z = SC_[u]
            flat = "p i k h e -> p (i k h e)"
            c_pick(v, u, z.gate, z.k1, z.ix, z.m, "k1")
            step(v, "vector", v.scalar_tensor_tensor(out=z.k2.rearrange(flat), in0=z.k1.rearrange(flat), scalar=NEG, in1=z.gate.rearrange(flat), op0=ALU.mult, op1=ALU.add), "C.rest", u)
            c_pick(v, u, z.k2, z.k2, z.ix, z.m, "k2")
            step(v, "vector", v.tensor_tensor(z.k1.rearrange(flat), z.k1.rearrange(flat), z.k2.rearrange(flat), ALU.add), "C.mask", u)
            v.wait_ge(*at("C.sig", u))
            mark(v, "vector", v.tensor_tensor(z.mix, z.mix, z.k1[:, :, 0, :, :], ALU.mult), "C.mix", u)

        def c_v_vector(v, m):
            u, j, i = m // 8, m % 8 // 2, m % 2
            z = SC_[u]
            v.wait_ge(*at(f"C.prodv{m % 8}", u))
            mark(v, "vector", v.tensor_reduce(z.v[:, i, 4 * j:4 * j + 4, :], z.prod[m % 2].rearrange("p (h e d) -> p h d e", h=4, e=CE), AX.X, ALU.add),
                 f"C.v{m % 8}", u)

        def c_g_vector(v, u, n):
            i, c = n // 4, n % 4
            z = SC_[u]
            v.wait_ge(*at(f"C.prodo{n}", u))
            mark(v, "vector", v.tensor_reduce(z.g[:, i, 2 * c:2 * c + 2, :], z.prod[n % 2].rearrange("p (e h d) -> p e d h", e=2, h=CH), AX.X, ALU.add),
                 f"C.g{n}", u)

        C_G_AT = {19: 0, 21: 1, 23: 2, 24: 3, 26: 4, 28: 5, 30: 6, 32: 7}

        def c_vector(v):
            for u in LANES:
                v.wait_ge(*at("C.xT_p", u))
                mark(v, "vector", v.tensor_copy(XT[u][:, :], ps[u][:, 0, 0:S]), "C.xT", u)
            for u in LANES:
                v.wait_ge(*at("C.gate_p", u))
                step(v, "vector", v.tensor_copy(SC_[u].gate.rearrange("p i k h e -> p (i k h e)"), ps[0][:, u, :]), "C.gate", u)
            for u in LANES:
                c_gates_vector(v, u)
            for m in range(2):
                c_v_vector(v, m)
            last = len(C_UNITS)
            for n in range(last + 2):
                if n < last:
                    u, h = C_UNITS[n]
                    z = SC_[u]
                    v.wait_ge(*at(f"C.s_p{n}"))
                    mark(v, "vector", v.tensor_reduce(z.mx[:, h, :], ps[0][:, n % 2, :].rearrange("p (i k) -> p i k", i=TT), AX.X, ALU.max, negate=True), f"C.nmx{n}")
                if n + 2 < C_GROUPS:
                    c_v_vector(v, n + 2)
                if n in C_G_AT:
                    c_g_vector(v, 0, C_G_AT[n])
                if n >= 2:
                    o = n - 2
                    u, h = C_UNITS[o]
                    z = SC_[u]
                    v.wait_ge(*at(f"C.exp{o}"))
                    step(v, "vector", v.reciprocal(z.rs[:, h, :], z.rs[:, h, :]), f"C.rs{o}", 0)
                    v.wait_ge(*at(f"C.o_p{o}"))
                    mark(v, "vector", v.tensor_tensor(z.att[:, :, h, :], ps[1][:, o % 2, 0:TT * CD].rearrange("p (i d) -> p i d", i=TT),
                                                      over(z.rs[:, h, :].unsqueeze(2), [P, TT, CD]), ALU.mult), f"C.att{o}")
            for n in range(3):
                c_g_vector(v, 1, n)
            v.wait_ge(*at("C.y_p", 0))
            norm_vector_1(v, "C", 0, ps[1][:, 0, 0:S].rearrange("p (i d) -> p i d", i=TT))
            for n in range(3, 6):
                c_g_vector(v, 1, n)
            norm_vector_2(v, "C", 0)
            for n in range(6, 8):
                c_g_vector(v, 1, n)
            v.wait_ge(*at("C.y_p", 1))
            norm_vector_1(v, "C", 1, ps[1][:, 1, 0:S].rearrange("p (i d) -> p i d", i=TT))
            norm_vector_2(v, "C", 1)

        def c_scalar(a):
            for u in LANES:
                z = SC_[u]
                a.wait_ge(*at("C.gate", u))
                step(a, "scalar", a.activation(z.mix, z.gate[:, :, 0, :, :], ACT.Exp, scale=-1.0), "C.gexp", u)
                step(a, "scalar", a.activation(z.mix, z.mix, ACT.Ln, bias=one_col[:, 0:1]), "C.gln", u)
                mark(a, "scalar", a.activation(z.mix, z.mix, ACT.Exp, scale=-1.0), "C.sig", u)
            for m in range(2):
                c_qk_scalar(a, m)
            for u in LANES:
                a.wait_ge(*at("C.pv_p", u))
                mark(a, "scalar", a.activation(SC_[u].pv.rearrange("p i e d -> p (i e d)"), c_pv_banks(u).rearrange("p a b -> p (a b)"), ACT.Copy), "C.pv", u)
            last = len(C_UNITS)
            for n in range(last + 1):
                if n < last:
                    u, h = C_UNITS[n]
                    z = SC_[u]
                    a.wait_ge(*at(f"C.nmx{n}"))
                    if n >= 2:
                        a.wait_ge(*at(f"C.pT_p{n - 2}"))
                    for i in range(TT):
                        m = a.activation(cp_[n % 2][:, i, :], ps[0][:, n % 2, S * i:S * i + S], ACT.Exp, bias=z.mx[:, h, i:i + 1], accum_out=z.rs[:, h, i:i + 1])
                        mark(a, "scalar", m, f"C.exp{n}" if i == TT - 1 else f"C.expa{n}")
                if n in C_QK_AT:
                    c_qk_scalar(a, C_QK_AT[n])
                if n >= 1:
                    o = n - 1
                    a.wait_ge(*at(f"C.pT_p{o}"))
                    if o >= 2:
                        a.wait_ge(*at(f"C.o_p{o - 2}"))
                    mark(a, "scalar", a.activation(ct_[o % 2][:, :, :].rearrange("p j i -> p (j i)"), ps[0][:, 2 + o % 2, :], ACT.Copy), f"C.pT{o}")
            for u in LANES:
                z = SC_[u]
                a.wait_ge(*at("C.gT_p", u))
                mark(a, "scalar", a.activation(z.gT.rearrange("p i c q -> p (i c q)"), ps[1][:, 2:4, :].rearrange("p a b -> p (a b)"), ACT.Copy), "C.gT", u)
                norm_scalar(a, "C", u)

        def c_pool(g):
            g.wait_ge(*at("B.x1", 1))
            mark(g, "pool", g.memset(area[1][:, 0:2048], 0.0), "C.zero")
            for u in LANES:
                z = SC_[u]
                g.wait_ge(*at("C.mix", u))
                g.wait_ge(*at("C.pv", u))
                for n in range(8):
                    j, i = n // 2, n % 2
                    if n >= 2:
                        g.wait_ge(*at(f"C.v{n - 2}", u))
                    mark(g, "pool", g.tensor_tensor(z.prod[n % 2].rearrange("p (h e d) -> p h e d", h=4, e=CE),
                                                    over(z.mix[:, i, 4 * j:4 * j + 4, :].unsqueeze(3), [P, 4, CE, CD]),
                                                    over(z.pv[:, i:i + 1, :, :], [P, 4, CE, CD]), ALU.mult), f"C.prodv{n}", u)
            for u in LANES:
                z = SC_[u]
                g.wait_ge(*at(f"C.att{CH * u + CH - 1}"))
                for n in range(8):
                    i, c = n // 4, n % 4
                    if n >= 2:
                        g.wait_ge(*at(f"C.g{n - 2}", u))
                    mark(g, "pool", g.tensor_tensor(z.prod[n % 2].rearrange("p (e h d) -> p e h d", e=2, h=CH),
                                                    over(z.k1[:, i, 1, :, 2 * c:2 * c + 2].rearrange("p h e -> p e h").unsqueeze(3), [P, 2, CH, CD]),
                                                    over(z.att[:, i:i + 1, :, :], [P, 2, CH, CD]), ALU.mult), f"C.prodo{n}", u)

        DI, DS, DJ = 256, 16, 2
        NC_ = 4
        SELU_L, SELU_A = 1.0507009873554805, 1.6732632423543772
        d_win = sb("d_win", [P, DI])
        d_bin = sb("d_bin", [P, DJ])
        d_A = sb("d_A", [P, DJ, DS])
        d_wbc = sb("d_wbc", [P, DJ, 2 * DS])
        d_bbc = sb("d_bbc", [2 * DS, 1])
        d_wd = sb("d_wd", [P, DJ, DI])
        d_bd = sb("d_bd", [P, DJ])
        d_D = sb("d_D", [P, DJ])
        d_wo = sb("d_wo", [P, DJ, P])
        d_bo = sb("d_bo", [1, P])
        d_pick = sb("d_pick", [96, 2 * DS])
        d_sel = sb("d_sel", [96, 2 * DS, P], BF16)
        d_bc3 = [sb(f"d_bc3{u}", [96, S], BF16) for u in LANES]
        one_col = sb("one_col", [P, 1])

        class StageD:
            def __init__(self, u):
                c = Carve(u)
                self.h = c(DJ, S)
                self.lo = c(DJ, S)
                self.hi = c(DJ, S)
                self.a = c(DJ, S)
                self.dt = c(DJ, S)
                self.dh = c(DJ, S)
                self.bc = c(S)
                self.part = c(S)
                self.dA = [c(NC_, S) for _ in range(2)]
                self.dBu = c(NC_, S)
                self.s = c(NC_, S)
                self.yc = [c(NC_, S) for _ in range(2)]
                self.ys = [c(NC_, S) for _ in range(DJ)]
                self.y = c(DJ, S)

        SD = [StageD(u) for u in LANES]

        def d_load(sp):
            def jp(t):
                return t.rearrange("(j p) c -> p j c", p=P)
            n = "L1_attn_"
            sp.dma_start(d_win[:, :], w[n + "W_in"]).then_inc(s_weights, 16)
            sp.dma_start(d_bin[:, :], col(n + "b_in"), allow_slow_non_contiguous=True).then_inc(s_weights, 16)
            sp.dma_start(d_A[:, :, :], jp(w[n + "A_log"])).then_inc(s_weights, 16)
            sp.dma_start(d_wbc[:, :, 0:DS], jp(w[n + "W_B"])).then_inc(s_weights, 16)
            sp.dma_start(d_wbc[:, :, DS:2 * DS], jp(w[n + "W_C"])).then_inc(s_weights, 16)
            sp.dma_start(d_bbc[0:DS, :], w[n + "b_B"].rearrange("(p a) -> p a", a=1)).then_inc(s_weights, 16)
            sp.dma_start(d_bbc[DS:2 * DS, :], w[n + "b_C"].rearrange("(p a) -> p a", a=1)).then_inc(s_weights, 16)
            sp.dma_start(d_wd[:, :, :], jp(w[n + "W_delta"])).then_inc(s_weights, 16)
            sp.dma_start(d_bd[:, :], col(n + "b_delta"), allow_slow_non_contiguous=True).then_inc(s_weights, 16)
            sp.dma_start(d_D[:, :], col(n + "D_param"), allow_slow_non_contiguous=True).then_inc(s_weights, 16)
            sp.dma_start(d_wo[:, :, :], jp(w[n + "W_out"])).then_inc(s_weights, 16)
            sp.dma_start(d_bo[:, :], w[n + "b_out"].rearrange("(a p) -> a p", a=1)).then_inc(s_weights, 16)

        def d_setup_pool(g):
            g.memset(one_col[:, :], 1.0).then_inc(s_pool, 1)

        def d_setup_scalar(a):
            a.wait_ge(s_weights, 16 * 54)
            step(a, "scalar", a.activation(d_A[:, :, :], d_A[:, :, :], ACT.Exp), "setup.expA")

        def d_setup_vector(v):
            v.wait_ge(*at("setup.expA"))
            step(v, "vector", v.tensor_scalar(d_A[:, :, :], d_A[:, :, :], -1.0, None, ALU.mult), "setup.A")
            step(v, "vector", v.tensor_tensor(d_pick[:, :], ident[0:96, 0:32], ident[0:96, 32:64], ALU.add), "setup.pick0")
            step(v, "vector", v.tensor_tensor(d_pick[:, :], d_pick[:, :], ident[0:96, 64:96], ALU.add), "setup.pick")
            step(v, "vector", v.tensor_copy(d_sel[:, :, :], over(d_pick[:, :].unsqueeze(2), [96, 2 * DS, P])), "setup.sel")

        def d_tensor(pe):
            for u in LANES:
                pe.wait_ge(*at("C.x1", u))
                for i in range(TT):
                    m = pe.transpose(ps[u][:, 0, P * i:P * i + P], X[u][:, i, :], ident[:, :])
                m.then_inc(*done("tensor", "D.xT_p", u))
            for u in LANES:
                pe.wait_ge(*at("D.xT", u))
                for j in range(DJ):
                    m = pe.matmul(ps[u][:, 1, S * j:S * j + S], d_win[:, P * j:P * j + P], XT[u][:, :], start=True, stop=True)
                m.then_inc(*done("tensor", "D.h_p", u))
            for u in LANES:
                z = SD[u]
                pe.wait_ge(*at("D.h", u))
                for k in range(DJ):
                    m = pe.matmul(ps[u][0:2 * DS, 2, 0:S], d_wbc[:, k, :], z.h[:, k, :], start=k == 0, stop=k == 1)
                m.then_inc(*done("tensor", "D.bc_p", u))
                for j in range(DJ):
                    for k in range(DJ):
                        m = pe.matmul(ps[u][:, 3, S * j:S * j + S], d_wd[:, k, P * j:P * j + P], z.h[:, k, :], start=k == 0, stop=k == 1)
                m.then_inc(*done("tensor", "D.delta_p", u))
            for c in range(DS // NC_):
                for u in LANES:
                    pe.wait_ge(*at("D.bc3" if c == 0 else f"D.dbu{c - 1}1", u))
                    for n in range(NC_):
                        m = pe.matmul(ps[u][:, n // 2, S * (n % 2):S * (n % 2) + S], d_sel[:, NC_ * c + n, :], d_bc3[u][:, :], start=True, stop=True)
                    m.then_inc(*done("tensor", f"D.b_p{c}", u))
                for u in LANES:
                    pe.wait_ge(*at("D.dh" if c == 0 else f"D.yc{c - 1}1", u))
                    for n in range(NC_):
                        m = pe.matmul(ps[u][:, 2 + n // 2, S * (n % 2):S * (n % 2) + S], d_sel[:, DS + NC_ * c + n, :], d_bc3[u][:, :], start=True, stop=True)
                    m.then_inc(*done("tensor", f"D.c_p{c}", u))
            for u in LANES:
                z = SD[u]
                pe.wait_ge(*at("D.y", u))
                for i in range(TT):
                    for j in range(DJ):
                        pe.matmul(ps[u][:, 0, P * i:P * i + P], z.y[:, j, P * i:P * i + P], d_wo[:, j, :], start=j == 0, stop=False)
                    m = pe.matmul(ps[u][:, 0, P * i:P * i + P], ones_row[:, :], d_bo[:, :], start=False, stop=True)
                m.then_inc(*done("tensor", "D.y_p", u))

        def d_vector(v):
            copy_xT(v, "D")
            for u in LANES:
                z = SD[u]
                v.wait_ge(*at("D.h_p", u))
                for j in range(DJ):
                    mark(v, "vector", v.tensor_scalar(z.lo[:, j, :], ps[u][:, 1, S * j:S * j + S], d_bin[:, j:j + 1], 0.0, ALU.add, ALU.min), f"D.lo{j}", u)
                for j in range(DJ):
                    mark(v, "vector", v.tensor_scalar(z.hi[:, j, :], ps[u][:, 1, S * j:S * j + S], d_bin[:, j:j + 1], 0.0, ALU.add, ALU.max), f"D.hi{j}", u)
            for u in LANES:
                z = SD[u]
                v.wait_ge(*at("D.elo", u))
                step(v, "vector", v.tensor_scalar(z.lo, z.lo, SELU_L * SELU_A, -SELU_L * SELU_A, ALU.mult, ALU.add), "D.neg", u)
                step(v, "vector", v.scalar_tensor_tensor(out=z.h, in0=z.hi, scalar=SELU_L, in1=z.lo, op0=ALU.mult, op1=ALU.add), "D.h", u)
            for u in LANES:
                z = SD[u]
                v.wait_ge(*at("D.bc_p", u))
                r = slice(0, 2 * DS)
                step(v, "vector", v.tensor_scalar(z.bc[r, :], ps[u][r, 2, 0:S], d_bbc[:, :], None, ALU.add), "D.bc", u)
                for k in range(3):
                    step(v, "vector", v.tensor_copy(d_bc3[u][32 * k:32 * k + 32, :], z.bc[r, :]), f"D.bc3{k}" if k < 2 else "D.bc3", u)
                    if k < 2:
                        step(v, "vector", v.tensor_copy(z.part[r, :], d_bc3[u][32 * k:32 * k + 32, :]), f"D.part{k}", u)
                        step(v, "vector", v.tensor_tensor(z.bc[r, :], z.bc[r, :], z.part[r, :], ALU.subtract), f"D.rest{k}", u)
                v.wait_ge(*at("D.delta_p", u))
                for j in range(DJ):
                    mark(v, "vector", v.tensor_scalar(z.a[:, j, :], ps[u][:, 3, S * j:S * j + S], d_bd[:, j:j + 1], None, ALU.add), f"D.a{j}", u)
                v.wait_ge(*at("D.a1", u))
                mark(v, "vector", v.scalar_tensor_tensor(out=z.dt, in0=z.a, scalar=-1.0, in1=z.a, op0=ALU.mult, op1=ALU.max), "D.abs", u)
            for u in LANES:
                z = SD[u]
                v.wait_ge(*at("D.log", u))
                step(v, "vector", v.scalar_tensor_tensor(out=z.dt, in0=z.a, scalar=0.0, in1=z.dt, op0=ALU.max, op1=ALU.add), "D.dt", u)
                step(v, "vector", v.tensor_tensor(z.dh, z.dt, z.h, ALU.mult), "D.dh", u)
                for b in range(2):
                    step(v, "vector", v.memset(z.dA[b][:, :, 0:1], 0.0), f"D.start{b}", u)
            for c in range(DS // NC_):
                for u in LANES:
                    z = SD[u]
                    for j in range(DJ):
                        if j == 0:
                            v.wait_ge(*at(f"D.b_p{c}", u))
                        step(v, "vector", v.tensor_tensor(z.dBu, over(z.dh[:, j:j + 1, :], [P, NC_, S]), ps[u][:, 0:2, :].rearrange("p b (n t) -> p (b n) t", t=S), ALU.mult), f"D.dbu{c}{j}", u)
                        v.wait_ge(*at(f"D.dA{c}{j}", u))
                        step(v, "vector", v.tensor_tensor_scan(z.s.rearrange("p n t -> p (n t)"), z.dA[j].rearrange("p n t -> p (n t)"),
                                                               z.dBu.rearrange("p n t -> p (n t)"), 0.0, ALU.mult, ALU.add), f"D.s{c}{j}", u)
                        if j == 0:
                            v.wait_ge(*at(f"D.c_p{c}", u))
                        dst = z.ys[j] if c == 0 else z.yc[j]
                        if c >= 2:
                            v.wait_ge(*at(f"D.ys{c - 1}{j}", u))
                        step(v, "vector", v.tensor_tensor(dst, z.s, ps[u][:, 2:4, :].rearrange("p b (n t) -> p (b n) t", t=S), ALU.mult), f"D.yc{c}{j}", u)
            for u in LANES:
                z = SD[u]
                for j in range(DJ):
                    v.wait_ge(*at(f"D.ys{DS // NC_ - 1}{j}", u))
                    step(v, "vector", v.tensor_reduce(z.y[:, j, :], z.ys[j].rearrange("p n t -> p t n"), AX.X, ALU.add), f"D.y0{j}", u)
                    step(v, "vector", v.scalar_tensor_tensor(out=z.y[:, j, :], in0=z.h[:, j, :], scalar=d_D[:, j:j + 1], in1=z.y[:, j, :], op0=ALU.mult, op1=ALU.add), "D.y" if j else "D.y_", u)
            for u in LANES:
                v.wait_ge(*at("D.y_p", u))
                norm_vector_1(v, "D", u, ps[u][:, 0, 0:S].rearrange("p (i d) -> p i d", i=TT))
            for u in LANES:
                norm_vector_2(v, "D", u)

        def d_scalar(a):
            for u in LANES:
                z = SD[u]
                a.wait_ge(*at("D.lo1", u))
                step(a, "scalar", a.activation(z.lo, z.lo, ACT.Exp), "D.elo", u)
            for u in LANES:
                z = SD[u]
                a.wait_ge(*at("D.abs", u))
                step(a, "scalar", a.activation(z.dt, z.dt, ACT.Exp, scale=-1.0), "D.eabs", u)
                step(a, "scalar", a.activation(z.dt, z.dt, ACT.Ln, bias=one_col[:, 0:1]), "D.log", u)
            for c in range(DS // NC_):
                for u in LANES:
                    z = SD[u]
                    for j in range(DJ):
                        if c == 0 and j == 0:
                            a.wait_ge(*at("D.start1", u))
                        if c >= 1:
                            a.wait_ge(*at(f"D.s{c - 1}{j}", u))
                        for n in range(NC_):
                            s = NC_ * c + n
                            m = a.activation(z.dA[j][:, n, 1:S], z.dt[:, j, 1:S], ACT.Exp, scale=d_A[:, j, s:s + 1])
                            mark(a, "scalar", m, f"D.dA{c}{j}" if n == NC_ - 1 else f"D.dA{c}{j}_{n}", u)
            for u in LANES:
                norm_scalar(a, "D", u)

        def d_pool(g):
            for c in range(1, DS // NC_):
                for u in LANES:
                    z = SD[u]
                    for j in range(DJ):
                        g.wait_ge(*at(f"D.yc{c}{j}", u))
                        step(g, "pool", g.tensor_tensor(z.ys[j], z.ys[j], z.yc[j], ALU.add), f"D.ys{c}{j}", u)

        EH, ED = 8, 64
        ET = (KV + P - 1) // P
        EL = KV - (ET - 1) * P
        CHUNKS = [(BANK * i, min(BANK, KV - BANK * i)) for i in range((KV + BANK - 1) // BANK)]
        TC = [range(4 * c, min(4 * c + 4, ET)) for c in range(4)]
        e_wq = sb("e_wq", [P, EH * ED])
        e_wkv = sb("e_wkv", [P, 2 * EH * ED])
        e_wo = sb("e_wo", [P, 4, P])
        e_go = sb("e_go", [P, P])
        e_bo = sb("e_bo", [P, P])

        c0, c1 = Carve(0), Carve(1)
        e_k = c0(4, KV)
        e_v = c0(ET, EH * ED)
        e_s = [c1(KV) for _ in range(2)]
        e_pT = c1(ET, P)
        e_neg = c1(KV)
        e_q = [c1(EH, S) for _ in LANES]
        e_o = [c1(TT, EH, ED) for _ in LANES]
        e_oT = [c1(TT, 4, P) for _ in LANES]
        e_mx = [c1(EH, TT) for _ in LANES]
        e_rs = [c1(EH, TT) for _ in LANES]
        e_mask8 = sb("e_mask8", [P, SC], U8)
        E_UNITS = [(h, i) for h in range(EH) for i in range(TT)]
        NU = len(E_UNITS)

        def erows(t):
            return EL if t == ET - 1 else P

        def e_load(sp):
            n = "L1_xattn_"
            sp.dma_start(e_wq[:, :], w[n + "w_q"]).then_inc(s_weights, 16)
            sp.dma_start(e_wkv[:, :], w[n + "w_kv"]).then_inc(s_weights, 16)
            sp.dma_start(e_wo[:, :, :], w[n + "w_out"].rearrange("(c p) n -> p c n", p=P)).then_inc(s_weights, 16)
            sp.dma_start(e_go[:, :], w[n + "g_o"].rearrange("(a n) -> a n", a=1).to_broadcast([P, P])).then_inc(s_weights, 16)
            sp.dma_start(e_bo[:, :], w[n + "b_o"].rearrange("(a n) -> a n", a=1).to_broadcast([P, P])).then_inc(s_weights, 16)

        def e_sync(sp, it):
            for u in LANES:
                if u:
                    sp.wait_ge(*at("E.neg", 0))
                sp.dma_start(e_mask8[:, :], w["mask_BxS2_bf1"][it * 2 + u].unsqueeze(0).to_broadcast([P, SC])).then_inc(s_mask[u], 16)

        def e_transposes(pe, u, o, c):
            g = 4 * o + c
            if g >= 3:
                pe.wait_ge(*at(f"E.pT{g - 3}", u))
            for t in TC[c]:
                m = pe.transpose(ps[1][0:erows(t), g % 3, P * (t % 4):P * (t % 4) + P], e_s[o % 2][:, P * t:P * t + erows(t)], ident[:, :])
            m.then_inc(*done("tensor", f"E.pT_p{g}", u))

        def e_products(pe, u, o, c):
            h, i = E_UNITS[o]
            if c == 0 and o >= 1:
                pe.wait_ge(*at(f"E.att{o - 1}", u))
            pe.wait_ge(*at(f"E.pT{4 * o + c}", u))
            for t in TC[c]:
                m = pe.matmul(ps[1][:, 3, 0:ED], e_pT[0:erows(t), t, :], e_v[0:erows(t), t, ED * h:ED * h + ED], start=t == 0, stop=t == ET - 1)
            m.then_inc(*done("tensor", f"E.o_p{o}" if c == 3 else f"E.o_p{o}.{c}", u))

        def e_tensor(pe):
            for u in LANES:
                pe.wait_ge(*at("E.l.x1", u))
                for i in range(TT):
                    m = pe.transpose(ps[u][:, 0, P * i:P * i + P], res[u][:, i, :], ident[:, :])
                m.then_inc(*done("tensor", "E.lT_p", u))
            for u in LANES:
                pe.wait_ge(*at("E.lT", u))
                for c in range(4):
                    m = pe.matmul(ps[u][:, 1 + c // 2, S * (c % 2):S * (c % 2) + S], e_wq[:, P * c:P * c + P], kvT[u][:, SC:KV], start=True, stop=True)
                m.then_inc(*done("tensor", "E.q_p", u))
            for u in LANES:
                pe.wait_ge(*at("E.q", 0))
                pe.wait_ge(*at("E.q", 1))
                if u:
                    pe.wait_ge(*at(f"E.att{NU - 1}", 0))
                for g in range(8):
                    b = ps[g % 2]
                    if g >= 2:
                        pe.wait_ge(*at(f"E.kv{g - 2}", u))
                    if g < 4:
                        for j, (a0, n) in enumerate(CHUNKS):
                            m = pe.matmul(b[:, j, 0:n], e_wkv[:, P * g:P * g + P], kvT[u][:, a0:a0 + n], start=True, stop=True)
                    else:
                        for t in TC[g - 4]:
                            m = pe.matmul(b[0:erows(t), t % 4, :], kvT[u][:, P * t:P * t + erows(t)], e_wkv[:, 512:1024], start=True, stop=True)
                    m.then_inc(*done("tensor", f"E.kv_p{g}", u))
                pe.wait_ge(*at("E.kv6", u))
                pe.wait_ge(*at("E.kv7", u))
                for n in range(NU + 2):
                    for j, (a0, k) in enumerate(CHUNKS if n < NU else ()):
                        h, i = E_UNITS[n]
                        if n >= 1 and j == 0:
                            pe.wait_ge(*at(f"E.max{n - 1}", u))
                        m = pe.matmul(ps[0][:, j, 0:k], e_q[u][:, h, P * i:P * i + P], e_k[:, h // 2, a0:a0 + k], start=True, stop=True)
                        if j == len(CHUNKS) - 1:
                            m.then_inc(*done("tensor", f"E.s_p{n}", u))
                        if n >= 2 and j < 2:
                            e_products(pe, u, n - 2, 2 + j)
                    if n == NU:
                        for c in range(2, 4):
                            e_products(pe, u, n - 2, c)
                    if 1 <= n < NU + 1:
                        pe.wait_ge(*at(f"E.exp{n - 1}", u))
                        for c in range(3):
                            e_transposes(pe, u, n - 1, c)
                        e_products(pe, u, n - 1, 0)
                        e_transposes(pe, u, n - 1, 3)
                        e_products(pe, u, n - 1, 1)
                    if n == NU + 1:
                        for c in range(2, 4):
                            e_products(pe, u, n - 2, c)
            for u in LANES:
                pe.wait_ge(*at(f"E.att{NU - 1}", 1))
                for i in range(TT):
                    for c in range(4):
                        m = pe.transpose(ps[u][:, 2 + i, P * c:P * c + P], e_o[u][:, i, 2 * c:2 * c + 2, :], ident[:, :])
                m.then_inc(*done("tensor", "E.oT_p", u))
            for u in LANES:
                pe.wait_ge(*at("E.oT", u))
                for i in range(TT):
                    for c in range(4):
                        m = pe.matmul(ps[u][:, 0, P * i:P * i + P], e_oT[u][:, i, c, :], e_wo[:, c, :], start=c == 0, stop=c == 3)
                m.then_inc(*done("tensor", "E.y_p", u))

        def e_kv_copy(g):
            if g < 4:
                return (P, ps[g % 2][:, :, :].rearrange("p b c -> p (b c)")[:, 0:KV], e_k[:, g, :])
            t = TC[g - 4]
            return (P, ps[g % 2][:, 0:len(t), :], e_v[:, t[0]:t[0] + len(t), :])

        def e_vector(v):
            for u in LANES:
                moments(v, "E.l", u, X[u], 1e-5)
            for u in LANES:
                norm_vector_2(v, "E.l", u, X[u], res[u])
            for u in LANES:
                v.wait_ge(s_mask[u], 16)
                if u == 0:
                    v.wait_ge(*at("D.x1", 1))
                    step(v, "vector", v.memset(e_neg[:, SC:KV], 0.0), "E.neg0", u)
                step(v, "vector", v.tensor_scalar(e_neg[:, 0:SC], e_mask8[:, :], -1.0, -NEG, ALU.add, ALU.mult), "E.neg", u)
                for g in range(0, 8, 2):
                    v.wait_ge(*at(f"E.kv_p{g}", u))
                    q, src, dst = e_kv_copy(g)
                    step(v, "vector", v.tensor_copy(dst, src), f"E.kv{g}", u)
                for n in range(NU + 2):
                    if n >= 2:
                        o = n - 2
                        h, i = E_UNITS[o]
                        v.wait_ge(*at(f"E.exp{o}", u))
                        step(v, "vector", v.reciprocal(e_rs[u][:, h, i:i + 1], e_rs[u][:, h, i:i + 1]), f"E.rs{o}", u)
                        v.wait_ge(*at(f"E.o_p{o}", u))
                        mark(v, "vector", v.tensor_scalar(e_o[u][:, i, h, :], ps[1][:, 3, 0:ED], e_rs[u][:, h, i:i + 1], None, ALU.mult), f"E.att{o}", u)
                    if n < NU:
                        h, i = E_UNITS[n]
                        v.wait_ge(*at(f"E.s_p{n}", u))
                        if n >= 2:
                            v.wait_ge(*at(f"E.pT_p{4 * (n - 2) + 3}", u))
                        step(v, "vector", v.tensor_tensor_reduce(out=e_s[n % 2], in0=ps[0][:, :, :].rearrange("p b c -> p (b c)")[:, 0:KV], in1=e_neg,
                                                                 scale=1.0, scalar=-3.0e38, op0=ALU.add, op1=ALU.max, accum_out=e_mx[u][:, h, i:i + 1]), f"E.max{n}", u)
                        mark(v, "vector", v.tensor_scalar(e_mx[u][:, h, i:i + 1], e_mx[u][:, h, i:i + 1], -1.0, None, ALU.mult), f"E.nmx{n}", u)
            for u in LANES:
                v.wait_ge(*at("E.oT_p", u))
                step(v, "vector", v.tensor_copy(e_oT[u].rearrange("p i c q -> p (i c q)"), ps[u][:, 2:4, :].rearrange("p a b -> p (a b)")), "E.oT", u)
            for u in LANES:
                v.wait_ge(*at("E.y_p", u))
                step(v, "vector", v.tensor_copy(res[u][:, :, :], ps[u][:, 0, 0:S].rearrange("p (i d) -> p i d", i=TT)), "E.o.y", u)
                moments(v, "E.o", u, res[u], 1e-5)
            for u in LANES:
                norm_vector_2(v, "E.o", u, res[u], res[u])
                for name, gain, op in (("go", e_go, ALU.mult), ("bo", e_bo, ALU.add)):
                    step(v, "vector", v.tensor_tensor(res[u][:, :, :], res[u][:, :, :], over(gain[:, :].unsqueeze(1), [P, TT, P]), op), f"E.{name}", u)
                norm_vector_1(v, "E", u, res[u][:, :, :])
            for u in LANES:
                norm_vector_2(v, "E", u)

        def e_scalar(a):
            for u in LANES:
                norm_scalar(a, "E.l", u)
            for u in LANES:
                a.wait_ge(*at("E.lT_p", u))
                step(a, "scalar", a.activation(kvT[u][:, SC:KV], ps[u][:, 0, 0:S], ACT.Identity, scale=e_ln[:, 2:3], bias=e_ln[:, 3:4]), "E.lT", u)
            for u in LANES:
                a.wait_ge(*at("E.q_p", u))
                a.wait_ge(*at("E.zero", u))
                for half in range(2):
                    r = ED * half
                    mark(a, "scalar", a.activation(e_q[u][r:r + ED, half:EH:2, :], ps[u][r:r + ED, 1:3, :].rearrange("p a (b q) -> p (a b) q", b=2), ACT.Copy, scale=float(ED) ** -0.5),
                         "E.q" if half else "E.qa", u)
            for u in LANES:
                for g in range(1, 8, 2):
                    a.wait_ge(*at(f"E.kv_p{g}", u))
                    q, src, dst = e_kv_copy(g)
                    step(a, "scalar", a.activation(dst, src, ACT.Copy), f"E.kv{g}", u)
                for n in range(NU + 1):
                    if n >= 1:
                        o = n - 1
                        for c in range(4):
                            t = TC[c]
                            a.wait_ge(*at(f"E.pT_p{4 * o + c}", u))
                            if o >= 1:
                                a.wait_ge(*at(f"E.o_p{o - 1}" if c == 3 else f"E.o_p{o - 1}.{c}", u))
                            mark(a, "scalar", a.activation(e_pT[:, t[0]:t[0] + len(t), :], ps[1][:, (4 * o + c) % 3, 0:P * len(t)].rearrange("p (t q) -> p t q", t=len(t)), ACT.Copy),
                                 f"E.pT{4 * o + c}", u)
                    if n < NU:
                        h, i = E_UNITS[n]
                        a.wait_ge(*at(f"E.nmx{n}", u))
                        mark(a, "scalar", a.activation(e_s[n % 2], e_s[n % 2], ACT.Exp, bias=e_mx[u][:, h, i:i + 1], accum_out=e_rs[u][:, h, i:i + 1]), f"E.exp{n}", u)
            for u in LANES:
                norm_scalar(a, "E.o", u)
                norm_scalar(a, "E", u)

        def e_pool(g):
            g.wait_ge(*at("D.x1", 1))
            for u in LANES:
                mark(g, "pool", g.memset(e_q[u].rearrange("p h q -> p (h q)"), 0.0), "E.zero", u)

        FE = 8
        f_wg = sb("f_wg", [P, P])
        f_bg = sb("f_bg", [1, P])
        f_we = sb("f_we", [P, FE, P])
        f_be = sb("f_be", [FE, P])
        f_order = sb("f_order", [P, P])

        class StageF:
            def __init__(self, u):
                c = Carve(u)
                self.l = c(TT, P)
                self.one = c(TT, P)
                self.m = c(TT)
                self.p = c(TT)
                self.f = c(TT)
                self.hot = c(TT, FE)
                self.hotT = c(TT, P)
                self.h = c(TT, FE, P)
                self.y = c(TT, P)

        SF = [StageF(u) for u in LANES]

        def f_load(sp):
            n = "L1_ffn_"
            sp.dma_start(f_wg[:, :], w[n + "Wg"]).then_inc(s_weights, 16)
            sp.dma_start(f_bg[:, :], w[n + "bg"].rearrange("(a n) -> a n", a=1)).then_inc(s_weights, 16)
            sp.dma_start(f_we[:, :, :], w[n + "We"].rearrange("e d f -> d e f")).then_inc(s_weights, 16)
            sp.dma_start(f_be[:, :], w[n + "be"]).then_inc(s_weights, 16)

        def f_setup_pool(g):
            g.iota(f_order[:, :], pattern=[[-1, P]], base=P, channel_multiplier=0, allow_small_or_imprecise_dtypes=True).then_inc(s_pool, 1)

        def f_tensor(pe):
            for u in LANES:
                pe.wait_ge(*at("E.x1", u))
                for i in range(TT):
                    m = pe.transpose(ps[u][:, 0, P * i:P * i + P], X[u][:, i, :], ident[:, :])
                m.then_inc(*done("tensor", "F.xT_p", u))
            for u in LANES:
                pe.wait_ge(*at("F.xT", u))
                for i in range(TT):
                    pe.matmul(ps[u][:, 1, P * i:P * i + P], XT[u][:, P * i:P * i + P], f_wg[:, :], start=True, stop=False)
                    m = pe.matmul(ps[u][:, 1, P * i:P * i + P], ones_row[:, :], f_bg[:, :], start=False, stop=True)
                m.then_inc(*done("tensor", "F.l_p", u))
            def experts(i):
                for u in LANES:
                    if i:
                        pe.wait_ge(*at("F.sel0", u))
                    for k in range(2):
                        m = pe.matmul(ps[u][:, 2 + k, :], XT[u][:, P * i:P * i + P], f_we[:, 4 * k:4 * k + 4, :], start=True, stop=True)
                    m.then_inc(*done("tensor", f"F.h_p{i}", u))

            experts(0)
            for u in LANES:
                z = SF[u]
                pe.wait_ge(*at("F.hot", u))
                for i in range(TT):
                    m = pe.transpose(ps[u][0:FE, 0, P * i:P * i + P], z.hot[:, i, :], ident[:, :])
                m.then_inc(*done("tensor", "F.hotT_p", u))
            for u in LANES:
                z = SF[u]
                pe.wait_ge(*at("F.hotT", u))
                for i in range(TT):
                    m = pe.matmul(ps[u][:, 1, P * i:P * i + P], z.hotT[0:FE, i, :], f_be[:, :], start=True, stop=True)
                m.then_inc(*done("tensor", "F.b_p", u))
            experts(1)

        def f_vector(v):
            copy_xT(v, "F")
            for u in LANES:
                z = SF[u]
                v.wait_ge(*at("F.l_p", u))
                l = ps[u][:, 1, 0:S].rearrange("p (i c) -> p i c", i=TT)
                step(v, "vector", v.tensor_reduce(z.m, l, AX.X, ALU.max), "F.max", u)
                step(v, "vector", v.tensor_tensor(z.l, l, over(z.m.unsqueeze(2), [P, TT, P]), ALU.subtract), "F.l", u)
                step(v, "vector", v.tensor_scalar(z.one, z.l, 0.0, None, ALU.is_equal), "F.one0", u)
                step(v, "vector", v.tensor_tensor(z.one, z.one, over(f_order[:, :].unsqueeze(1), [P, TT, P]), ALU.mult), "F.one1", u)
                step(v, "vector", v.tensor_reduce(z.f, z.one, AX.X, ALU.max), "F.first", u)
                step(v, "vector", v.tensor_tensor(z.one, z.one, over(z.f.unsqueeze(2), [P, TT, P]), ALU.is_equal), "F.one2", u)
                step(v, "vector", v.tensor_reduce(z.hot, z.one.rearrange("p i (g e) -> p i e g", e=FE), AX.X, ALU.add), "F.hot", u)
            for u in LANES:
                z = SF[u]
                v.wait_ge(*at("F.exp1", u))
                step(v, "vector", v.reciprocal(z.p, z.p), "F.p", u)
                v.wait_ge(*at("F.hotT_p", u))
                step(v, "vector", v.tensor_copy(z.hotT[0:FE, :, :].rearrange("p i q -> p (i q)"), ps[u][0:FE, 0, 0:S]), "F.hotT", u)
            for i in range(TT):
                for u in LANES:
                    z = SF[u]
                    v.wait_ge(*at(f"F.h_p{i}", u))
                    step(v, "vector", v.tensor_tensor(z.h[:, i, :, :], ps[u][:, 2:4, :].rearrange("p b (e f) -> p (b e) f", f=P),
                                                      over(z.hot[:, i, :].unsqueeze(2), [P, FE, P]), ALU.mult), f"F.sel{i}", u)
                    step(v, "vector", v.tensor_reduce(z.y[:, i, :], z.h[:, i, :, :].rearrange("p e f -> p f e"), AX.X, ALU.add), f"F.y{i}", u)
            for u in LANES:
                z = SF[u]
                v.wait_ge(*at("F.b_p", u))
                step(v, "vector", v.tensor_tensor(z.y, z.y, ps[u][:, 1, 0:S].rearrange("p (i f) -> p i f", i=TT), ALU.add), "F.yb", u)
                step(v, "vector", v.scalar_tensor_tensor(out=z.y, in0=z.y, scalar=0.0, in1=over(z.p.unsqueeze(2), [P, TT, P]), op0=ALU.max, op1=ALU.mult), "F.yp", u)
                norm_vector_1(v, "F", u, z.y)
            for u in LANES:
                norm_vector_2(v, "F", u)

        def f_scalar(a):
            for u in LANES:
                z = SF[u]
                a.wait_ge(*at("F.one2", u))
                for i in range(TT):
                    mark(a, "scalar", a.activation(z.l[:, i, :], z.l[:, i, :], ACT.Exp, accum_out=z.p[:, i:i + 1]), f"F.exp{i}", u)
            for u in LANES:
                norm_scalar(a, "F", u)

        def end_round(eng, engine):
            eng.drain().then_inc(s_round_done, 1)
            eng.wait_ge(s_open[engine], 1)
            eng.sem_clear(s_open[engine])

        block = ctx.enter_context(nc.Block())

        @block.sync
        def _(sp):
            a_load(sp)
            b_load(sp)
            c_load(sp)
            d_load(sp)
            e_load(sp)
            f_load(sp)
            sp.wait_ge(*at("setup.end"))
            with sp.Fori(0, rounds) as it:
                for u in LANES:
                    sp.dma_start(X[u][:, :, :], x_in[it * 2 + u]).then_inc(s_x[u], 16)
                b_sync(sp, it)
                e_sync(sp, it)
                for u in LANES:
                    sp.wait_ge(*at(f"F.x1", u))
                    sp.dma_start(x_out[it * 2 + u], X[u][:, :, :]).then_inc(s_out, 16)
                sp.wait_ge(s_round_done, 4)
                sp.wait_ge(s_out, 16 * len(LANES))
                sp.sem_clear(cleared)
                for engine in ENGINES:
                    sp.drain().then_inc(s_open[engine], 1)

        @block.gpsimd
        def _(g):
            g.memset(ident[:, :], 0.0).then_inc(s_id, 1)
            g.memset(ones_row[:, :], 1.0).then_inc(s_id, 1)
            g.memset(eps6[:, :], 1e-6).then_inc(s_id, 1)
            g.wait_ge(s_id, 3)
            g.affine_select(out=ident[:, :], in_=ident[:, :], compare_op=ALU.not_equal, fill=1.0, base=0,
                            pattern=[[-1, P]], channel_multiplier=1).then_inc(s_id, 1)
            a_setup_pool(g)
            b_setup_pool(g)
            c_setup_pool(g)
            d_setup_pool(g)
            f_setup_pool(g)
            with g.Fori(0, rounds):
                a_pool(g)
                b_pool(g)
                c_pool(g)
                d_pool(g)
                e_pool(g)
                end_round(g, "pool")

        @block.vector
        def _(v):
            v.wait_ge(s_id, 4)
            v.wait_ge(s_weights, 16 * 54)
            v.wait_ge(s_pool, 24)
            step(v, "vector", v.tensor_reduce(head_of[:, :], ident[:, :].rearrange("p (h d) -> p h d", d=8), AX.X, ALU.add), "setup.head_of")
            step(v, "vector", v.tensor_reduce(head_mod[:, :], head_of[:, :].rearrange("p (g r) -> p r g", r=4), AX.X, ALU.add), "setup.head_mod")
            a_setup_vector(v)
            b_setup_vector(v)
            c_setup_vector(v)
            d_setup_vector(v)
            step(v, "vector", v.memset(lnt[0][:, :], 0.0), "setup.end")
            with v.Fori(0, rounds):
                a_vector(v)
                b_vector(v)
                c_vector(v)
                d_vector(v)
                e_vector(v)
                f_vector(v)
                end_round(v, "vector")

        @block.scalar
        def _(a):
            a.preload_act_table_set("natural_log_exp_and_others")
            d_setup_scalar(a)
            a.wait_ge(*at("setup.end"))
            with a.Fori(0, rounds):
                a_scalar(a)
                b_scalar(a)
                c_scalar(a)
                d_scalar(a)
                e_scalar(a)
                f_scalar(a)
                end_round(a, "scalar")

        @block.tensor
        def _(pe):
            pe.wait_ge(s_id, 4)
            pe.wait_ge(s_weights, 16 * 54)
            b_setup_tensor(pe)
            c_setup_tensor(pe)
            pe.wait_ge(*at("setup.end"))
            with pe.Fori(0, rounds):
                a_tensor(pe)
                b_tensor(pe)
                c_tensor(pe)
                d_tensor(pe)
                e_tensor(pe)
                f_tensor(pe)
                end_round(pe, "tensor")
        return marks


_NAMES = ['x',
          'ctx_1024',
          'mask_BxS2_bf1',
          'L0_attn_wq',
          'L0_attn_wk',
          'L0_attn_wv',
          'L0_attn_wgq',
          'L0_attn_wgk',
          'L0_attn_wgv',
          'L0_attn_r_out_w',
          'L0_attn_gate_local_w',
          'L0_attn_gate_remote_w',
          'L0_attn_w_out',
          'L0_xattn_Wq',
          'L0_xattn_Wk',
          'L0_xattn_Wv',
          'L0_xattn_gru_wih',
          'L0_xattn_gru_whh',
          'L0_xattn_gru_bih',
          'L0_xattn_gru_bhh',
          'L0_xattn_slot_norm_w',
          'L0_xattn_input_norm_w',
          'L0_ffn_Wq',
          'L0_ffn_Wk',
          'L0_ffn_Wv',
          'L0_ffn_Ws',
          'L0_ffn_Wd',
          'L0_ffn_Wo',
          'L1_attn_W_in',
          'L1_attn_b_in',
          'L1_attn_A_log',
          'L1_attn_W_B',
          'L1_attn_b_B',
          'L1_attn_W_C',
          'L1_attn_b_C',
          'L1_attn_W_delta',
          'L1_attn_b_delta',
          'L1_attn_D_param',
          'L1_attn_W_out',
          'L1_attn_b_out',
          'L1_xattn_g_x',
          'L1_xattn_b_x',
          'L1_xattn_g_l',
          'L1_xattn_b_l',
          'L1_xattn_w_q',
          'L1_xattn_w_kv',
          'L1_xattn_w_out',
          'L1_xattn_g_o',
          'L1_xattn_b_o',
          'L1_ffn_Wg',
          'L1_ffn_bg',
          'L1_ffn_We',
          'L1_ffn_be']


def kernel(**inputs):
    import numpy as _np
    import concourse.bacc as _bacc
    from concourse import mybir as _mybir
    from concourse.bass_utils import run_bass_kernel_spmd as _run

    known = None
    for _ in range(2):
        nc = _bacc.Bacc("TRN2", target_bir_lowering=False, num_devices=1)
        arrays, aps = {}, {}
        for name in _NAMES:
            a = _np.ascontiguousarray(inputs[name])
            if a.dtype == _np.bool_:
                a = a.view(_np.uint8)
            arrays[f"in_{name}"] = a
            aps[name] = nc.dram_tensor(f"in_{name}", a.shape, _mybir.dt.from_np(a.dtype), kind="ExternalInput").ap()
        out = nc.dram_tensor("out_0", (B, S, D), F32, kind="ExternalOutput").ap()
        known = build(nc, aps, out, known, B // len(LANES))
    r = _run(nc, [arrays], core_ids=[0])
    return r.results[0]["out_0"]
```

```python
import concourse.bass as bass
from concourse import mybir
from contextlib import ExitStack

F32 = mybir.dt.float32
BF16 = mybir.dt.bfloat16
U8 = mybir.dt.uint8
ACT = mybir.ActivationFunctionType
ALU = mybir.AluOpType
AX = mybir.AxisListType

B, S, D = 16, 256, 128
SC = 1601
P = 128
LANES = (0, 1)
TT = S // P
NEG = -1e30
BANK = 512


class Marks:

    def __init__(self, make, known):
        self.known = known
        self.count, self.place = {}, {}
        keys = sorted(known.count) if known else []
        self.make = make
        self.sems = {key: make("_".join(map(str, key))) for key in keys if key[0] != "setup"}
        self.round_sems = list(self.sems.values())
        self.sems.update({key: make("_".join(map(str, key))) for key in keys if key[0] == "setup"})
        self.dry = None if known else make("dry")

    def done(self, engine, name, lane=0):
        key = (name.split(".")[0], engine, lane)
        self.count[key] = self.count.get(key, 0) + 1
        assert (name, lane) not in self.place, name
        self.place[name, lane] = (key, self.count[key])
        return self.sems.get(key, self.dry), 1

    def at(self, name, lane=0):
        if self.known is None:
            return self.dry, 1
        key, value = self.known.place[name, lane]
        return self.sems[key], value


def build(nc, w, out, known, rounds):
    ctx = ExitStack()
    with ctx:
        def sb(name, shape, dt=F32):
            return ctx.enter_context(nc.sbuf_tensor(name, shape, dt))

        def sem(name):
            return ctx.enter_context(nc.semaphore(name))

        s_x = [sem(f"x_loaded{u}") for u in LANES]
        s_ctx = [sem(f"context_loaded{u}") for u in LANES]
        s_mask = [sem(f"mask_loaded{u}") for u in LANES]
        s_out = sem("x_stored")
        s_round_done = sem("round_done")
        marks = Marks(sem, known)
        round_sems = [*s_x, *s_ctx, *s_mask, s_out, s_round_done, *marks.round_sems]
        cleared = range(round_sems[0].num, round_sems[-1].num + 1)
        assert [s.num for s in round_sems] == list(cleared)
        at, done = marks.at, marks.done

        ps = [ctx.enter_context(nc.psum_tensor(f"ps{u}", [P, 4, BANK], F32)) for u in LANES]

        ident = sb("ident", [P, P])
        ones_row = sb("ones_row", [1, P])
        eps6 = sb("eps6", [P, 1])
        one_col = sb("one_col", [P, 1])
        head_of = sb("head_of", [P, 16])
        head_mod = sb("head_mod", [P, 4])
        quarter_of = sb("quarter_of", [P, 4])
        X = [sb(f"X{u}", [P, TT, P]) for u in LANES]
        XT = [sb(f"XT{u}", [P, S]) for u in LANES]
        lnt = [sb(f"lnt{u}", [P, 32]) for u in LANES]
        res = [sb(f"res{u}", [P, TT, P]) for u in LANES]
        AREA = 15760
        B_KEPT = AREA - 13 * P - 13 * (P + 1) - 260
        area = [sb(f"area{u}", [P, AREA]) for u in LANES]

        class Carve:

            def __init__(self, u, start=0):
                self.u, self.at = u, start

            def __call__(self, *shape):
                n = 1
                for s in shape:
                    n *= s
                a = area[self.u][:, self.at:self.at + n]
                self.at += n
                assert self.at <= AREA, self.at
                if len(shape) == 1:
                    return a
                names = " ".join("abcde"[:len(shape)])
                return a.rearrange(f"p ({names}) -> p {names}", **dict(zip("abcde", shape)))

        def over(ap, shape):
            return ap.to_broadcast(shape)

        s_weights = sem("weights_loaded")
        s_pool = sem("positions_made")
        s_id = sem("identity_made")
        ENGINES = ("tensor", "vector", "scalar", "pool")
        s_open = {engine: sem(f"round_open_{engine}") for engine in ENGINES}
        x_in = w["x"].rearrange("b (t p) d -> b p t d", p=P)
        x_out = out.rearrange("b (t p) d -> b p t d", p=P)

        def step(eng, engine, instruction, name, u=0):
            instruction.then_inc(*done(engine, name, u))
            eng.wait_ge(*at(name, u))

        def mark(eng, engine, instruction, name, u=0):
            instruction.then_inc(*done(engine, name, u))

        def rsqrt_newton(v, tag, u, y, x, t):
            step(v, "vector", v.tensor_tensor(t, y, y, ALU.mult), f"{tag}.nt0", u)
            step(v, "vector", v.tensor_tensor(t, t, x, ALU.mult), f"{tag}.nt1", u)
            step(v, "vector", v.tensor_scalar(t, t, -0.5, 1.5, ALU.mult, ALU.add), f"{tag}.nt2", u)
            step(v, "vector", v.tensor_tensor(y, y, t, ALU.mult), f"{tag}.rstd", u)

        def moments(v, tag, u, src, eps):
            st = lnt[u]
            for i in range(TT):
                step(v, "vector", v.bn_stats(st[:, 16 + 6 * i:22 + 6 * i], src[:, i, :]), f"{tag}.st{i}", u)
            v.memset(st[:, 12:14], 0.0).then_inc(*done("vector", f"{tag}.clear", u))
            for i in range(TT):
                mark(v, "vector", v.bn_aggr(st[:, 2 * i:2 * i + 2], st[:, 16 + 6 * i:22 + 6 * i]), f"{tag}.mv{i}", u)
            v.wait_ge(*at(f"{tag}.mv{TT - 1}", u))
            step(v, "vector", v.tensor_scalar(st[:, 4:6], st[:, 0:4].rearrange("p (i c) -> p c i", c=2)[:, 1, :], eps, None, ALU.add), f"{tag}.var", u)

        def norm_vector_1(v, tag, u, y):
            step(v, "vector", v.tensor_tensor(res[u][:, :, :], y, X[u][:, :, :], ALU.add), f"{tag}.res", u)
            moments(v, tag, u, res[u], 1e-5)

        def norm_scalar(a, tag, u):
            st = lnt[u]
            a.wait_ge(*at(f"{tag}.var", u))
            step(a, "scalar", a.activation(st[:, 6:8], st[:, 4:6], ACT.Ln), f"{tag}.ln", u)
            step(a, "scalar", a.activation(st[:, 8:10], st[:, 6:8], ACT.Exp, scale=-0.5), f"{tag}.power", u)

        def norm_vector_2(v, tag, u, src=None, dst=None):
            st = lnt[u]
            src = res[u] if src is None else src
            dst = X[u] if dst is None else dst
            v.wait_ge(*at(f"{tag}.power", u))
            rsqrt_newton(v, tag, u, st[:, 8:10], st[:, 4:6], st[:, 10:12])
            for i in range(TT):
                step(v, "vector", v.tensor_scalar(dst[:, i, :], src[:, i, :], st[:, 2 * i:2 * i + 1], st[:, 8 + i:9 + i], ALU.subtract, ALU.mult),
                     f"{tag}.x{i}", u)

        AH, AHD, AW = 16, 8, 32
        LH, LN = 8, 64
        POOL = S // LN
        QT = [(0, 96, 0, 96), (96, 96, 64, 128), (160, 96, 128, 128)]
        A_SCALE = float(AHD) ** -0.5
        a_w = sb("a_w", [P, 3, P])
        a_wg = sb("a_wg", [P, 3, 64])
        a_wo = sb("a_wo", [P, P])
        a_ro = sb("a_ro", [64, P])
        a_gate = sb("a_gate", [P, 2])
        a_gates = sb("a_gates", [P, 32])
        a_mask = [sb(f"a_mask{t}", [P, P]) for t in range(3)]
        a_lmask = sb("a_lmask", [P, TT, LN])

        class StageA:
            def __init__(self, u):
                c = Carve(u)
                self.qT = c(S)
                self.qg = c(4, S)
                self.kT = c(4, S)
                self.gqT = c(S)
                self.gkT = c(4, LN)
                self.xp = c(2, LN)
                self.gv = c(4, 2, 9)
                self.v = c(3, AH, 9)
                self.s = [c(AH, P) for _ in range(2)]
                latent = Carve(u, c.at - AH * P)
                self.pT = c(AH, P)
                self.ls = latent(TT, LH, LN)
                self.lpT = latent(TT * 4, P)
                self.mx = [c(16) for _ in range(2)]
                self.rs = c(32)
                self.rem = c(TT, 64)
                self.remT = c(S)
                self.g = c(32)
                self.loc = c(AH, AHD)
                self.o = c(AH, AHD)
                self.oT = c(S)
                assert c.at <= B_KEPT

        SA = [StageA(u) for u in LANES]

        def a_load(sp):
            for i, n in enumerate(("wq", "wk", "wv")):
                sp.dma_start(a_w[:, i, :], w[f"L0_attn_{n}"]).then_inc(s_weights, 16)
            for i, n in enumerate(("wgq", "wgk", "wgv")):
                sp.dma_start(a_wg[:, i, :], w[f"L0_attn_{n}"]).then_inc(s_weights, 16)
            sp.dma_start(a_wo[:, :], w["L0_attn_w_out"]).then_inc(s_weights, 16)
            sp.dma_start(a_ro[:, :], w["L0_attn_r_out_w"]).then_inc(s_weights, 16)
            sp.dma_start(a_gate[:, 0:1], w["L0_attn_gate_local_w"].rearrange("h (d a) -> (h d) a", a=1)).then_inc(s_weights, 16)
            sp.dma_start(a_gate[:, 1:2], w["L0_attn_gate_remote_w"].rearrange("h (d a) -> (h d) a", a=1)).then_inc(s_weights, 16)
            return 10

        def a_setup_pool(g):
            for t, (qs, qn, ks, kn) in enumerate(QT):
                g.memset(a_mask[t][:, :], 0.0).then_inc(s_pool, 1)
            g.memset(a_lmask[:, :, :], 0.0).then_inc(s_pool, 1)
            g.wait_ge(s_pool, 4)
            for t, (qs, qn, ks, kn) in enumerate(QT):
                m = a_mask[t][:, :]
                g.affine_select(out=m, in_=m, compare_op=ALU.is_ge, fill=NEG, base=qs - ks,
                                pattern=[[-1, P]], channel_multiplier=1).then_inc(s_pool, 1)
            g.affine_select(out=a_lmask[:, :, :], in_=a_lmask[:, :, :], compare_op=ALU.is_ge, fill=NEG, base=0,
                            pattern=[[P, TT], [-POOL, LN]], channel_multiplier=1).then_inc(s_pool, 1)
            g.wait_ge(s_pool, 8)
            for t, (qs, qn, ks, kn) in enumerate(QT):
                m = a_mask[t][:, :]
                g.affine_select(out=m, in_=m, compare_op=ALU.is_ge, fill=NEG, base=AW - 1 + ks - qs,
                                pattern=[[1, P]], channel_multiplier=-1).then_inc(s_pool, 1)

        def a_setup_vector(v):
            for i in range(2):
                step(v, "vector", v.tensor_scalar(a_gates[:, 16 * i:16 * i + 16], head_of[:, :], a_gate[:, i:i + 1], None, ALU.mult), "setup.gates%d" % i)

        def a_scores(pe, u, t):
            z = SA[u]
            qs, qn, ks, kn = QT[t]
            pe.wait_ge(*at("A.qg", u))
            pe.wait_ge(*at(f"A.oT{t - 2}" if t >= 2 else "A.remT", u))
            if t >= 1:
                pe.wait_ge(*at(f"A.sm{t - 1}", u))
            for g in range(4):
                m = pe.matmul(ps[u][0:qn, g, :].rearrange("p (r k) -> p r k", r=4)[:, :, 0:kn], z.qg[:, g, qs:qs + qn],
                              z.kT[:, :, ks:ks + kn], start=True, stop=True)
            m.then_inc(*done("tensor", f"A.s_p{t}", u))

        def a_tensor(pe):
            for u in LANES:
                pe.wait_ge(s_x[u], 16)
                for t in range(TT):
                    m = pe.transpose(ps[u][:, 0, P * t:P * t + P], X[u][:, t, :], ident[:, :])
                m.then_inc(*done("tensor", "A.xT_p", u))
            for u in LANES:
                z = SA[u]
                pe.wait_ge(*at("A.xp", u))
                for i in range(2):
                    pe.matmul(ps[u][:, 1, S * i:S * i + S], a_w[:, i, :], XT[u][:, :], start=True, stop=True)
                pe.matmul(ps[u][0:64, 2, 0:S], a_wg[:, 0, :], XT[u][:, :], start=True, stop=True)
                pe.matmul(ps[u][0:64, 2, 256:256 + LN], a_wg[:, 1, :], z.xp[:, 0, :], start=True, stop=True)
                pe.matmul(ps[u][:, 2, 320:384], z.xp, a_wg[:, 2, :], start=True, stop=True)
                for t, (qs, qn, ks, kn) in enumerate(QT):
                    m = pe.matmul(ps[u][0:kn, 3, P * t:P * t + P], XT[u][:, ks:ks + kn], a_w[:, 2, :], start=True, stop=True)
                m.then_inc(*done("tensor", "A.proj_p", u))
            for u in LANES:
                z = SA[u]
                pe.wait_ge(*at("A.proj", u))
                pe.wait_ge(*at("A.proj_a", u))
                for i in range(TT):
                    for g in range(2):
                        for r in range(4):
                            m = pe.matmul(ps[u][:, g, 256 * i + 64 * r:256 * i + 64 * r + 64],
                                          z.gqT[32 * g:32 * g + 32, P * i:P * i + P],
                                          z.gkT[32 * g:32 * g + 32, r, :], start=True, stop=True)
                m.then_inc(*done("tensor", "A.ls_p", u))
            for u in LANES:
                z = SA[u]
                pe.wait_ge(*at("A.lprob", u))
                for i in range(TT):
                    for c in range(4):
                        m = pe.transpose(ps[u][:, 2 + i, P * c:P * c + P], z.ls[:, i, 2 * c:2 * c + 2, :], ident[:, :])
                m.then_inc(*done("tensor", "A.lpT_p", u))
            for u in LANES:
                z = SA[u]
                pe.wait_ge(*at("A.lpT", u))
                for i in range(TT):
                    for c in range(4):
                        m = pe.matmul(ps[u][:, 0, P * i + 18 * c:P * i + 18 * c + 18], z.lpT[:, 4 * i + c, :],
                                      z.gv[:, c, :, :], start=True, stop=True)
                m.then_inc(*done("tensor", "A.rem_p", u))
            for u in LANES:
                z = SA[u]
                pe.wait_ge(*at("A.rem", u))
                m = pe.transpose(ps[u][:, 1, 0:P], z.rem, ident[:, :])
                m.then_inc(*done("tensor", "A.remT_p", u))
            for t in range(len(QT) + 1):
                if t < len(QT):
                    for u in LANES:
                        a_scores(pe, u, t)
                if t == 0:
                    continue
                o = t - 1
                qs, qn, ks, kn = QT[o]
                for u in LANES:
                    z = SA[u]
                    pe.wait_ge(*at(f"A.sm{t}" if t < len(QT) else f"A.oT{o - 1}", u))
                    pe.wait_ge(*at(f"A.prob{o}", u))
                    for h in range(AH):
                        m = pe.transpose(ps[u][0:kn, h // 4, P * (h % 4):P * (h % 4) + qn], z.s[o % 2][0:qn, h, 0:kn], ident[0:qn, 0:qn])
                    m.then_inc(*done("tensor", f"A.pT_p{o}", u))
                for u in LANES:
                    z = SA[u]
                    pe.wait_ge(*at(f"A.pT{o}", u))
                    for h in range(AH):
                        pe.matmul(ps[u][0:qn, 0, 9 * h:9 * h + 9], z.pT[0:kn, h, 0:qn], z.v[0:kn, o, h, :], start=True, stop=True)
                    pe.matmul(ps[u][0:qn, 0, 160:192], z.qT[:, qs:qs + qn], a_gates[:, :], start=True, stop=True)
                    pe.matmul(ps[u][0:qn, 0, 256:384], z.remT[0:64, qs:qs + qn], a_ro[:, :], start=True, stop=True)\
                        .then_inc(*done("tensor", f"A.o_p{o}", u))
                for u in LANES:
                    z = SA[u]
                    pe.wait_ge(*at(f"A.o{o}", u))
                    pe.transpose(ps[u][:, 1, 0:qn], z.o[0:qn, :, :], ident[0:qn, 0:qn])\
                        .then_inc(*done("tensor", f"A.oT_p{o}", u))
            for u in LANES:
                pe.wait_ge(*at(f"A.oT{len(QT) - 1}", u))
            for u in LANES:
                z = SA[u]
                for i in range(TT):
                    m = pe.matmul(ps[u][:, 0, P * i:P * i + P], z.oT[:, P * i:P * i + P], a_wo[:, :], start=True, stop=True)
                m.then_inc(*done("tensor", "A.y_p", u))

        def a_maxima(v, u, t):
            z = SA[u]
            qs, qn, ks, kn = QT[t]
            v.wait_ge(*at(f"A.s_p{t}", u))
            if t >= 2:
                v.wait_ge(*at(f"A.pT_p{t - 2}", u))
            sc = ps[u][0:qn, :, :].rearrange("p g (r k) -> p (g r) k", k=P)[:, :, 0:kn]
            step(v, "vector", v.tensor_tensor(z.s[t % 2][0:qn, :, 0:kn], sc, over(a_mask[t][0:qn, 0:kn].unsqueeze(1), [qn, AH, kn]), ALU.add), f"A.sm{t}", u)
            mark(v, "vector", v.tensor_reduce(z.mx[t % 2][0:qn, :], z.s[t % 2][0:qn, :, 0:kn], AX.X, ALU.max), f"A.mx{t}", u)

        def a_heads(v, u, o):
            z = SA[u]
            qs, qn, ks, kn = QT[o]
            v.wait_ge(*at(f"A.o_p{o}", u))
            v.wait_ge(*at(f"A.gsig{o}", u))
            q = ps[u][0:qn, 0, 0:144].rearrange("p (h d) -> p h d", d=9)
            mark(v, "vector", v.tensor_tensor(z.o[0:qn, :, :], ps[u][0:qn, 0, 256:384].rearrange("p (h d) -> p h d", d=8),
                                              over(z.g[0:qn, 16:32].unsqueeze(2), [qn, AH, 8]), ALU.mult), f"A.orem{o}", u)
            step(v, "vector", v.reciprocal(z.rs[0:qn, 0:16].unsqueeze(2), q[:, :, 8:9]), f"A.rs{o}", u)
            step(v, "vector", v.tensor_tensor(z.rs[0:qn, 0:16], z.rs[0:qn, 0:16], z.g[0:qn, 0:16], ALU.mult), f"A.grs{o}", u)
            step(v, "vector", v.tensor_tensor(z.loc[0:qn, :, :], q[:, :, 0:8], over(z.rs[0:qn, 0:16].unsqueeze(2), [qn, AH, 8]), ALU.mult), f"A.loc{o}", u)
            mark(v, "vector", v.tensor_tensor(z.o[0:qn, :, :], z.o[0:qn, :, :], z.loc[0:qn, :, :], ALU.add), f"A.o{o}", u)

        def a_vector(v):
            for u in LANES:
                z = SA[u]
                v.wait_ge(*at("A.xT_p", u))
                step(v, "vector", v.tensor_copy(XT[u][:, :], ps[u][:, 0, 0:S]), "A.xT", u)
                step(v, "vector", v.tensor_reduce(z.xp[:, 0, :], XT[u][:, :].rearrange("p (n c) -> p n c", c=POOL), AX.X, ALU.add), "A.xp0", u)
                step(v, "vector", v.tensor_scalar(z.xp[:, 0, :], z.xp[:, 0, :], 1.0 / POOL, None, ALU.mult), "A.xp1", u)
                step(v, "vector", v.tensor_copy(z.xp[:, 1, :], z.xp[:, 0, :]), "A.xp", u)
            for u in LANES:
                z = SA[u]
                v.wait_ge(*at("A.proj_p", u))
                step(v, "vector", v.tensor_tensor(z.kT, over(ps[u][:, 1, S:2 * S].unsqueeze(1), [P, 4, S]),
                                                  over(head_mod[:, :].unsqueeze(2), [P, 4, S]), ALU.mult), "A.kT", u)
                mark(v, "vector", v.tensor_tensor(z.qg, over(ps[u][:, 1, 0:S].unsqueeze(1), [P, 4, S]),
                                                  over(quarter_of[:, :].unsqueeze(2), [P, 4, S]), ALU.mult), "A.qg", u)
                step(v, "vector", v.tensor_tensor(z.gkT[0:64, :, :], over(ps[u][0:64, 2, 256:256 + LN].unsqueeze(1), [64, 4, LN]),
                                                  over(head_mod[0:64, :].unsqueeze(2), [64, 4, LN]), ALU.mult), "A.gkT", u)
                for k in range(2):
                    src = ps[u][64 * k:64 * k + 64, 2, 320:384].rearrange("p (c e d) -> p c e d", c=4, e=2)
                    step(v, "vector", v.tensor_copy(z.gv[64 * k:64 * k + 64, :, k, 0:8], src[:, :, k, :]), f"A.gv{k}", u)
                    step(v, "vector", v.memset(z.gv[64 * k:64 * k + 64, :, k, 8:9], 1.0), f"A.gvone{k}", u)
                    step(v, "vector", v.memset(z.gv[64 * k:64 * k + 64, :, 1 - k, :], 0.0), f"A.gvnil{k}", u)
                step(v, "vector", v.memset(z.v[:, :, :, 8:9], 1.0), "A.vone", u)
                for t, (qs, qn, ks, kn) in enumerate(QT):
                    step(v, "vector", v.tensor_copy(z.v[0:kn, t, :, 0:8], ps[u][0:kn, 3, P * t:P * t + P].rearrange("p (h d) -> p h d", d=AHD)),
                         f"A.v{t}" if t < 2 else "A.proj", u)
            for u in LANES:
                z = SA[u]
                v.wait_ge(*at("A.ls_p", u))
                for i in range(TT):
                    step(v, "vector", v.tensor_tensor(
                        z.ls[:, i, :, :].rearrange("p (g r) n -> p g r n", g=2),
                        ps[u][:, 0:2, 256 * i:256 * i + 256].rearrange("p g (r n) -> p g r n", r=4),
                        over(a_lmask[:, i:i + 1, :].unsqueeze(1), [P, 2, 4, LN]), ALU.add), f"A.lsm{i}", u)
                step(v, "vector", v.tensor_reduce(z.mx[0], z.ls, AX.X, ALU.max), "A.lmx", u)
                step(v, "vector", v.tensor_tensor(z.ls, z.ls, over(z.mx[0].rearrange("p (i h) -> p i h", i=TT).unsqueeze(3), [P, TT, LH, LN]), ALU.subtract), "A.lsub", u)
            for u in LANES:
                z = SA[u]
                v.wait_ge(*at("A.rem_p", u))
                o = ps[u][:, 0, 0:2 * P].rearrange("p (i c) -> p i c", i=TT)[:, :, 0:72].rearrange("p i (h d) -> p i h d", d=9)
                rs = z.rs[:, 0:16].rearrange("p (i h) -> p i h", i=TT)
                step(v, "vector", v.reciprocal(rs.unsqueeze(3), o[:, :, :, 8:9]), "A.rrs", u)
                step(v, "vector", v.tensor_tensor(z.rem.rearrange("p i (h d) -> p i h d", d=8), o[:, :, :, 0:8],
                                                  over(rs.unsqueeze(3), [P, TT, LH, 8]), ALU.mult), "A.rem", u)
            for u in LANES:
                z = SA[u]
                v.wait_ge(*at("A.remT_p", u))
                step(v, "vector", v.tensor_copy(z.remT[0:64, 0:P], ps[u][0:64, 1, 0:P]), "A.remT0", u)
                step(v, "vector", v.tensor_copy(z.remT[0:64, P:S], ps[u][64:P, 1, 0:P]), "A.remT", u)
            for t in range(len(QT) + 1):
                if t < len(QT):
                    for u in LANES:
                        a_maxima(v, u, t)
                if t == 0:
                    continue
                if t == 1:
                    b_statistics(v, 0)
                if t == 2:
                    b_statistics(v, 1)
                o = t - 1
                for u in LANES:
                    a_heads(v, u, o)
                qs, qn, ks, kn = QT[o]
                for u in LANES:
                    z = SA[u]
                    v.wait_ge(*at(f"A.oT_p{o}", u))
                    mark(v, "vector", v.tensor_copy(z.oT[:, qs:qs + qn], ps[u][:, 1, 0:qn]), f"A.oT{o}", u)
            for u in LANES:
                b_normed(v, u)
            for u in LANES:
                v.wait_ge(*at("A.y_p", u))
                norm_vector_1(v, "A", u, ps[u][:, 0, 0:S].rearrange("p (i d) -> p i d", i=TT))
            for u in LANES:
                norm_vector_2(v, "A", u)

        def a_transposed(a, u, o):
            z = SA[u]
            qs, qn, ks, kn = QT[o]
            a.wait_ge(*at(f"A.pT_p{o}", u))
            src = ps[u][0:kn, :, :].rearrange("p g (r k) -> p (g r) k", k=P)[:, :, 0:qn]
            mark(a, "scalar", a.activation(z.pT[0:kn, :, 0:qn], src, ACT.Copy), f"A.pT{o}", u)

        def a_scalar(a):
            for u in LANES:
                z = SA[u]
                a.wait_ge(*at("A.proj_p", u))
                a.wait_ge(*at("A.qg", u))
                step(a, "scalar", a.activation(z.qT, ps[u][:, 1, 0:S], ACT.Copy), "A.qT", u)
                a.wait_ge(*at("A.proj", u))
                step(a, "scalar", a.activation(z.gqT[0:64, :], ps[u][0:64, 2, 0:S], ACT.Copy), "A.proj_a", u)
            for u in LANES:
                z = SA[u]
                a.wait_ge(*at("A.lsub", u))
                step(a, "scalar", a.activation(z.ls, z.ls, ACT.Exp, scale=A_SCALE), "A.lprob", u)
            for u in LANES:
                z = SA[u]
                a.wait_ge(*at("A.lpT_p", u))
                step(a, "scalar", a.activation(z.lpT, ps[u][:, 2:4, :].rearrange("p b (c q) -> p (b c) q", c=4), ACT.Copy), "A.lpT", u)
            for t in range(len(QT) + 1):
                for u in LANES if t < len(QT) else ():
                    z = SA[u]
                    qs, qn, ks, kn = QT[t]
                    a.wait_ge(*at(f"A.ssub{t}", u))
                    mark(a, "scalar", a.activation(z.s[t % 2][0:qn, :, 0:kn], z.s[t % 2][0:qn, :, 0:kn], ACT.Exp, scale=A_SCALE), f"A.prob{t}", u)
                    if t >= 1:
                        a_transposed(a, u, t - 1)
                if 1 <= t < len(QT):
                    b_powers(a, t - 1)
                for u in LANES if t == len(QT) else ():
                    a_transposed(a, u, t - 1)
                for u in LANES if t >= 1 else ():
                    z = SA[u]
                    qn = QT[t - 1][1]
                    a.wait_ge(*at(f"A.o_p{t - 1}", u))
                    step(a, "scalar", a.activation(z.g[0:qn, :], ps[u][0:qn, 0, 160:192], ACT.Exp, scale=-1.0), f"A.gexp{t - 1}", u)
                    step(a, "scalar", a.activation(z.g[0:qn, :], z.g[0:qn, :], ACT.Ln, bias=one_col[0:qn, 0:1]), f"A.gln{t - 1}", u)
                    mark(a, "scalar", a.activation(z.g[0:qn, :], z.g[0:qn, :], ACT.Exp, scale=-1.0), f"A.gsig{t - 1}", u)
            for u in LANES:
                norm_scalar(a, "A", u)

        def a_pool(g):
            for t, (qs, qn, ks, kn) in enumerate(QT):
                for u in LANES:
                    z = SA[u]
                    g.wait_ge(*at(f"A.mx{t}", u))
                    mark(g, "pool", g.tensor_tensor(z.s[t % 2][0:qn, :, 0:kn], z.s[t % 2][0:qn, :, 0:kn],
                                                    over(z.mx[t % 2][0:qn, :].unsqueeze(2), [qn, AH, kn]), ALU.subtract), f"A.ssub{t}", u)

        MT = (SC + P - 1) // P
        ML = SC - (MT - 1) * P
        MP = (MT + 1) // 2
        ITERS = 3
        b_w = [XT[0][:, 0:P], XT[0][:, P:S], XT[1][:, 0:P]]
        b_gw = [[X[0][:, 0, :], X[0][:, 1, :], X[1][:, 0, :]],
                [X[1][:, 1, :], res[0][:, 0, :], res[0][:, 1, :]]]
        b_hhT = sb("b_hhT", [P, 3 * P])
        c_wqT = sb("c_wqT", [P, 1024])
        b_ihT = c_wqT[:, 0:3 * P]
        b_A = sb("b_A", [P, P])
        b_C = sb("b_C", [P, 3 * P])
        b_bias = sb("b_bias", [P, 2, 3])
        b_nw = sb("b_nw", [P, 2])
        b_small = sb("b_small", [P, 8])
        b_mean = sb("b_mean", [P, P])
        e_ln = sb("e_ln", [P, 4])
        KV = SC + S
        kvT = [sb(f"kvT{u}", [P, KV]) for u in LANES]

        class StageB:
            def __init__(self, u):
                c = Carve(u, AREA - MT * P)
                self.ctx = c(MT, P)
                c = Carve(u, B_KEPT)
                self.p = c(MT, P + 1)
                self.st = c(MT, 6)
                self.vv = c(2, MT)
                self.rr = c(2, MT)
                self.t1 = c(2, MT)
                self.mean = c(MT)
                self.df = c(MT)
                assert c.at <= AREA - MT * P
                c = Carve(u)
                self.pT = c(SC)
                self.att = c(MT, S)
                self.xn = c(MT, P)
                self.pw = c(MT, P + 1)
                self.sl = c(S)
                self.sq = c(S)
                self.qk = c(S)
                self.mx = c(2 * MP)
                self.rs = c(2 * MP)
                self.rd = c(2)
                self.un = c(2, P)
                self.uT = c(S)
                self.rz = c(2 * S)
                self.n = c(S)
                self.t = c(S)
                assert c.at <= B_KEPT

        SB = [StageB(u) for u in LANES]

        def col(name, a=1):
            return w[name].rearrange("(g p) -> p g", p=P)

        def b_load(sp):
            for i, n in enumerate(("Wq", "Wk", "Wv")):
                sp.dma_start(b_w[i], w[f"L0_xattn_{n}"]).then_inc(s_weights, 16)
            for i, n in enumerate(("gru_wih", "gru_whh")):
                for g in range(3):
                    sp.dma_start(b_gw[i][g], w[f"L0_xattn_{n}"][P * g:P * g + P, :]).then_inc(s_weights, 16)
            for i, n in enumerate(("gru_bih", "gru_bhh")):
                sp.dma_start(b_bias[:, i, :], col(f"L0_xattn_{n}"), allow_slow_non_contiguous=True).then_inc(s_weights, 16)
            for i, n in enumerate(("slot_norm_w", "input_norm_w")):
                sp.dma_start(b_nw[:, i:i + 1], col(f"L0_xattn_{n}"), allow_slow_non_contiguous=True).then_inc(s_weights, 16)
            for i, n in enumerate(("g_x", "b_x", "g_l", "b_l")):
                sp.dma_start(e_ln[:, i:i + 1], col(f"L1_xattn_{n}"), allow_slow_non_contiguous=True).then_inc(s_weights, 16)

        def b_setup_pool(g):
            for u in LANES:
                g.memset(area[u][:, :], 0.0).then_inc(s_pool, 1)
            g.memset(b_mean[:, :], 1.0 / P).then_inc(s_pool, 1)

        def b_setup_tensor(pe):
            pe.matmul(ps[0][:, 0, 0:P], b_w[0], b_w[1], start=True, stop=True)
            for i in range(3):
                pe.transpose(ps[0][:, 1, P * i:P * i + P], b_gw[0][i], ident[:, :])
            for i in range(3):
                m = pe.transpose(ps[0][:, 2, P * i:P * i + P], b_gw[1][i], ident[:, :])
            m.then_inc(*done("tensor", "setup.b1_p"))
            pe.wait_ge(*at("setup.b_ihT"))
            pe.matmul(ps[0][:, 3, 0:3 * P], b_w[2], b_ihT, start=True, stop=True).then_inc(*done("tensor", "setup.b2_p"))

        def b_setup_vector(v):
            v.wait_ge(*at("setup.b1_p"))
            step(v, "vector", v.tensor_scalar(b_A[:, :], ps[0][:, 0, 0:P], b_nw[:, 0:1], None, ALU.mult), "setup.b_A")
            step(v, "vector", v.tensor_copy(b_hhT[:, :], ps[0][:, 2, 0:3 * P]), "setup.b_hhT")
            step(v, "vector", v.tensor_copy(b_ihT, ps[0][:, 1, 0:3 * P]), "setup.b_ihT")
            v.wait_ge(*at("setup.b2_p"))
            step(v, "vector", v.tensor_scalar(b_C[:, :], ps[0][:, 3, 0:3 * P], b_nw[:, 1:2], None, ALU.mult), "setup.b_C")
            step(v, "vector", v.tensor_tensor(b_small[:, 0:2], b_bias[:, 0, 0:2], b_bias[:, 1, 0:2], ALU.add), "setup.b_s0")
            step(v, "vector", v.tensor_scalar(b_small[:, 0:2], b_small[:, 0:2], -1.0, None, ALU.mult), "setup.b_s1")
            step(v, "vector", v.tensor_scalar(b_small[:, 2:3], b_bias[:, 0, 2:3], 2.0, None, ALU.mult), "setup.b_s2")
            step(v, "vector", v.tensor_scalar(b_small[:, 3:4], b_nw[:, 1:2], float(D) ** -0.5, None, ALU.mult), "setup.b_s3")

        def b_sync(sp, it):
            for u in LANES:
                src = w["ctx_1024"][it * 2 + u]
                sp.dma_start(SB[u].ctx[:, 0:MT - 1, :], src[0:P * (MT - 1), :].rearrange("(t p) d -> p t d", p=P)).then_inc(s_ctx[u], 16)
                sp.dma_start(SB[u].ctx[0:ML, MT - 1, :], src[P * (MT - 1):SC, :]).then_inc(s_ctx[u], 16)

        def rows(m):
            return ML if m == MT - 1 else P

        def b_tensor(pe):
            for u in LANES:
                pe.wait_ge(*at("B.p", u))
                pe.wait_ge(*at("A.res", u))
                for m in range(MT):
                    o = pe.transpose(ps[u][:, m // 4, P * (m % 4):P * (m % 4) + rows(m)], SB[u].p[0:rows(m), m, 0:P], ident[0:rows(m), 0:rows(m)])
                o.then_inc(*done("tensor", "B.pT_p", u))
            for u in LANES:
                pe.wait_ge(*at("B.pT", u))
                pe.wait_ge(*at("A.x1", u))
                for i in range(TT):
                    o = pe.transpose(ps[u][:, 0, P * i:P * i + P], X[u][:, i, :], ident[:, :])
                o.then_inc(*done("tensor", "B.slT_p", u))
            for r in range(ITERS):
                k = f"B.{r}"
                for u in LANES:
                    pe.wait_ge(*at("B.sl" if r == 0 else f"B.{r - 1}.sl", u))
                    pe.matmul(ps[u][:, 3, S:2 * S], b_A[:, :], SB[u].sl, start=True, stop=True)
                    pe.wait_ge(*at(f"{k}.sq", u))
                    pe.matmul(ps[u][:, 3, 0:S], b_mean[:, :], SB[u].sq, start=True, stop=True).then_inc(*done("tensor", f"{k}.ms_p", u))
                for g in range(MP + 2):
                    for u in LANES:
                        z = SB[u]
                        if g == 0:
                            pe.wait_ge(*at(f"{k}.qk", u))
                        if 2 <= g < MP:
                            pe.wait_ge(*at(f"{k}.att{2 * g - 3}", u))
                        for m in range(2 * g, min(2 * g + 2, MT)):
                            o = pe.matmul(ps[u][0:rows(m), g % 2, S * (m % 2):S * (m % 2) + S], z.pT[:, P * m:P * m + rows(m)], z.qk, start=True, stop=True)
                            if m % 2 or m == MT - 1:
                                o.then_inc(*done("tensor", f"{k}.s_p{g}", u))
                    for u in LANES:
                        z = SB[u]
                        if g == MP + 1:
                            pe.wait_ge(*at(f"{k}.att{MT - 1}", u))
                            for j in range(2):
                                pe.matmul(ps[u][:, j, 0:S], b_hhT[:, P * j:P * j + P], z.sl, start=True, stop=False)
                        if g >= 2:
                            pe.wait_ge(*at(f"{k}.pw{g - 2}", u))
                        for m in range(max(2 * g - 4, 0), min(2 * g - 2, MT)):
                            for j in range(2):
                                o = pe.matmul(ps[u][:, 2 + j, 0:P + 1], z.att[0:rows(m), m, P * j:P * j + P], z.pw[0:rows(m), m, :],
                                              start=m == 0, stop=m == MT - 1)
                        if g == MP + 1:
                            o.then_inc(*done("tensor", f"{k}.u_p", u))
                for u in LANES:
                    pe.wait_ge(*at(f"{k}.un", u))
                    for j in range(2):
                        o = pe.transpose(ps[u][:, 2, P * j:P * j + P], SB[u].un[:, j, :], ident[:, :])
                    o.then_inc(*done("tensor", f"{k}.uT_p", u))
                    pe.matmul(ps[u][:, 3, S:2 * S], b_hhT[:, 2 * P:3 * P], SB[u].sl, start=True, stop=True)
                for u in LANES:
                    z = SB[u]
                    pe.wait_ge(*at(f"{k}.uT", u))
                    for j in range(2):
                        pe.matmul(ps[u][:, j, 0:S], b_C[:, P * j:P * j + P], z.uT, start=False, stop=True)
                    pe.matmul(ps[u][:, 3, 0:S], b_C[:, 2 * P:3 * P], z.uT, start=True, stop=True).then_inc(*done("tensor", f"{k}.gru_p", u))
            for u in LANES:
                pe.wait_ge(*at(f"B.{ITERS - 1}.sl", u))
                for i in range(TT):
                    o = pe.transpose(ps[u][:, 0, P * i:P * i + P], SB[u].sl[:, P * i:P * i + P], ident[:, :])
                o.then_inc(*done("tensor", "B.y_p", u))
            for u in LANES:
                pe.wait_ge(*at("B.xn", u))
                pe.wait_ge(*at("B.res", u))
                for m in range(MT):
                    o = pe.transpose(ps[u][:, m // 4, P * (m % 4):P * (m % 4) + rows(m)], SB[u].xn[0:rows(m), m, :], ident[0:rows(m), 0:rows(m)])
                o.then_inc(*done("tensor", "B.xnT_p", u))

        def b_statistics(v, u):
            z = SB[u]
            v.wait_ge(s_ctx[u], 32)
            for m in range(MT):
                mark(v, "vector", v.bn_stats(z.st[:, m, :], z.ctx[:, m, :]), f"B.cst{m}", u)
            v.wait_ge(*at(f"B.cst{MT - 1}", u))
            me, mo, ce, co = (z.st[:, :, i] for i in (1, 4, 2, 5))
            step(v, "vector", v.tensor_tensor(z.mean, me, mo, ALU.add), "B.cmean0", u)
            step(v, "vector", v.tensor_tensor(z.df, me, mo, ALU.subtract), "B.df", u)
            step(v, "vector", v.tensor_scalar(z.mean, z.mean, 0.5, None, ALU.mult), "B.cmean", u)
            step(v, "vector", v.tensor_tensor(z.df, z.df, z.df, ALU.mult), "B.df2", u)
            step(v, "vector", v.tensor_tensor(z.vv[:, 0, :], ce, co, ALU.add), "B.cv", u)
            step(v, "vector", v.tensor_scalar(z.vv[:, 0, :], z.vv[:, 0, :], 1.0 / D, None, ALU.mult), "B.cvd", u)
            step(v, "vector", v.scalar_tensor_tensor(out=z.vv[:, 0, :], in0=z.df, scalar=0.25, in1=z.vv[:, 0, :], op0=ALU.mult, op1=ALU.add), "B.cvar", u)
            step(v, "vector", v.tensor_tensor(z.vv[:, 1, :], z.mean, z.mean, ALU.mult), "B.msq", u)
            step(v, "vector", v.tensor_tensor(z.vv[:, 1, :], z.vv[:, 1, :], z.vv[:, 0, :], ALU.add), "B.ms", u)
            step(v, "vector", v.tensor_scalar(z.vv[:, 0, :], z.vv[:, 0, :], 1e-5, None, ALU.add), "B.vare", u)
            step(v, "vector", v.tensor_scalar(z.vv[:, 1, :], z.vv[:, 1, :], 1e-6, None, ALU.add), "B.vv", u)

        def b_normed(v, u):
            z = SB[u]
            v.wait_ge(*at("B.cpower", u))
            rsqrt_newton(v, "B.c", u, z.rr, z.vv, z.t1)
            step(v, "vector", v.tensor_tensor(z.p[:, :, 0:P], z.ctx, over(z.rr[:, 1, :].unsqueeze(2), [P, MT, P]), ALU.mult), "B.p0", u)
            step(v, "vector", v.memset(z.p[:, :, P:P + 1], 1.0), "B.p", u)

        def b_vector(v):
            for u in LANES:
                v.wait_ge(*at("B.slT_p", u))
                step(v, "vector", v.tensor_copy(SB[u].sl, ps[u][:, 0, 0:S]), "B.sl", u)
            for r in range(ITERS):
                k = f"B.{r}"
                for u in LANES:
                    z = SB[u]
                    mark(v, "vector", v.tensor_tensor(z.sq, z.sl, z.sl, ALU.mult), f"{k}.sq", u)
                for u in LANES:
                    z = SB[u]
                    v.wait_ge(*at(f"{k}.power", u))
                    mark(v, "vector", v.scalar_tensor_tensor(out=z.qk, in0=ps[u][:, 3, S:2 * S], scalar=b_small[:, 3:4], in1=z.t, op0=ALU.mult, op1=ALU.mult), f"{k}.qk", u)
                for g in range(MP):
                    n = min(2, MT - 2 * g)
                    q = rows(2 * g + n - 1)
                    for u in LANES:
                        z = SB[u]
                        v.wait_ge(*at(f"{k}.s_p{g}", u))
                        mark(v, "vector", v.tensor_reduce(z.mx[0:q, 2 * g:2 * g + n], ps[u][0:q, g % 2, 0:S * n].rearrange("p (m k) -> p m k", m=n), AX.X, ALU.max, negate=True), f"{k}.nmx{g}", u)
                    if g >= 1:
                        b_weigh(v, k, g - 1)
                b_weigh(v, k, MP - 1)
                for u in LANES:
                    z = SB[u]
                    v.wait_ge(*at(f"{k}.u_p", u))
                    step(v, "vector", v.tensor_scalar(z.rd, ps[u][:, 2:4, P], 1e-6, None, ALU.add), f"{k}.rd0", u)
                    step(v, "vector", v.reciprocal(z.rd, z.rd), f"{k}.rd", u)
                    step(v, "vector", v.tensor_tensor(z.un, ps[u][:, 2:4, 0:P], over(z.rd.unsqueeze(2), [P, 2, P]), ALU.mult), f"{k}.un", u)
                for u in LANES:
                    z = SB[u]
                    v.wait_ge(*at(f"{k}.r", u))
                    step(v, "vector", v.scalar_tensor_tensor(out=z.t, in0=ps[u][:, 3, S:2 * S], scalar=b_bias[:, 1, 2:3], in1=z.rz[:, 0:S], op0=ALU.add, op1=ALU.mult), f"{k}.t0", u)
                    step(v, "vector", v.tensor_tensor(z.t, ps[u][:, 3, 0:S], z.t, ALU.add), f"{k}.t1", u)
                for u in LANES:
                    z = SB[u]
                    v.wait_ge(*at(f"{k}.en", u))
                    step(v, "vector", v.tensor_scalar(z.n, z.n, -2.0, 1.0, ALU.mult, ALU.add), f"{k}.n", u)
                    step(v, "vector", v.tensor_tensor(z.t, z.sl, z.n, ALU.subtract), f"{k}.d0", u)
                    v.wait_ge(*at(f"{k}.z", u))
                    step(v, "vector", v.tensor_tensor(z.t, z.rz[:, S:2 * S], z.t, ALU.mult), f"{k}.d1", u)
                    step(v, "vector", v.tensor_tensor(z.sl, z.n, z.t, ALU.add), f"{k}.sl", u)
            for u in LANES:
                v.wait_ge(*at("B.y_p", u))
                norm_vector_1(v, "B", u, ps[u][:, 0, 0:S].rearrange("p (i d) -> p i d", i=TT))
            for u in LANES:
                norm_vector_2(v, "B", u)

        def b_weigh(v, k, g):
            n = min(2, MT - 2 * g)
            q = rows(2 * g + n - 1)
            for u in LANES:
                z = SB[u]
                v.wait_ge(*at(f"{k}.att{2 * g + n - 1}", u))
                step(v, "vector", v.reciprocal(z.rs[0:q, 2 * g:2 * g + n], z.rs[0:q, 2 * g:2 * g + n]), f"{k}.rs{g}", u)
                mark(v, "vector", v.tensor_tensor(z.pw[0:q, 2 * g:2 * g + n, :], z.p[0:q, 2 * g:2 * g + n, :],
                                                  over(z.rs[0:q, 2 * g:2 * g + n].unsqueeze(2), [q, n, P + 1]), ALU.mult), f"{k}.pw{g}", u)

        def b_powers(a, u):
            z = SB[u]
            a.wait_ge(*at("B.vv", u))
            step(a, "scalar", a.activation(z.t1, z.vv, ACT.Ln), "B.cln", u)
            mark(a, "scalar", a.activation(z.rr, z.t1, ACT.Exp, scale=-0.5), "B.cpower", u)

        def b_sigmoid(a, k, u, j):
            z = SB[u]
            g = z.rz[:, S * j:S * j + S]
            name = "rz"[j]
            a.wait_ge(*at(f"{k}.gru_p", u))
            step(a, "scalar", a.activation(g, ps[u][:, j, 0:S], ACT.Exp, scale=-1.0, bias=b_small[:, j:j + 1]), f"{k}.e{name}", u)
            step(a, "scalar", a.activation(g, g, ACT.Ln, bias=one_col[:, 0:1]), f"{k}.l{name}", u)
            mark(a, "scalar", a.activation(g, g, ACT.Exp, scale=-1.0), f"{k}.{name}", u)

        def b_tanh(a, k, u):
            z = SB[u]
            a.wait_ge(*at(f"{k}.t1", u))
            step(a, "scalar", a.activation(z.n, z.t, ACT.Exp, scale=2.0, bias=b_small[:, 2:3]), f"{k}.en0", u)
            step(a, "scalar", a.activation(z.n, z.n, ACT.Ln, bias=one_col[:, 0:1]), f"{k}.ln1", u)
            mark(a, "scalar", a.activation(z.n, z.n, ACT.Exp, scale=-1.0), f"{k}.en", u)

        def b_scalar(a):
            for u in LANES:
                a.wait_ge(*at("B.pT_p", u))
                mark(a, "scalar", a.activation(SB[u].pT, ps[u][:, :, :].rearrange("p b c -> p (b c)")[:, 0:SC], ACT.Copy), "B.pT", u)
            for r in range(ITERS):
                k = f"B.{r}"
                for u in LANES:
                    z = SB[u]
                    a.wait_ge(*at(f"{k}.ms_p", u))
                    step(a, "scalar", a.activation(z.t, ps[u][:, 3, 0:S], ACT.Ln, bias=eps6[:, 0:1]), f"{k}.ln", u)
                    step(a, "scalar", a.activation(z.t, z.t, ACT.Exp, scale=-0.5), f"{k}.power", u)
                for g in range(MP):
                    for u in LANES:
                        z = SB[u]
                        a.wait_ge(*at(f"{k}.nmx{g}", u))
                        for m in range(2 * g, min(2 * g + 2, MT)):
                            q = rows(m)
                            mark(a, "scalar", a.activation(z.att[0:q, m, :], ps[u][0:q, g % 2, S * (m % 2):S * (m % 2) + S], ACT.Exp,
                                                           bias=z.mx[0:q, m:m + 1], accum_out=z.rs[0:q, m:m + 1]), f"{k}.att{m}", u)
                for u in LANES:
                    a.wait_ge(*at(f"{k}.uT_p", u))
                    step(a, "scalar", a.activation(SB[u].uT, ps[u][:, 2, 0:S], ACT.Copy), f"{k}.uT", u)
                b_sigmoid(a, k, 0, 0)
                b_sigmoid(a, k, 0, 1)
                b_sigmoid(a, k, 1, 0)
                b_tanh(a, k, 0)
                b_sigmoid(a, k, 1, 1)
                b_tanh(a, k, 1)
            for u in LANES:
                norm_scalar(a, "B", u)
            for u in LANES:
                a.wait_ge(*at("B.xnT_p", u))
                mark(a, "scalar", a.activation(kvT[u][:, 0:SC], ps[u][:, :, :].rearrange("p b c -> p (b c)")[:, 0:SC], ACT.Identity,
                                               scale=e_ln[:, 0:1], bias=e_ln[:, 1:2]), "B.xnT", u)

        def b_pool(g):
            for u in LANES:
                z = SB[u]
                g.wait_ge(*at("B.c.rstd", u))
                g.wait_ge(*at("A.x1", u))
                step(g, "pool", g.tensor_tensor(z.xn, z.ctx, over(z.mean.unsqueeze(2), [P, MT, P]), ALU.subtract), "B.xn0", u)
                step(g, "pool", g.tensor_tensor(z.xn, z.xn, over(z.rr[:, 0, :].unsqueeze(2), [P, MT, P]), ALU.mult), "B.xn", u)

        CH, CD, CE = 16, 64, 8
        CP = CH // 2
        c_wkT = sb("c_wkT", [P, CH * CD])
        c_wvT = sb("c_wvT", [P, CE * CD])
        c_wgT = sb("c_wgT", [P, 2 * CH * CE])
        c_woT = sb("c_woT", [P, 4, P])
        c_order = sb("c_order", [P, CE])
        cp_ = [sb(f"c_prob{i}", [P, TT, S]) for i in range(2)]
        ct_ = [sb(f"c_probT{i}", [P, TT, S]) for i in range(2)]

        class StageC:
            def __init__(self, u):
                c = Carve(u)
                self.gT = c(TT, 4, P)
                c(CP * S - TT * 4 * P)
                self.k = c(CP, S)
                self.pv = c(TT, CE, CD)
                self.v = c(TT, CH, CD)
                self.att = c(TT, CH, CD)
                self.e1 = c(2048)
                self.gate = c(TT, 2, CH, CE)
                self.k1 = c(TT, 2, CH, CE)
                self.k2 = c(TT, 2, CH, CE)
                self.ix = c(TT, 2, CH, CE)
                self.m = c(TT * 2 * CH)
                self.mix = c(TT, CH, CE)
                self.mx = c(CH, TT)
                self.rs = c(CH, TT)
                self.e2 = c(2048)
                self.prod = [self.e1, self.e2]
                self.g = self.pv

        SC_ = [StageC(u) for u in LANES]
        c_q = [area[1][:, 1024 * i:1024 * i + 1024].rearrange("p (h q) -> p h q", h=4) for i in range(2)]
        C_UNITS = [(u, h) for u in LANES for h in range(CH)]

        def c_load(sp):
            def rows_of(t):
                return t.rearrange("a b c -> (a b) c").rearrange("(g p) c -> p g c", p=P)
            def part(u, a, g):
                return kvT[u][:, a:a + g * P].rearrange("p (g c) -> p g c", g=g)
            sp.dma_start(part(0, 0, 8), rows_of(w["L0_ffn_Wq"])).then_inc(s_weights, 16)
            sp.dma_start(part(1, 0, 8), rows_of(w["L0_ffn_Wk"])).then_inc(s_weights, 16)
            sp.dma_start(part(0, 1024, 4), rows_of(w["L0_ffn_Wv"])).then_inc(s_weights, 16)
            sp.dma_start(part(0, 1536, 1), rows_of(w["L0_ffn_Ws"])).then_inc(s_weights, 16)
            sp.dma_start(part(1, 1536, 1), rows_of(w["L0_ffn_Wd"])).then_inc(s_weights, 16)
            sp.dma_start(kvT[1][:, 1024:1536].rearrange("p (e d) -> p e d", e=CE), w["L0_ffn_Wo"].rearrange("e f d -> f e d")).then_inc(s_weights, 16)

        def c_setup_pool(g):
            for e in range(CE):
                g.memset(c_order[:, e:e + 1], float(CE - e)).then_inc(s_pool, 1)

        def c_setup_tensor(pe):
            for i in range(8):
                for u in LANES:
                    m = pe.transpose(ps[1][:, 2 * u + i // 4, P * (i % 4):P * (i % 4) + P], kvT[u][:, P * i:P * i + P], ident[:, :])
            m.then_inc(*done("tensor", "setup.c1_p"))
            pe.wait_ge(*at("setup.c_wk"))
            for i in range(4):
                pe.transpose(ps[1][:, 0, P * i:P * i + P], kvT[0][:, 1024 + P * i:1024 + P * i + P], ident[:, :])
                pe.transpose(ps[1][:, 1, P * i:P * i + P], kvT[1][:, 1024 + P * i:1024 + P * i + P], ident[:, :])
            for u in LANES:
                m = pe.transpose(ps[1][:, 2, P * u:P * u + P], kvT[u][:, 1536:1536 + P], ident[:, :])
            m.then_inc(*done("tensor", "setup.c2_p"))

        def c_setup_vector(v):
            v.wait_ge(*at("setup.c1_p"))
            step(v, "vector", v.tensor_scalar(c_wqT[:, :], ps[1][:, 0:2, :].rearrange("p a b -> p (a b)"), float(CD) ** -0.5, None, ALU.mult), "setup.c_wq")
            step(v, "vector", v.tensor_copy(c_wkT[:, :], ps[1][:, 2:4, :].rearrange("p a b -> p (a b)")), "setup.c_wk")
            v.wait_ge(*at("setup.c2_p"))
            step(v, "vector", v.tensor_copy(c_wvT[:, :], ps[1][:, 0, :]), "setup.c_wv")
            step(v, "vector", v.tensor_copy(c_woT[:, :, :], ps[1][:, 1, :].rearrange("p (a b) -> p a b", a=4)), "setup.c_wo")
            step(v, "vector", v.tensor_copy(c_wgT[:, :], ps[1][:, 2, 0:2 * P]), "setup.c_wg")

        def transposed_x(pe, tag):
            for u in LANES:
                for i in range(TT):
                    m = pe.transpose(ps[u][:, 0, P * i:P * i + P], X[u][:, i, :], ident[:, :])
                m.then_inc(*done("tensor", f"{tag}.xT_p", u))

        def copy_xT(v, tag):
            for u in LANES:
                v.wait_ge(*at(f"{tag}.xT_p", u))
                step(v, "vector", v.tensor_copy(XT[u][:, :], ps[u][:, 0, 0:S]), f"{tag}.xT", u)

        C_GROUPS = len(LANES) * 2 * (CH // 4)
        C_QK_AT = {4 * (m // 2 - 1) + m % 2: m for m in range(2, C_GROUPS)}

        def c_qk_tensor(pe, m):
            u, j = m // 8, m % 8 // 2
            weights = c_wqT if m % 2 == 0 else c_wkT
            if m >= 2:
                pe.wait_ge(*at(f"C.qk{m - 2}"))
            for c in range(2):
                q = pe.matmul(ps[1][:, 2 + m % 2, S * c:S * c + S], weights[:, P * (2 * j + c):P * (2 * j + c) + P], XT[u][:, :], start=True, stop=True)
            q.then_inc(*done("tensor", f"C.qk_p{m}"))

        def c_qk_scalar(a, m):
            u, j = m // 8, m % 8 // 2
            if m == 0:
                a.wait_ge(*at("C.zero"))
            a.wait_ge(*at(f"C.qk_p{m}"))
            if m % 2 == 0:
                if m >= 4:
                    a.wait_ge(*at(f"C.s_p{4 * (m // 2 - 2) + 3}"))
                for half in range(2):
                    r = CD * half
                    mark(a, "scalar", a.activation(c_q[m // 2 % 2][r:r + CD, half:4:2, :], ps[1][r:r + CD, 2, :].rearrange("p (c q) -> p c q", c=2), ACT.Copy),
                         f"C.qk{m}" if half else f"C.qka{m}")
            else:
                mark(a, "scalar", a.activation(SC_[u].k[:, 2 * j:2 * j + 2, :].rearrange("p a b -> p (a b)"), ps[1][:, 3, :], ACT.Copy), f"C.qk{m}")

        def c_pv_banks(u):
            return ps[0][:, 2:4, :] if u == 0 else ps[1][:, 0:2, :]

        def c_tensor(pe):
            for u in LANES:
                pe.wait_ge(*at("B.x1", u))
                pe.wait_ge(*at("B.xnT", u))
                for i in range(TT):
                    m = pe.transpose(ps[u][:, 0, P * i:P * i + P], X[u][:, i, :], ident[:, :])
                m.then_inc(*done("tensor", "C.xT_p", u))
            for u in LANES:
                pe.wait_ge(*at("C.xT", u))
                for i in range(TT):
                    m = pe.matmul(ps[0][:, u, S * i:S * i + S], XT[u][:, P * i:P * i + P], c_wgT[:, :], start=True, stop=True)
                m.then_inc(*done("tensor", "C.gate_p", u))
            for m in range(2):
                c_qk_tensor(pe, m)
            for u in LANES:
                for i in range(TT):
                    m = pe.matmul(c_pv_banks(u)[:, i, :], XT[u][:, P * i:P * i + P], c_wvT[:, :], start=True, stop=True)
                m.then_inc(*done("tensor", "C.pv_p", u))
            last = len(C_UNITS)
            for n in range(last + 2):
                if n < last:
                    u, h = C_UNITS[n]
                    z = SC_[u]
                    if n < 2:
                        pe.wait_ge(*at("C.gate", n))
                    if n >= 2:
                        pe.wait_ge(*at(f"C.exp{n - 2}"))
                    if h % 4 == 0:
                        pe.wait_ge(*at(f"C.qk{CH // 2 * u + 2 * (h // 4) + 1}"))
                    for i in range(TT):
                        m = pe.matmul(ps[0][:, n % 2, S * i:S * i + S], c_q[n // 4 % 2][:, h % 4, P * i:P * i + P], z.k[:, h // 2, :], start=True, stop=True)
                    m.then_inc(*done("tensor", f"C.s_p{n}"))
                if n in C_QK_AT:
                    c_qk_tensor(pe, C_QK_AT[n])
                if 1 <= n < last + 1:
                    o = n - 1
                    pe.wait_ge(*at(f"C.exp{o}"))
                    if o == 0:
                        pe.wait_ge(*at("C.pv", 0))
                    if o >= 2:
                        pe.wait_ge(*at(f"C.pT{o - 2}"))
                    for j in range(TT):
                        for i in range(TT):
                            m = pe.transpose(ps[0][:, 2 + o % 2, S * j + P * i:S * j + P * i + P], cp_[o % 2][:, i, P * j:P * j + P], ident[:, :])
                    m.then_inc(*done("tensor", f"C.pT_p{o}"))
                if n >= 2:
                    o = n - 2
                    u, h = C_UNITS[o]
                    z = SC_[u]
                    if o == 0:
                        pe.wait_ge(*at("C.pv", 1))
                    if h % 4 == 0:
                        pe.wait_ge(*at(f"C.v{2 * (h // 4) + 1}", u))
                    pe.wait_ge(*at(f"C.pT{o}"))
                    if o >= 2:
                        pe.wait_ge(*at(f"C.att{o - 2}"))
                    for i in range(TT):
                        for j in range(TT):
                            m = pe.matmul(ps[1][:, o % 2, CD * i:CD * i + CD], ct_[o % 2][:, j, P * i:P * i + P], z.v[:, j, h, :], start=j == 0, stop=j == TT - 1)
                    m.then_inc(*done("tensor", f"C.o_p{o}"))
            for u in LANES:
                z = SC_[u]
                pe.wait_ge(*at("C.g7", u))
                if u == 1:
                    pe.wait_ge(*at("C.res", 0))
                for i in range(TT):
                    for c in range(4):
                        m = pe.transpose(ps[1][:, 2 + i, P * c:P * c + P], z.g[:, i, 2 * c:2 * c + 2, :], ident[:, :])
                m.then_inc(*done("tensor", "C.gT_p", u))
                if u == 0:
                    pe.wait_ge(*at(f"C.att{last - 1}"))
                pe.wait_ge(*at("C.gT", u))
                for i in range(TT):
                    for c in range(4):
                        m = pe.matmul(ps[1][:, u, P * i:P * i + P], z.gT[:, i, c, :], c_woT[:, c, :], start=c == 0, stop=c == 3)
                m.then_inc(*done("tensor", "C.y_p", u))

        C_PICK = 12

        def c_pick(v, u, k, i):
            z = SC_[u]
            gate, k1, k2, ix = (t[:, :, k, :, :] for t in (z.gate, z.k1, z.k2, z.ix))
            m = z.m.rearrange("p (i k h) -> p i k h", i=TT, k=2)[:, :, k, :]
            mb = over(m.unsqueeze(3), [P, TT, CH, CE])
            order = over(c_order[:, :].unsqueeze(1).unsqueeze(1), [P, TT, CH, CE])
            if i:
                v.wait_ge(*at(f"C.pick{k}{i - 1}", u))
            src, dst = (gate, k1) if i < 5 else (k2, k2)
            if i == 5:
                o = v.scalar_tensor_tensor(out=k2, in0=k1, scalar=NEG, in1=gate, op0=ALU.mult, op1=ALU.add)
            elif i == 11:
                o = v.tensor_tensor(k1, k1, k2, ALU.add)
            elif i in (0, 6):
                o = v.tensor_reduce(m, src, AX.X, ALU.max)
            elif i in (1, 7):
                o = v.tensor_tensor(ix, src, mb, ALU.is_equal)
            elif i in (2, 8):
                o = v.tensor_tensor(ix, ix, order, ALU.mult)
            elif i in (3, 9):
                o = v.tensor_reduce(m, ix, AX.X, ALU.max)
            else:
                o = v.tensor_tensor(dst, ix, mb, ALU.is_equal)
            mark(v, "vector", o, f"C.pick{k}{i}", u)

        def c_mix(v, u):
            z = SC_[u]
            v.wait_ge(*at(f"C.pick0{C_PICK - 1}", u))
            v.wait_ge(*at("C.sig", u))
            mark(v, "vector", v.tensor_tensor(z.mix, z.mix, z.k1[:, :, 0, :, :], ALU.mult), "C.mix", u)

        def c_v_vector(v, m):
            u, j, i = m // 8, m % 8 // 2, m % 2
            z = SC_[u]
            v.wait_ge(*at(f"C.prodv{m % 8}", u))
            mark(v, "vector", v.tensor_reduce(z.v[:, i, 4 * j:4 * j + 4, :], z.prod[m % 2].rearrange("p (h e d) -> p h d e", h=4, e=CE), AX.X, ALU.add),
                 f"C.v{m % 8}", u)

        C_PROD_VECTOR = (1, 4)

        def c_prod_o(u, n):
            z = SC_[u]
            if u == 1 and n in C_PROD_VECTOR:
                return z.v.rearrange("p i h d -> p (i h d)")
            if u == 1:
                n -= sum(m < n for m in C_PROD_VECTOR)
            return z.prod[n % 2]

        def c_g_vector(v, u, n):
            i, c = n // 4, n % 4
            z = SC_[u]
            v.wait_ge(*at(f"C.prodo{n}", u))
            mark(v, "vector", v.tensor_reduce(z.g[:, i, 2 * c:2 * c + 2, :], c_prod_o(u, n).rearrange("p (e h d) -> p e d h", e=2, h=CH), AX.X, ALU.add),
                 f"C.g{n}", u)

        C_V_AT = {4 * m // 3: m + 2 for m in range(C_GROUPS - 2)}
        C_G_AT = {20 + 3 * n // 2: n for n in range(8)}

        def c_prod_vector(v, u, n):
            z = SC_[u]
            i, c = n // 4, n % 4
            step(v, "vector", v.tensor_tensor(c_prod_o(u, n).rearrange("p (e h d) -> p e h d", e=2, h=CH),
                                              over(z.k1[:, i, 1, :, 2 * c:2 * c + 2].rearrange("p h e -> p e h").unsqueeze(3), [P, 2, CH, CD]),
                                              over(z.att[:, i:i + 1, :, :], [P, 2, CH, CD]), ALU.mult), f"C.prodo{n}", u)

        def c_vector(v):
            for u in LANES:
                v.wait_ge(*at("C.xT_p", u))
                mark(v, "vector", v.tensor_copy(XT[u][:, :], ps[u][:, 0, 0:S]), "C.xT", u)
            for u in LANES:
                v.wait_ge(*at("C.gate_p", u))
                step(v, "vector", v.tensor_copy(SC_[u].gate.rearrange("p i k h e -> p (i k h e)"), ps[0][:, u, :]), "C.gate", u)
            for u in LANES:
                for i in range(C_PICK):
                    c_pick(v, u, 0, i)
                c_mix(v, u)
            for m in range(2):
                c_v_vector(v, m)
            last = len(C_UNITS)
            for n in range(last + 2):
                if n < last:
                    u, h = C_UNITS[n]
                    z = SC_[u]
                    v.wait_ge(*at(f"C.s_p{n}"))
                    mark(v, "vector", v.tensor_reduce(z.mx[:, h, :], ps[0][:, n % 2, :].rearrange("p (i k) -> p i k", i=TT), AX.X, ALU.max, negate=True), f"C.nmx{n}")
                if n in C_V_AT:
                    c_v_vector(v, C_V_AT[n])
                if n < 2 * C_PICK:
                    c_pick(v, n // C_PICK, 1, n % C_PICK)
                if n in C_G_AT:
                    c_g_vector(v, 0, C_G_AT[n])
                if n >= 2:
                    o = n - 2
                    u, h = C_UNITS[o]
                    z = SC_[u]
                    v.wait_ge(*at(f"C.exp{o}"))
                    step(v, "vector", v.reciprocal(z.rs[:, h, :], z.rs[:, h, :]), f"C.rs{o}", 0)
                    v.wait_ge(*at(f"C.o_p{o}"))
                    mark(v, "vector", v.tensor_tensor(z.att[:, :, h, :], ps[1][:, o % 2, 0:TT * CD].rearrange("p (i d) -> p i d", i=TT),
                                                      over(z.rs[:, h, :].unsqueeze(2), [P, TT, CD]), ALU.mult), f"C.att{o}")
            v.wait_ge(*at(f"C.att{last - 1}"))
            for n in range(3):
                if n in C_PROD_VECTOR:
                    c_prod_vector(v, 1, n)
                c_g_vector(v, 1, n)
            v.wait_ge(*at("C.y_p", 0))
            norm_vector_1(v, "C", 0, ps[1][:, 0, 0:S].rearrange("p (i d) -> p i d", i=TT))
            for n in range(3, 6):
                if n in C_PROD_VECTOR:
                    c_prod_vector(v, 1, n)
                c_g_vector(v, 1, n)
            norm_vector_2(v, "C", 0)
            for n in range(6, 8):
                c_g_vector(v, 1, n)
            v.wait_ge(*at("C.y_p", 1))
            norm_vector_1(v, "C", 1, ps[1][:, 1, 0:S].rearrange("p (i d) -> p i d", i=TT))
            norm_vector_2(v, "C", 1)

        def c_scalar(a):
            for u in LANES:
                z = SC_[u]
                a.wait_ge(*at("C.gate", u))
                step(a, "scalar", a.activation(z.mix, z.gate[:, :, 0, :, :], ACT.Exp, scale=-1.0), "C.gexp", u)
                step(a, "scalar", a.activation(z.mix, z.mix, ACT.Ln, bias=one_col[:, 0:1]), "C.gln", u)
                mark(a, "scalar", a.activation(z.mix, z.mix, ACT.Exp, scale=-1.0), "C.sig", u)
            for m in range(2):
                c_qk_scalar(a, m)
            for u in LANES:
                a.wait_ge(*at("C.pv_p", u))
                mark(a, "scalar", a.activation(SC_[u].pv.rearrange("p i e d -> p (i e d)"), c_pv_banks(u).rearrange("p a b -> p (a b)"), ACT.Copy), "C.pv", u)
            last = len(C_UNITS)
            for n in range(last + 1):
                if n < last:
                    u, h = C_UNITS[n]
                    z = SC_[u]
                    a.wait_ge(*at(f"C.nmx{n}"))
                    if n >= 2:
                        a.wait_ge(*at(f"C.pT_p{n - 2}"))
                    for i in range(TT):
                        m = a.activation(cp_[n % 2][:, i, :], ps[0][:, n % 2, S * i:S * i + S], ACT.Exp, bias=z.mx[:, h, i:i + 1], accum_out=z.rs[:, h, i:i + 1])
                        mark(a, "scalar", m, f"C.exp{n}" if i == TT - 1 else f"C.expa{n}")
                if n in C_QK_AT:
                    c_qk_scalar(a, C_QK_AT[n])
                if n >= 1:
                    o = n - 1
                    a.wait_ge(*at(f"C.pT_p{o}"))
                    if o >= 2:
                        a.wait_ge(*at(f"C.o_p{o - 2}"))
                    mark(a, "scalar", a.activation(ct_[o % 2][:, :, :].rearrange("p j i -> p (j i)"), ps[0][:, 2 + o % 2, :], ACT.Copy), f"C.pT{o}")
            for u in LANES:
                z = SC_[u]
                a.wait_ge(*at("C.gT_p", u))
                mark(a, "scalar", a.activation(z.gT.rearrange("p i c q -> p (i c q)"), ps[1][:, 2:4, :].rearrange("p a b -> p (a b)"), ACT.Copy), "C.gT", u)
                norm_scalar(a, "C", u)

        def c_pool(g):
            g.wait_ge(*at("B.x1", 1))
            mark(g, "pool", g.memset(area[1][:, 0:2048], 0.0), "C.zero")
            for u in LANES:
                z = SC_[u]
                g.wait_ge(*at("C.mix", u))
                g.wait_ge(*at("C.pv", u))
                for n in range(8):
                    j, i = n // 2, n % 2
                    if n >= 2:
                        g.wait_ge(*at(f"C.v{n - 2}", u))
                    mark(g, "pool", g.tensor_tensor(z.prod[n % 2].rearrange("p (h e d) -> p h e d", h=4, e=CE),
                                                    over(z.mix[:, i, 4 * j:4 * j + 4, :].unsqueeze(3), [P, 4, CE, CD]),
                                                    over(z.pv[:, i:i + 1, :, :], [P, 4, CE, CD]), ALU.mult), f"C.prodv{n}", u)
            for u in LANES:
                z = SC_[u]
                g.wait_ge(*at(f"C.att{CH * u + CH - 1}"))
                g.wait_ge(*at(f"C.pick1{C_PICK - 1}", u))
                groups = [n for n in range(8) if u == 0 or n not in C_PROD_VECTOR]
                for k, n in enumerate(groups):
                    i, c = n // 4, n % 4
                    if k >= 2:
                        g.wait_ge(*at(f"C.g{groups[k - 2]}", u))
                    mark(g, "pool", g.tensor_tensor(c_prod_o(u, n).rearrange("p (e h d) -> p e h d", e=2, h=CH),
                                                    over(z.k1[:, i, 1, :, 2 * c:2 * c + 2].rearrange("p h e -> p e h").unsqueeze(3), [P, 2, CH, CD]),
                                                    over(z.att[:, i:i + 1, :, :], [P, 2, CH, CD]), ALU.mult), f"C.prodo{n}", u)

        DI, DS, DJ = 256, 16, 2
        NC_ = 4
        SELU_L, SELU_A = 1.0507009873554805, 1.6732632423543772
        d_win = sb("d_win", [P, DI])
        d_bin = sb("d_bin", [P, DJ])
        d_A = sb("d_A", [P, DJ, DS])
        d_wbc = sb("d_wbc", [P, DJ, 2 * DS])
        d_bbc = sb("d_bbc", [2 * DS, 1])
        d_wd = sb("d_wd", [P, DJ, DI])
        d_bd = sb("d_bd", [P, DJ])
        d_D = sb("d_D", [P, DJ])
        d_wo = sb("d_wo", [P, DJ, P])
        d_bo = sb("d_bo", [1, P])
        d_pick = sb("d_pick", [96, 2 * DS])
        d_sel = sb("d_sel", [96, 2 * DS, P], BF16)
        d_bc3 = [sb(f"d_bc3{u}", [96, S], BF16) for u in LANES]

        class StageD:
            def __init__(self, u):
                c = Carve(u)
                self.h = c(DJ, S)
                self.lo = c(DJ, S)
                self.hi = c(DJ, S)
                self.a = c(DJ, S)
                self.dt = c(DJ, S)
                self.dh = c(DJ, S)
                self.bc = c(S)
                self.part = c(S)
                self.dA = [c(NC_, S) for _ in range(2)]
                self.B = [c(NC_, S) for _ in range(2)]
                self.dBu = [c(NC_, S) for _ in range(2)]
                self.s = [c(NC_, S) for _ in range(DJ)]
                self.yc = c(DJ, NC_, S)
                self.y = c(DJ, S)

        SD = [StageD(u) for u in LANES]

        def d_load(sp):
            def jp(t):
                return t.rearrange("(j p) c -> p j c", p=P)
            n = "L1_attn_"
            sp.dma_start(d_win[:, :], w[n + "W_in"]).then_inc(s_weights, 16)
            sp.dma_start(d_bin[:, :], col(n + "b_in"), allow_slow_non_contiguous=True).then_inc(s_weights, 16)
            sp.dma_start(d_A[:, :, :], jp(w[n + "A_log"])).then_inc(s_weights, 16)
            sp.dma_start(d_wbc[:, :, 0:DS], jp(w[n + "W_B"])).then_inc(s_weights, 16)
            sp.dma_start(d_wbc[:, :, DS:2 * DS], jp(w[n + "W_C"])).then_inc(s_weights, 16)
            sp.dma_start(d_bbc[0:DS, :], w[n + "b_B"].rearrange("(p a) -> p a", a=1)).then_inc(s_weights, 16)
            sp.dma_start(d_bbc[DS:2 * DS, :], w[n + "b_C"].rearrange("(p a) -> p a", a=1)).then_inc(s_weights, 16)
            sp.dma_start(d_wd[:, :, :], jp(w[n + "W_delta"])).then_inc(s_weights, 16)
            sp.dma_start(d_bd[:, :], col(n + "b_delta"), allow_slow_non_contiguous=True).then_inc(s_weights, 16)
            sp.dma_start(d_D[:, :], col(n + "D_param"), allow_slow_non_contiguous=True).then_inc(s_weights, 16)
            sp.dma_start(d_wo[:, :, :], jp(w[n + "W_out"])).then_inc(s_weights, 16)
            sp.dma_start(d_bo[:, :], w[n + "b_out"].rearrange("(a p) -> a p", a=1)).then_inc(s_weights, 16)

        def d_setup_pool(g):
            g.memset(one_col[:, :], 1.0).then_inc(s_pool, 1)

        def d_setup_scalar(a):
            a.wait_ge(s_weights, 16 * 54)
            step(a, "scalar", a.activation(d_A[:, :, :], d_A[:, :, :], ACT.Exp), "setup.expA")

        def d_setup_vector(v):
            v.wait_ge(*at("setup.expA"))
            step(v, "vector", v.tensor_scalar(d_A[:, :, :], d_A[:, :, :], -1.0, None, ALU.mult), "setup.A")
            step(v, "vector", v.tensor_tensor(d_pick[:, :], ident[0:96, 0:32], ident[0:96, 32:64], ALU.add), "setup.pick0")
            step(v, "vector", v.tensor_tensor(d_pick[:, :], d_pick[:, :], ident[0:96, 64:96], ALU.add), "setup.pick")
            step(v, "vector", v.tensor_copy(d_sel[:, :, :], over(d_pick[:, :].unsqueeze(2), [96, 2 * DS, P])), "setup.sel")

        def d_rows_tensor(pe, c):
            for h in range(NC_ // 2):
                for u in LANES:
                    k = NC_ // 2 * c + h
                    pe.wait_ge(*at("D.bc3" if k == 0 else f"D.B{k - 1}", u))
                    for n in range(2):
                        m = pe.matmul(ps[u][:, 0, S * n:S * n + S], d_sel[:, 2 * k + n, :], d_bc3[u][:, :], start=True, stop=True)
                    m.then_inc(*done("tensor", f"D.b_p{k}", u))

        def d_tensor(pe):
            for u in LANES:
                pe.wait_ge(*at("C.x1", u))
                for i in range(TT):
                    m = pe.transpose(ps[u][:, 0, P * i:P * i + P], X[u][:, i, :], ident[:, :])
                m.then_inc(*done("tensor", "D.xT_p", u))
            for u in LANES:
                pe.wait_ge(*at("D.xT", u))
                for j in range(DJ):
                    m = pe.matmul(ps[u][:, 1, S * j:S * j + S], d_win[:, P * j:P * j + P], XT[u][:, :], start=True, stop=True)
                m.then_inc(*done("tensor", "D.h_p", u))
            for u in LANES:
                z = SD[u]
                pe.wait_ge(*at("D.h", u))
                for k in range(DJ):
                    m = pe.matmul(ps[u][0:2 * DS, 2, 0:S], d_wbc[:, k, :], z.h[:, k, :], start=k == 0, stop=k == 1)
                m.then_inc(*done("tensor", "D.bc_p", u))
                for j in range(DJ):
                    for k in range(DJ):
                        m = pe.matmul(ps[u][:, 3, S * j:S * j + S], d_wd[:, k, P * j:P * j + P], z.h[:, k, :], start=k == 0, stop=k == 1)
                m.then_inc(*done("tensor", "D.delta_p", u))
            d_rows_tensor(pe, 0)
            for c in range(DS // NC_ + 1):
                if c + 1 < DS // NC_:
                    d_rows_tensor(pe, c + 1)
                for u in LANES:
                    pe.wait_ge(*at("D.dh" if c == 0 else f"D.yc{c - 1}1", u))
                    if c < DS // NC_:
                        for n in range(NC_):
                            m = pe.matmul(ps[u][:, 1 + n // 2, S * (n % 2):S * (n % 2) + S], d_sel[:, DS + NC_ * c + n, :], d_bc3[u][:, :], start=True, stop=True)
                        m.then_inc(*done("tensor", f"D.c_p{c}", u))
                    if c >= 1:
                        for n in range(NC_):
                            m = pe.matmul(ps[u][:, 3, :], ident[:, :], SD[u].yc[:, :, n, :], start=c == 1 and n == 0, stop=c == DS // NC_ and n == NC_ - 1)
                        m.then_inc(*done("tensor", f"D.sum_p{c - 1}", u))
            for u in LANES:
                z = SD[u]
                pe.wait_ge(*at("D.y", u))
                for i in range(TT):
                    for j in range(DJ):
                        pe.matmul(ps[u][:, 0, P * i:P * i + P], z.y[:, j, P * i:P * i + P], d_wo[:, j, :], start=j == 0, stop=False)
                    m = pe.matmul(ps[u][:, 0, P * i:P * i + P], ones_row[:, :], d_bo[:, :], start=False, stop=True)
                m.then_inc(*done("tensor", "D.y_p", u))

        def d_vector(v):
            copy_xT(v, "D")
            for u in LANES:
                z = SD[u]
                v.wait_ge(*at("D.h_p", u))
                for j in range(DJ):
                    mark(v, "vector", v.tensor_scalar(z.lo[:, j, :], ps[u][:, 1, S * j:S * j + S], d_bin[:, j:j + 1], 0.0, ALU.add, ALU.min), f"D.lo{j}", u)
                for j in range(DJ):
                    mark(v, "vector", v.tensor_scalar(z.hi[:, j, :], ps[u][:, 1, S * j:S * j + S], d_bin[:, j:j + 1], 0.0, ALU.add, ALU.max), f"D.hi{j}", u)
            for u in LANES:
                z = SD[u]
                v.wait_ge(*at("D.elo", u))
                step(v, "vector", v.tensor_scalar(z.lo, z.lo, SELU_L * SELU_A, -SELU_L * SELU_A, ALU.mult, ALU.add), "D.neg", u)
                step(v, "vector", v.scalar_tensor_tensor(out=z.h, in0=z.hi, scalar=SELU_L, in1=z.lo, op0=ALU.mult, op1=ALU.add), "D.h", u)
            for u in LANES:
                z = SD[u]
                v.wait_ge(*at("D.bc_p", u))
                r = slice(0, 2 * DS)
                step(v, "vector", v.tensor_scalar(z.bc[r, :], ps[u][r, 2, 0:S], d_bbc[:, :], None, ALU.add), "D.bc", u)
                for k in range(3):
                    step(v, "vector", v.tensor_copy(d_bc3[u][32 * k:32 * k + 32, :], z.bc[r, :]), f"D.bc3{k}" if k < 2 else "D.bc3", u)
                    if k < 2:
                        step(v, "vector", v.tensor_copy(z.part[r, :], d_bc3[u][32 * k:32 * k + 32, :]), f"D.part{k}", u)
                        step(v, "vector", v.tensor_tensor(z.bc[r, :], z.bc[r, :], z.part[r, :], ALU.subtract), f"D.rest{k}", u)
                v.wait_ge(*at("D.delta_p", u))
                for j in range(DJ):
                    mark(v, "vector", v.tensor_scalar(z.a[:, j, :], ps[u][:, 3, S * j:S * j + S], d_bd[:, j:j + 1], None, ALU.add), f"D.a{j}", u)
                v.wait_ge(*at("D.a1", u))
                mark(v, "vector", v.scalar_tensor_tensor(out=z.dt, in0=z.a, scalar=-1.0, in1=z.a, op0=ALU.mult, op1=ALU.max), "D.abs", u)
            for u in LANES:
                z = SD[u]
                v.wait_ge(*at("D.log", u))
                step(v, "vector", v.scalar_tensor_tensor(out=z.dt, in0=z.a, scalar=0.0, in1=z.dt, op0=ALU.max, op1=ALU.add), "D.dt", u)
                step(v, "vector", v.tensor_tensor(z.dh, z.dt, z.h, ALU.mult), "D.dh", u)
                for b in range(2):
                    step(v, "vector", v.memset(z.dA[b][:, :, 0:1], 0.0), f"D.start{b}", u)
            for c in range(DS // NC_):
                for u in LANES:
                    z = SD[u]
                    for j in range(DJ):
                        v.wait_ge(*at(f"D.dbu{c}{j}", u))
                        v.wait_ge(*at(f"D.dA{c}{j}", u))
                        if c >= 1:
                            v.wait_ge(*at(f"D.yc{c - 1}{j}", u))
                        mark(v, "vector", v.tensor_tensor_scan(z.s[j].rearrange("p n t -> p (n t)"), z.dA[j].rearrange("p n t -> p (n t)"),
                                                               z.dBu[j].rearrange("p n t -> p (n t)"), 0.0, ALU.mult, ALU.add), f"D.s{c}{j}", u)
                    v.wait_ge(*at(f"D.c_p{c}", u))
                    if c >= 1:
                        v.wait_ge(*at(f"D.sum_p{c - 1}", u))
                    for j in range(DJ):
                        v.wait_ge(*at(f"D.s{c}{j}", u))
                        mark(v, "vector", v.tensor_tensor(z.yc[:, j, :, :], z.s[j], ps[u][:, 1:3, :].rearrange("p b (n t) -> p (b n) t", t=S), ALU.mult), f"D.yc{c}{j}", u)
            for u in LANES:
                z = SD[u]
                v.wait_ge(*at(f"D.sum_p{DS // NC_ - 1}", u))
                for j in range(DJ):
                    mark(v, "vector", v.scalar_tensor_tensor(out=z.y[:, j, :], in0=z.h[:, j, :], scalar=d_D[:, j:j + 1], in1=ps[u][:, 3, S * j:S * j + S], op0=ALU.mult, op1=ALU.add), "D.y" if j else "D.y_", u)
            for u in LANES:
                v.wait_ge(*at("D.y_p", u))
                norm_vector_1(v, "D", u, ps[u][:, 0, 0:S].rearrange("p (i d) -> p i d", i=TT))
            for u in LANES:
                norm_vector_2(v, "D", u)

        def d_rows(a, c):
            for h in range(NC_ // 2):
                for u in LANES:
                    k = NC_ // 2 * c + h
                    a.wait_ge(*at(f"D.b_p{k}", u))
                    if c >= 2:
                        a.wait_ge(*at(f"D.dbu{c - 2}1", u))
                    mark(a, "scalar", a.activation(SD[u].B[c % 2][:, 2 * h:2 * h + 2, :].rearrange("p n t -> p (n t)"), ps[u][:, 0, :], ACT.Copy), f"D.B{k}", u)

        def d_scalar(a):
            for u in LANES:
                z = SD[u]
                a.wait_ge(*at("D.lo1", u))
                step(a, "scalar", a.activation(z.lo, z.lo, ACT.Exp), "D.elo", u)
            for u in LANES:
                z = SD[u]
                a.wait_ge(*at("D.abs", u))
                step(a, "scalar", a.activation(z.dt, z.dt, ACT.Exp, scale=-1.0), "D.eabs", u)
                step(a, "scalar", a.activation(z.dt, z.dt, ACT.Ln, bias=one_col[:, 0:1]), "D.log", u)
            d_rows(a, 0)
            for c in range(DS // NC_):
                if c + 1 < DS // NC_:
                    d_rows(a, c + 1)
                for u in LANES:
                    z = SD[u]
                    for j in range(DJ):
                        if c == 0 and j == 0:
                            a.wait_ge(*at("D.start1", u))
                        if c >= 1:
                            a.wait_ge(*at(f"D.s{c - 1}{j}", u))
                        for n in range(NC_):
                            s = NC_ * c + n
                            m = a.activation(z.dA[j][:, n, 1:S], z.dt[:, j, 1:S], ACT.Exp, scale=d_A[:, j, s:s + 1])
                            mark(a, "scalar", m, f"D.dA{c}{j}" if n == NC_ - 1 else f"D.dA{c}{j}_{n}", u)
            for u in LANES:
                norm_scalar(a, "D", u)

        def d_pool(g):
            for c in range(DS // NC_):
                for u in LANES:
                    z = SD[u]
                    g.wait_ge(*at(f"D.B{NC_ // 2 * c + NC_ // 2 - 1}", u))
                    if c == 0:
                        g.wait_ge(*at("D.dh", u))
                    for j in range(DJ):
                        if c >= 1:
                            g.wait_ge(*at(f"D.s{c - 1}{j}", u))
                        mark(g, "pool", g.tensor_tensor(z.dBu[j], over(z.dh[:, j:j + 1, :], [P, NC_, S]), z.B[c % 2], ALU.mult), f"D.dbu{c}{j}", u)

        EH, ED = 8, 64
        ET = (KV + P - 1) // P
        EL = KV - (ET - 1) * P
        CHUNKS = [(BANK * i, min(BANK, KV - BANK * i)) for i in range((KV + BANK - 1) // BANK)]
        TC = [range(4 * c, min(4 * c + 4, ET)) for c in range(4)]
        e_wq = sb("e_wq", [P, EH * ED])
        e_wkv = sb("e_wkv", [P, 2 * EH * ED])
        e_wo = sb("e_wo", [P, 4, P])
        e_go = sb("e_go", [P, P])
        e_bo = sb("e_bo", [P, P])

        c0, c1 = Carve(0), Carve(1)
        e_k = c0(4, KV)
        e_v = c0(ET, EH * ED)
        e_s = [c1(KV) for _ in range(2)]
        e_pT = c1(ET, P)
        e_neg = c1(KV)
        e_q = [c1(EH, S) for _ in LANES]
        e_o = [c1(TT, EH, ED) for _ in LANES]
        e_oT = [c1(TT, 4, P) for _ in LANES]
        e_mx = [c1(EH, TT) for _ in LANES]
        e_rs = [c1(EH, TT) for _ in LANES]
        e_mask8 = sb("e_mask8", [P, SC], U8)
        E_UNITS = [(h, i) for h in range(EH) for i in range(TT)]
        NU = len(E_UNITS)

        def erows(t):
            return EL if t == ET - 1 else P

        def e_load(sp):
            n = "L1_xattn_"
            sp.dma_start(e_wq[:, :], w[n + "w_q"]).then_inc(s_weights, 16)
            sp.dma_start(e_wkv[:, :], w[n + "w_kv"]).then_inc(s_weights, 16)
            sp.dma_start(e_wo[:, :, :], w[n + "w_out"].rearrange("(c p) n -> p c n", p=P)).then_inc(s_weights, 16)
            sp.dma_start(e_go[:, :], w[n + "g_o"].rearrange("(a n) -> a n", a=1).to_broadcast([P, P])).then_inc(s_weights, 16)
            sp.dma_start(e_bo[:, :], w[n + "b_o"].rearrange("(a n) -> a n", a=1).to_broadcast([P, P])).then_inc(s_weights, 16)

        def e_sync(sp, it):
            for u in LANES:
                if u:
                    sp.wait_ge(*at("E.neg", 0))
                sp.dma_start(e_mask8[:, :], w["mask_BxS2_bf1"][it * 2 + u].unsqueeze(0).to_broadcast([P, SC])).then_inc(s_mask[u], 16)

        def e_transposes(pe, u, o, c):
            g = 4 * o + c
            if g >= 3:
                pe.wait_ge(*at(f"E.pT{g - 3}", u))
            for t in TC[c]:
                m = pe.transpose(ps[1][0:erows(t), g % 3, P * (t % 4):P * (t % 4) + P], e_s[o % 2][:, P * t:P * t + erows(t)], ident[:, :])
            m.then_inc(*done("tensor", f"E.pT_p{g}", u))

        def e_products(pe, u, o, c):
            h, i = E_UNITS[o]
            if c == 0 and o >= 1:
                pe.wait_ge(*at(f"E.att{o - 1}", u))
            pe.wait_ge(*at(f"E.pT{4 * o + c}", u))
            for t in TC[c]:
                m = pe.matmul(ps[1][:, 3, 0:ED], e_pT[0:erows(t), t, :], e_v[0:erows(t), t, ED * h:ED * h + ED], start=t == 0, stop=t == ET - 1)
            m.then_inc(*done("tensor", f"E.o_p{o}" if c == 3 else f"E.o_p{o}.{c}", u))

        def e_tensor(pe):
            for u in LANES:
                pe.wait_ge(*at("E.l.x1", u))
                for i in range(TT):
                    m = pe.transpose(ps[u][:, 0, P * i:P * i + P], res[u][:, i, :], ident[:, :])
                m.then_inc(*done("tensor", "E.lT_p", u))
            for u in LANES:
                pe.wait_ge(*at("E.lT", u))
                for c in range(4):
                    m = pe.matmul(ps[u][:, 1 + c // 2, S * (c % 2):S * (c % 2) + S], e_wq[:, P * c:P * c + P], kvT[u][:, SC:KV], start=True, stop=True)
                m.then_inc(*done("tensor", "E.q_p", u))
            for u in LANES:
                for o in LANES:
                    pe.wait_ge(*at("E.q", o))
                    pe.wait_ge(*at("E.q2", o))
                if u:
                    pe.wait_ge(*at(f"E.att{NU - 1}", 0))
                for g in range(8):
                    b = ps[g % 2]
                    if g >= 2:
                        pe.wait_ge(*at(f"E.kv{g - 2}", u))
                    if g < 4:
                        for j, (a0, n) in enumerate(CHUNKS):
                            m = pe.matmul(b[:, j, 0:n], e_wkv[:, P * g:P * g + P], kvT[u][:, a0:a0 + n], start=True, stop=True)
                    else:
                        for t in TC[g - 4]:
                            m = pe.matmul(b[0:erows(t), t % 4, :], kvT[u][:, P * t:P * t + erows(t)], e_wkv[:, 512:1024], start=True, stop=True)
                    m.then_inc(*done("tensor", f"E.kv_p{g}", u))
                pe.wait_ge(*at("E.kv6", u))
                pe.wait_ge(*at("E.kv7", u))
                for n in range(NU + 2):
                    for j, (a0, k) in enumerate(CHUNKS if n < NU else ()):
                        h, i = E_UNITS[n]
                        if n >= 1 and j == 0:
                            pe.wait_ge(*at(f"E.max{n - 1}", u))
                        m = pe.matmul(ps[0][:, j, 0:k], e_q[u][:, h, P * i:P * i + P], e_k[:, h // 2, a0:a0 + k], start=True, stop=True)
                        if j == len(CHUNKS) - 1:
                            m.then_inc(*done("tensor", f"E.s_p{n}", u))
                        if n >= 2 and j < 2:
                            e_products(pe, u, n - 2, 2 + j)
                    if n == NU:
                        for c in range(2, 4):
                            e_products(pe, u, n - 2, c)
                    if 1 <= n < NU + 1:
                        pe.wait_ge(*at(f"E.exp{n - 1}", u))
                        for c in range(3):
                            e_transposes(pe, u, n - 1, c)
                        e_products(pe, u, n - 1, 0)
                        e_transposes(pe, u, n - 1, 3)
                        e_products(pe, u, n - 1, 1)
                    if n == NU + 1:
                        for c in range(2, 4):
                            e_products(pe, u, n - 2, c)
            for u in LANES:
                pe.wait_ge(*at(f"E.att{NU - 1}", 1))
                for i in range(TT):
                    for c in range(4):
                        m = pe.transpose(ps[u][:, 2 + i, P * c:P * c + P], e_o[u][:, i, 2 * c:2 * c + 2, :], ident[:, :])
                m.then_inc(*done("tensor", "E.oT_p", u))
            for u in LANES:
                pe.wait_ge(*at("E.oT", u))
                for i in range(TT):
                    for c in range(4):
                        m = pe.matmul(ps[u][:, 0, P * i:P * i + P], e_oT[u][:, i, c, :], e_wo[:, c, :], start=c == 0, stop=c == 3)
                m.then_inc(*done("tensor", "E.y_p", u))

        def e_kv_copy(g):
            if g < 4:
                return (P, ps[g % 2][:, :, :].rearrange("p b c -> p (b c)")[:, 0:KV], e_k[:, g, :])
            t = TC[g - 4]
            return (P, ps[g % 2][:, 0:len(t), :], e_v[:, t[0]:t[0] + len(t), :])

        def e_vector(v):
            for u in LANES:
                moments(v, "E.l", u, X[u], 1e-5)
            for u in LANES:
                norm_vector_2(v, "E.l", u, X[u], res[u])
            for u in LANES:
                v.wait_ge(*at("E.q_p", u))
                v.wait_ge(*at("E.zero", u))
                mark(v, "vector", v.tensor_scalar(e_q[u][ED:P, 1:EH:2, :], ps[u][ED:P, 1:3, :].rearrange("p a (b q) -> p (a b) q", b=2), float(ED) ** -0.5, None, ALU.mult), "E.q2", u)
            for u in LANES:
                v.wait_ge(s_mask[u], 16)
                if u == 0:
                    v.wait_ge(*at("D.x1", 1))
                    step(v, "vector", v.memset(e_neg[:, SC:KV], 0.0), "E.neg0", u)
                step(v, "vector", v.tensor_scalar(e_neg[:, 0:SC], e_mask8[:, :], -1.0, -NEG, ALU.add, ALU.mult), "E.neg", u)
                for g in range(0, 8, 2):
                    v.wait_ge(*at(f"E.kv_p{g}", u))
                    q, src, dst = e_kv_copy(g)
                    step(v, "vector", v.tensor_copy(dst, src), f"E.kv{g}", u)
                for n in range(NU + 2):
                    if n >= 2:
                        o = n - 2
                        h, i = E_UNITS[o]
                        v.wait_ge(*at(f"E.exp{o}", u))
                        step(v, "vector", v.reciprocal(e_rs[u][:, h, i:i + 1], e_rs[u][:, h, i:i + 1]), f"E.rs{o}", u)
                        v.wait_ge(*at(f"E.o_p{o}", u))
                        mark(v, "vector", v.tensor_scalar(e_o[u][:, i, h, :], ps[1][:, 3, 0:ED], e_rs[u][:, h, i:i + 1], None, ALU.mult), f"E.att{o}", u)
                    if n < NU:
                        h, i = E_UNITS[n]
                        v.wait_ge(*at(f"E.s_p{n}", u))
                        if n >= 2:
                            v.wait_ge(*at(f"E.pT_p{4 * (n - 2) + 3}", u))
                        step(v, "vector", v.tensor_tensor_reduce(out=e_s[n % 2], in0=ps[0][:, :, :].rearrange("p b c -> p (b c)")[:, 0:KV], in1=e_neg,
                                                                 scale=1.0, scalar=-3.0e38, op0=ALU.add, op1=ALU.max, accum_out=e_mx[u][:, h, i:i + 1]), f"E.max{n}", u)
                        mark(v, "vector", v.tensor_scalar(e_mx[u][:, h, i:i + 1], e_mx[u][:, h, i:i + 1], -1.0, None, ALU.mult), f"E.nmx{n}", u)
            for u in LANES:
                v.wait_ge(*at("E.oT_p", u))
                step(v, "vector", v.tensor_copy(e_oT[u].rearrange("p i c q -> p (i c q)"), ps[u][:, 2:4, :].rearrange("p a b -> p (a b)")), "E.oT", u)
            for u in LANES:
                v.wait_ge(*at("E.y_p", u))
                step(v, "vector", v.tensor_copy(res[u][:, :, :], ps[u][:, 0, 0:S].rearrange("p (i d) -> p i d", i=TT)), "E.o.y", u)
                moments(v, "E.o", u, res[u], 1e-5)
            for u in LANES:
                norm_vector_2(v, "E.o", u, res[u], res[u])
                for name, gain, op in (("go", e_go, ALU.mult), ("bo", e_bo, ALU.add)):
                    step(v, "vector", v.tensor_tensor(res[u][:, :, :], res[u][:, :, :], over(gain[:, :].unsqueeze(1), [P, TT, P]), op), f"E.{name}", u)
                norm_vector_1(v, "E", u, res[u][:, :, :])
            for u in LANES:
                norm_vector_2(v, "E", u)

        def e_scalar(a):
            for u in LANES:
                norm_scalar(a, "E.l", u)
            for u in LANES:
                a.wait_ge(*at("E.lT_p", u))
                step(a, "scalar", a.activation(kvT[u][:, SC:KV], ps[u][:, 0, 0:S], ACT.Identity, scale=e_ln[:, 2:3], bias=e_ln[:, 3:4]), "E.lT", u)
            for u in LANES:
                a.wait_ge(*at("E.q_p", u))
                a.wait_ge(*at("E.zero", u))
                mark(a, "scalar", a.activation(e_q[u][0:ED, 0:EH:2, :], ps[u][0:ED, 1:3, :].rearrange("p a (b q) -> p (a b) q", b=2), ACT.Copy, scale=float(ED) ** -0.5), "E.q", u)
            for u in LANES:
                for g in range(1, 8, 2):
                    a.wait_ge(*at(f"E.kv_p{g}", u))
                    q, src, dst = e_kv_copy(g)
                    step(a, "scalar", a.activation(dst, src, ACT.Copy), f"E.kv{g}", u)
                for n in range(NU + 1):
                    if n >= 1:
                        o = n - 1
                        for c in range(4):
                            t = TC[c]
                            a.wait_ge(*at(f"E.pT_p{4 * o + c}", u))
                            if o >= 1:
                                a.wait_ge(*at(f"E.o_p{o - 1}" if c == 3 else f"E.o_p{o - 1}.{c}", u))
                            mark(a, "scalar", a.activation(e_pT[:, t[0]:t[0] + len(t), :], ps[1][:, (4 * o + c) % 3, 0:P * len(t)].rearrange("p (t q) -> p t q", t=len(t)), ACT.Copy),
                                 f"E.pT{4 * o + c}", u)
                    if n < NU:
                        h, i = E_UNITS[n]
                        a.wait_ge(*at(f"E.nmx{n}", u))
                        mark(a, "scalar", a.activation(e_s[n % 2], e_s[n % 2], ACT.Exp, bias=e_mx[u][:, h, i:i + 1], accum_out=e_rs[u][:, h, i:i + 1]), f"E.exp{n}", u)
            for u in LANES:
                norm_scalar(a, "E.o", u)
                norm_scalar(a, "E", u)

        def e_pool(g):
            g.wait_ge(*at("D.x1", 1))
            for u in LANES:
                mark(g, "pool", g.memset(e_q[u].rearrange("p h q -> p (h q)"), 0.0), "E.zero", u)

        FE = 8
        f_wg = sb("f_wg", [P, P])
        f_bg = sb("f_bg", [1, P])
        f_we = sb("f_we", [P, FE, P])
        f_be = sb("f_be", [FE, P])
        f_order = sb("f_order", [P, P])

        class StageF:
            def __init__(self, u):
                c = Carve(u)
                self.l = c(TT, P)
                self.one = c(TT, P)
                self.m = c(TT)
                self.p = c(TT)
                self.f = c(TT)
                self.hot = c(TT, FE)
                self.hotT = c(TT, P)
                self.h = c(TT, FE, P)
                self.y = c(TT, P)

        SF = [StageF(u) for u in LANES]

        def f_load(sp):
            n = "L1_ffn_"
            sp.dma_start(f_wg[:, :], w[n + "Wg"]).then_inc(s_weights, 16)
            sp.dma_start(f_bg[:, :], w[n + "bg"].rearrange("(a n) -> a n", a=1)).then_inc(s_weights, 16)
            sp.dma_start(f_we[:, :, :], w[n + "We"].rearrange("e d f -> d e f")).then_inc(s_weights, 16)
            sp.dma_start(f_be[:, :], w[n + "be"]).then_inc(s_weights, 16)

        def f_setup_pool(g):
            g.iota(f_order[:, :], pattern=[[-1, P]], base=P, channel_multiplier=0, allow_small_or_imprecise_dtypes=True).then_inc(s_pool, 1)

        def f_tensor(pe):
            for u in LANES:
                pe.wait_ge(*at("E.x1", u))
                for i in range(TT):
                    m = pe.transpose(ps[u][:, 0, P * i:P * i + P], X[u][:, i, :], ident[:, :])
                m.then_inc(*done("tensor", "F.xT_p", u))
            for u in LANES:
                pe.wait_ge(*at("F.xT", u))
                for i in range(TT):
                    pe.matmul(ps[u][:, 1, P * i:P * i + P], XT[u][:, P * i:P * i + P], f_wg[:, :], start=True, stop=False)
                    m = pe.matmul(ps[u][:, 1, P * i:P * i + P], ones_row[:, :], f_bg[:, :], start=False, stop=True)
                m.then_inc(*done("tensor", "F.l_p", u))
            def experts(i):
                for u in LANES:
                    if i:
                        pe.wait_ge(*at("F.sel0", u))
                    for k in range(2):
                        m = pe.matmul(ps[u][:, 2 + k, :], XT[u][:, P * i:P * i + P], f_we[:, 4 * k:4 * k + 4, :], start=True, stop=True)
                    m.then_inc(*done("tensor", f"F.h_p{i}", u))

            experts(0)
            for u in LANES:
                z = SF[u]
                pe.wait_ge(*at("F.hot", u))
                for i in range(TT):
                    m = pe.transpose(ps[u][0:FE, 0, P * i:P * i + P], z.hot[:, i, :], ident[:, :])
                m.then_inc(*done("tensor", "F.hotT_p", u))
            for u in LANES:
                z = SF[u]
                pe.wait_ge(*at("F.hotT", u))
                for i in range(TT):
                    m = pe.matmul(ps[u][:, 1, P * i:P * i + P], z.hotT[0:FE, i, :], f_be[:, :], start=True, stop=True)
                m.then_inc(*done("tensor", "F.b_p", u))
            experts(1)

        def f_vector(v):
            copy_xT(v, "F")
            for u in LANES:
                z = SF[u]
                v.wait_ge(*at("F.l_p", u))
                l = ps[u][:, 1, 0:S].rearrange("p (i c) -> p i c", i=TT)
                step(v, "vector", v.tensor_reduce(z.m, l, AX.X, ALU.max), "F.max", u)
                step(v, "vector", v.tensor_tensor(z.l, l, over(z.m.unsqueeze(2), [P, TT, P]), ALU.subtract), "F.l", u)
                step(v, "vector", v.tensor_scalar(z.one, z.l, 0.0, None, ALU.is_equal), "F.one0", u)
                step(v, "vector", v.tensor_tensor(z.one, z.one, over(f_order[:, :].unsqueeze(1), [P, TT, P]), ALU.mult), "F.one1", u)
                step(v, "vector", v.tensor_reduce(z.f, z.one, AX.X, ALU.max), "F.first", u)
                step(v, "vector", v.tensor_tensor(z.one, z.one, over(z.f.unsqueeze(2), [P, TT, P]), ALU.is_equal), "F.one2", u)
                step(v, "vector", v.tensor_reduce(z.hot, z.one.rearrange("p i (g e) -> p i e g", e=FE), AX.X, ALU.add), "F.hot", u)
            for u in LANES:
                z = SF[u]
                v.wait_ge(*at("F.exp1", u))
                step(v, "vector", v.reciprocal(z.p, z.p), "F.p", u)
                v.wait_ge(*at("F.hotT_p", u))
                step(v, "vector", v.tensor_copy(z.hotT[0:FE, :, :].rearrange("p i q -> p (i q)"), ps[u][0:FE, 0, 0:S]), "F.hotT", u)
            for i in range(TT):
                for u in LANES:
                    z = SF[u]
                    v.wait_ge(*at(f"F.h_p{i}", u))
                    step(v, "vector", v.tensor_tensor(z.h[:, i, :, :], ps[u][:, 2:4, :].rearrange("p b (e f) -> p (b e) f", f=P),
                                                      over(z.hot[:, i, :].unsqueeze(2), [P, FE, P]), ALU.mult), f"F.sel{i}", u)
                    step(v, "vector", v.tensor_reduce(z.y[:, i, :], z.h[:, i, :, :].rearrange("p e f -> p f e"), AX.X, ALU.add), f"F.y{i}", u)
            for u in LANES:
                z = SF[u]
                v.wait_ge(*at("F.b_p", u))
                step(v, "vector", v.tensor_tensor(z.y, z.y, ps[u][:, 1, 0:S].rearrange("p (i f) -> p i f", i=TT), ALU.add), "F.yb", u)
                step(v, "vector", v.scalar_tensor_tensor(out=z.y, in0=z.y, scalar=0.0, in1=over(z.p.unsqueeze(2), [P, TT, P]), op0=ALU.max, op1=ALU.mult), "F.yp", u)
                norm_vector_1(v, "F", u, z.y)
            for u in LANES:
                norm_vector_2(v, "F", u)

        def f_scalar(a):
            for u in LANES:
                z = SF[u]
                a.wait_ge(*at("F.one2", u))
                for i in range(TT):
                    mark(a, "scalar", a.activation(z.l[:, i, :], z.l[:, i, :], ACT.Exp, accum_out=z.p[:, i:i + 1]), f"F.exp{i}", u)
            for u in LANES:
                norm_scalar(a, "F", u)

        def end_round(eng, engine):
            eng.drain().then_inc(s_round_done, 1)
            eng.wait_ge(s_open[engine], 1)
            eng.sem_clear(s_open[engine])

        block = ctx.enter_context(nc.Block())

        @block.sync
        def _(sp):
            a_load(sp)
            b_load(sp)
            c_load(sp)
            d_load(sp)
            e_load(sp)
            f_load(sp)
            sp.wait_ge(*at("setup.end"))
            with sp.Fori(0, rounds) as it:
                for u in LANES:
                    sp.dma_start(X[u][:, :, :], x_in[it * 2 + u]).then_inc(s_x[u], 16)
                b_sync(sp, it)
                e_sync(sp, it)
                for u in LANES:
                    sp.wait_ge(*at(f"F.x1", u))
                    sp.dma_start(x_out[it * 2 + u], X[u][:, :, :]).then_inc(s_out, 16)
                sp.wait_ge(s_round_done, 4)
                sp.wait_ge(s_out, 16 * len(LANES))
                sp.sem_clear(cleared)
                for engine in ENGINES:
                    sp.drain().then_inc(s_open[engine], 1)

        @block.gpsimd
        def _(g):
            g.memset(ident[:, :], 0.0).then_inc(s_id, 1)
            g.memset(ones_row[:, :], 1.0).then_inc(s_id, 1)
            g.memset(eps6[:, :], 1e-6).then_inc(s_id, 1)
            g.wait_ge(s_id, 3)
            g.affine_select(out=ident[:, :], in_=ident[:, :], compare_op=ALU.not_equal, fill=1.0, base=0,
                            pattern=[[-1, P]], channel_multiplier=1).then_inc(s_id, 1)
            a_setup_pool(g)
            b_setup_pool(g)
            c_setup_pool(g)
            d_setup_pool(g)
            f_setup_pool(g)
            with g.Fori(0, rounds):
                a_pool(g)
                b_pool(g)
                c_pool(g)
                d_pool(g)
                e_pool(g)
                end_round(g, "pool")

        @block.vector
        def _(v):
            v.wait_ge(s_id, 4)
            v.wait_ge(s_weights, 16 * 54)
            v.wait_ge(s_pool, 24)
            step(v, "vector", v.tensor_reduce(head_of[:, :], ident[:, :].rearrange("p (h d) -> p h d", d=8), AX.X, ALU.add), "setup.head_of")
            step(v, "vector", v.tensor_reduce(head_mod[:, :], head_of[:, :].rearrange("p (g r) -> p r g", r=4), AX.X, ALU.add), "setup.head_mod")
            step(v, "vector", v.tensor_reduce(quarter_of[:, :], head_of[:, :].rearrange("p (g r) -> p g r", r=4), AX.X, ALU.add), "setup.quarter_of")
            a_setup_vector(v)
            b_setup_vector(v)
            c_setup_vector(v)
            d_setup_vector(v)
            step(v, "vector", v.memset(lnt[0][:, :], 0.0), "setup.end")
            with v.Fori(0, rounds):
                a_vector(v)
                b_vector(v)
                c_vector(v)
                d_vector(v)
                e_vector(v)
                f_vector(v)
                end_round(v, "vector")

        @block.scalar
        def _(a):
            a.preload_act_table_set("natural_log_exp_and_others")
            d_setup_scalar(a)
            a.wait_ge(*at("setup.end"))
            with a.Fori(0, rounds):
                a_scalar(a)
                b_scalar(a)
                c_scalar(a)
                d_scalar(a)
                e_scalar(a)
                f_scalar(a)
                end_round(a, "scalar")

        @block.tensor
        def _(pe):
            pe.wait_ge(s_id, 4)
            pe.wait_ge(s_weights, 16 * 54)
            b_setup_tensor(pe)
            c_setup_tensor(pe)
            pe.wait_ge(*at("setup.end"))
            with pe.Fori(0, rounds):
                a_tensor(pe)
                b_tensor(pe)
                c_tensor(pe)
                d_tensor(pe)
                e_tensor(pe)
                f_tensor(pe)
                end_round(pe, "tensor")
        return marks


_NAMES = ['x',
          'ctx_1024',
          'mask_BxS2_bf1',
          'L0_attn_wq',
          'L0_attn_wk',
          'L0_attn_wv',
          'L0_attn_wgq',
          'L0_attn_wgk',
          'L0_attn_wgv',
          'L0_attn_r_out_w',
          'L0_attn_gate_local_w',
          'L0_attn_gate_remote_w',
          'L0_attn_w_out',
          'L0_xattn_Wq',
          'L0_xattn_Wk',
          'L0_xattn_Wv',
          'L0_xattn_gru_wih',
          'L0_xattn_gru_whh',
          'L0_xattn_gru_bih',
          'L0_xattn_gru_bhh',
          'L0_xattn_slot_norm_w',
          'L0_xattn_input_norm_w',
          'L0_ffn_Wq',
          'L0_ffn_Wk',
          'L0_ffn_Wv',
          'L0_ffn_Ws',
          'L0_ffn_Wd',
          'L0_ffn_Wo',
          'L1_attn_W_in',
          'L1_attn_b_in',
          'L1_attn_A_log',
          'L1_attn_W_B',
          'L1_attn_b_B',
          'L1_attn_W_C',
          'L1_attn_b_C',
          'L1_attn_W_delta',
          'L1_attn_b_delta',
          'L1_attn_D_param',
          'L1_attn_W_out',
          'L1_attn_b_out',
          'L1_xattn_g_x',
          'L1_xattn_b_x',
          'L1_xattn_g_l',
          'L1_xattn_b_l',
          'L1_xattn_w_q',
          'L1_xattn_w_kv',
          'L1_xattn_w_out',
          'L1_xattn_g_o',
          'L1_xattn_b_o',
          'L1_ffn_Wg',
          'L1_ffn_bg',
          'L1_ffn_We',
          'L1_ffn_be']


def kernel(**inputs):
    import numpy as _np
    import concourse.bacc as _bacc
    from concourse import mybir as _mybir
    from concourse.bass_utils import run_bass_kernel_spmd as _run

    known = None
    for _ in range(2):
        nc = _bacc.Bacc("TRN2", target_bir_lowering=False, num_devices=1)
        arrays, aps = {}, {}
        for name in _NAMES:
            a = _np.ascontiguousarray(inputs[name])
            if a.dtype == _np.bool_:
                a = a.view(_np.uint8)
            arrays[f"in_{name}"] = a
            aps[name] = nc.dram_tensor(f"in_{name}", a.shape, _mybir.dt.from_np(a.dtype), kind="ExternalInput").ap()
        out = nc.dram_tensor("out_0", (B, S, D), F32, kind="ExternalOutput").ap()
        known = build(nc, aps, out, known, B // len(LANES))
    r = _run(nc, [arrays], core_ids=[0])
    return r.results[0]["out_0"]
```

```python
import concourse.bass as bass
from concourse import mybir
from contextlib import ExitStack

F32 = mybir.dt.float32
BF16 = mybir.dt.bfloat16
U8 = mybir.dt.uint8
ACT = mybir.ActivationFunctionType
ALU = mybir.AluOpType
AX = mybir.AxisListType

B, S, D = 16, 256, 128
SC = 1601
P = 128
LANES = (0, 1)
TT = S // P
NEG = -1e30
BANK = 512


class Marks:

    def __init__(self, make, known):
        self.known = known
        self.count, self.place = {}, {}
        keys = sorted(known.count) if known else []
        self.make = make
        self.sems = {key: make("_".join(map(str, key))) for key in keys if key[0] != "setup"}
        self.round_sems = list(self.sems.values())
        self.sems.update({key: make("_".join(map(str, key))) for key in keys if key[0] == "setup"})
        self.dry = None if known else make("dry")

    def done(self, engine, name, lane=0):
        key = (name.split(".")[0], engine, lane)
        self.count[key] = self.count.get(key, 0) + 1
        assert (name, lane) not in self.place, name
        self.place[name, lane] = (key, self.count[key])
        return self.sems.get(key, self.dry), 1

    def at(self, name, lane=0):
        if self.known is None:
            return self.dry, 1
        key, value = self.known.place[name, lane]
        return self.sems[key], value


def build(nc, w, out, known, rounds):
    ctx = ExitStack()
    with ctx:
        def sb(name, shape, dt=F32):
            return ctx.enter_context(nc.sbuf_tensor(name, shape, dt))

        def sem(name):
            return ctx.enter_context(nc.semaphore(name))

        s_x = [sem(f"x_loaded{u}") for u in LANES]
        s_ctx = [sem(f"context_loaded{u}") for u in LANES]
        s_mask = [sem(f"mask_loaded{u}") for u in LANES]
        s_out = sem("x_stored")
        s_round_done = sem("round_done")
        marks = Marks(sem, known)
        round_sems = [*s_x, *s_ctx, *s_mask, s_out, s_round_done, *marks.round_sems]
        cleared = range(round_sems[0].num, round_sems[-1].num + 1)
        assert [s.num for s in round_sems] == list(cleared)
        at, done = marks.at, marks.done

        ps = [ctx.enter_context(nc.psum_tensor(f"ps{u}", [P, 4, BANK], F32)) for u in LANES]

        ident = sb("ident", [P, P])
        ones_row = sb("ones_row", [1, P])
        eps6 = sb("eps6", [P, 1])
        one_col = sb("one_col", [P, 1])
        head_of = sb("head_of", [P, 16])
        head_mod = sb("head_mod", [P, 4])
        quarter_of = sb("quarter_of", [P, 4])
        X = [sb(f"X{u}", [P, TT, P]) for u in LANES]
        XT = [sb(f"XT{u}", [P, S]) for u in LANES]
        lnt = [sb(f"lnt{u}", [P, 32]) for u in LANES]
        res = [sb(f"res{u}", [P, TT, P]) for u in LANES]
        AREA = 15760
        B_KEPT = AREA - 13 * P - 13 * (P + 1) - 260
        area = [sb(f"area{u}", [P, AREA]) for u in LANES]

        class Carve:

            def __init__(self, u, start=0):
                self.u, self.at = u, start

            def __call__(self, *shape):
                n = 1
                for s in shape:
                    n *= s
                a = area[self.u][:, self.at:self.at + n]
                self.at += n
                assert self.at <= AREA, self.at
                if len(shape) == 1:
                    return a
                names = " ".join("abcde"[:len(shape)])
                return a.rearrange(f"p ({names}) -> p {names}", **dict(zip("abcde", shape)))

        def over(ap, shape):
            return ap.to_broadcast(shape)

        WEIGHTS_LOADED = 16 * 55
        POSITIONS_MADE = 24
        s_weights = sem("weights_loaded")
        s_pool = sem("positions_made")
        s_id = sem("identity_made")
        ENGINES = ("tensor", "vector", "scalar", "pool")
        s_open = {engine: sem(f"round_open_{engine}") for engine in ENGINES}
        x_in = w["x"].rearrange("b (t p) d -> b p t d", p=P)
        x_out = out.rearrange("b (t p) d -> b p t d", p=P)

        def step(eng, engine, instruction, name, u=0):
            instruction.then_inc(*done(engine, name, u))
            eng.wait_ge(*at(name, u))

        def mark(eng, engine, instruction, name, u=0):
            instruction.then_inc(*done(engine, name, u))

        def rsqrt_newton(v, tag, u, y, x, t):
            step(v, "vector", v.scalar_tensor_tensor(out=t, in0=y, scalar=-0.5, in1=y, op0=ALU.mult, op1=ALU.mult), f"{tag}.nt0", u)
            step(v, "vector", v.tensor_tensor(t, t, x, ALU.mult), f"{tag}.nt1", u)
            step(v, "vector", v.scalar_tensor_tensor(out=y, in0=t, scalar=1.5, in1=y, op0=ALU.add, op1=ALU.mult), f"{tag}.rstd", u)

        def moments(v, tag, u, src, eps):
            st = lnt[u]
            for i in range(TT):
                mark(v, "vector", v.bn_stats(st[:, 16 + 6 * i:22 + 6 * i], src[:, i, :]), f"{tag}.st{i}", u)
            v.wait_ge(*at(f"{tag}.st{TT - 1}", u))
            v.memset(st[:, 12:14], 0.0).then_inc(*done("vector", f"{tag}.clear", u))
            for i in range(TT):
                mark(v, "vector", v.bn_aggr(st[:, 2 * i:2 * i + 2], st[:, 16 + 6 * i:22 + 6 * i]), f"{tag}.mv{i}", u)
            v.wait_ge(*at(f"{tag}.mv{TT - 1}", u))
            step(v, "vector", v.tensor_scalar(st[:, 4:6], st[:, 0:4].rearrange("p (i c) -> p c i", c=2)[:, 1, :], eps, None, ALU.add), f"{tag}.var", u)

        def norm_vector_1(v, tag, u, y):
            step(v, "vector", v.tensor_tensor(res[u][:, :, :], y, X[u][:, :, :], ALU.add), f"{tag}.res", u)
            moments(v, tag, u, res[u], 1e-5)

        def norm_scalar(a, tag, u):
            st = lnt[u]
            a.wait_ge(*at(f"{tag}.var", u))
            step(a, "scalar", a.activation(st[:, 6:8], st[:, 4:6], ACT.Ln), f"{tag}.ln", u)
            step(a, "scalar", a.activation(st[:, 8:10], st[:, 6:8], ACT.Exp, scale=-0.5), f"{tag}.power", u)

        def norm_vector_2(v, tag, u, src=None, dst=None):
            st = lnt[u]
            src = res[u] if src is None else src
            dst = X[u] if dst is None else dst
            v.wait_ge(*at(f"{tag}.power", u))
            rsqrt_newton(v, tag, u, st[:, 8:10], st[:, 4:6], st[:, 10:12])
            for i in range(TT):
                mark(v, "vector", v.tensor_scalar(dst[:, i, :], src[:, i, :], st[:, 2 * i:2 * i + 1], st[:, 8 + i:9 + i], ALU.subtract, ALU.mult),
                     f"{tag}.x{i}", u)

        AH, AHD, AW = 16, 8, 32
        LH, LN = 8, 64
        POOL = S // LN
        QT = [(0, 96, 0, 96), (96, 96, 64, 128), (160, 96, 128, 128)]
        A_SCALE = float(AHD) ** -0.5
        a_w = sb("a_w", [P, 3, P])
        a_wg = sb("a_wg", [P, 3, 64])
        a_wo = sb("a_wo", [P, P])
        a_ro = sb("a_ro", [64, P])
        a_gate = sb("a_gate", [P, 2])
        a_gates = sb("a_gates", [P, 32])
        a_mask = [sb(f"a_mask{t}", [P, P]) for t in range(3)]
        a_lmask = sb("a_lmask", [P, TT, LN])

        class StageA:
            def __init__(self, u):
                c = Carve(u)
                self.qT = c(S)
                self.qg = c(4, S)
                self.kT = c(4, S)
                self.gqT = c(S)
                self.gkT = c(4, LN)
                self.xp = c(2, LN)
                self.gv = c(4, 2, 9)
                self.v = c(3, AH, 9)
                self.s = [c(AH, P) for _ in range(2)]
                latent = Carve(u, c.at - AH * P)
                self.pT = c(AH, P)
                self.ls = latent(TT, LH, LN)
                self.lpT = latent(TT * 4, P)
                self.mx = [c(16) for _ in range(2)]
                self.lmx = c(16)
                self.rs = c(32)
                self.rem = c(TT, 64)
                self.remT = c(S)
                self.g = c(32)
                self.loc = c(AH, AHD)
                self.o = c(AH, AHD)
                self.oT = c(S)
                assert c.at <= B_KEPT

        SA = [StageA(u) for u in LANES]

        def a_load(sp):
            for i, n in enumerate(("wq", "wk", "wv")):
                sp.dma_start(a_w[:, i, :], w[f"L0_attn_{n}"]).then_inc(s_weights, 16)
            for i, n in enumerate(("wgq", "wgk", "wgv")):
                sp.dma_start(a_wg[:, i, :], w[f"L0_attn_{n}"]).then_inc(s_weights, 16)
            sp.dma_start(a_wo[:, :], w["L0_attn_w_out"]).then_inc(s_weights, 16)
            sp.dma_start(a_ro[:, :], w["L0_attn_r_out_w"]).then_inc(s_weights, 16)
            sp.dma_start(a_gate[:, 0:1], w["L0_attn_gate_local_w"].rearrange("h (d a) -> (h d) a", a=1)).then_inc(s_weights, 16)
            sp.dma_start(a_gate[:, 1:2], w["L0_attn_gate_remote_w"].rearrange("h (d a) -> (h d) a", a=1)).then_inc(s_weights, 16)

        def a_setup_pool(g):
            for t, (qs, qn, ks, kn) in enumerate(QT):
                g.memset(a_mask[t][:, :], 0.0).then_inc(s_pool, 1)
            g.memset(a_lmask[:, :, :], 0.0).then_inc(s_pool, 1)
            g.wait_ge(s_pool, 4)
            for t, (qs, qn, ks, kn) in enumerate(QT):
                m = a_mask[t][:, :]
                g.affine_select(out=m, in_=m, compare_op=ALU.is_ge, fill=NEG, base=qs - ks,
                                pattern=[[-1, P]], channel_multiplier=1).then_inc(s_pool, 1)
            g.affine_select(out=a_lmask[:, :, :], in_=a_lmask[:, :, :], compare_op=ALU.is_ge, fill=NEG, base=0,
                            pattern=[[P, TT], [-POOL, LN]], channel_multiplier=1).then_inc(s_pool, 1)
            g.wait_ge(s_pool, 8)
            for t, (qs, qn, ks, kn) in enumerate(QT):
                m = a_mask[t][:, :]
                g.affine_select(out=m, in_=m, compare_op=ALU.is_ge, fill=NEG, base=AW - 1 + ks - qs,
                                pattern=[[1, P]], channel_multiplier=-1).then_inc(s_pool, 1)

        def a_setup_vector(v):
            for i in range(2):
                step(v, "vector", v.tensor_scalar(a_gates[:, 16 * i:16 * i + 16], head_of[:, :], a_gate[:, i:i + 1], None, ALU.mult), "setup.gates%d" % i)

        def a_scores(pe, u, t):
            z = SA[u]
            qs, qn, ks, kn = QT[t]
            pe.wait_ge(*at("A.qg", u))
            if t == 0:
                pe.wait_ge(*at("A.proj", u))
                pe.wait_ge(*at("A.proj_a", u))
            else:
                pe.wait_ge(*at(f"A.oT{t - 2}" if t >= 2 else "A.remT", u))
            for g in range(4):
                m = pe.matmul(ps[u][0:qn, g, :].rearrange("p (r k) -> p r k", r=4)[:, :, 0:kn], z.qg[:, g, qs:qs + qn],
                              z.kT[:, :, ks:ks + kn], start=True, stop=True)
            m.then_inc(*done("tensor", f"A.s_p{t}", u))

        def a_tensor(pe):
            for u in LANES:
                pe.wait_ge(s_x[u], 16)
                for t in range(TT):
                    m = pe.transpose(ps[u][:, 0, P * t:P * t + P], X[u][:, t, :], ident[:, :])
                m.then_inc(*done("tensor", "A.xT_p", u))
            for u in LANES:
                z = SA[u]
                pe.wait_ge(*at("A.xp", u))
                for i in range(2):
                    pe.matmul(ps[u][:, 1, S * i:S * i + S], a_w[:, i, :], XT[u][:, :], start=True, stop=True)
                pe.matmul(ps[u][0:64, 2, 0:S], a_wg[:, 0, :], XT[u][:, :], start=True, stop=True)
                pe.matmul(ps[u][0:64, 2, 256:256 + LN], a_wg[:, 1, :], z.xp[:, 0, :], start=True, stop=True)
                pe.matmul(ps[u][:, 2, 320:384], z.xp, a_wg[:, 2, :], start=True, stop=True)
                for t, (qs, qn, ks, kn) in enumerate(QT):
                    m = pe.matmul(ps[u][0:kn, 3, P * t:P * t + P], XT[u][:, ks:ks + kn], a_w[:, 2, :], start=True, stop=True)
                m.then_inc(*done("tensor", "A.proj_p", u))
            for u in LANES:
                a_scores(pe, u, 0)
            for u in LANES:
                z = SA[u]
                pe.wait_ge(*at("A.sm0", u))
                for i in range(TT):
                    for g in range(2):
                        m = pe.matmul(ps[u][:, g, 256 * i:256 * i + 256], z.gqT[32 * g:32 * g + 32, P * i:P * i + P],
                                      z.gkT[32 * g:32 * g + 32, :, :], start=True, stop=True)
                m.then_inc(*done("tensor", "A.ls_p", u))
            for u in LANES:
                z = SA[u]
                pe.wait_ge(*at("A.lprob", u))
                for i in range(TT):
                    for c in range(4):
                        m = pe.transpose(ps[u][:, 2 + i, P * c:P * c + P], z.ls[:, i, 2 * c:2 * c + 2, :], ident[:, :])
                m.then_inc(*done("tensor", "A.lpT_p", u))
            for u in LANES:
                z = SA[u]
                pe.wait_ge(*at("A.lpT", u))
                for i in range(TT):
                    for c in range(4):
                        m = pe.matmul(ps[u][:, 0, P * i + 18 * c:P * i + 18 * c + 18], z.lpT[:, 4 * i + c, :],
                                      z.gv[:, c, :, :], start=True, stop=True)
                m.then_inc(*done("tensor", "A.rem_p", u))
            for u in LANES:
                z = SA[u]
                pe.wait_ge(*at("A.rem", u))
                m = pe.transpose(ps[u][:, 1, 0:P], z.rem, ident[:, :])
                m.then_inc(*done("tensor", "A.remT_p", u))
            for t in range(1, len(QT) + 1):
                if t < len(QT):
                    for u in LANES:
                        a_scores(pe, u, t)
                o = t - 1
                qs, qn, ks, kn = QT[o]
                for u in LANES:
                    z = SA[u]
                    pe.wait_ge(*at(f"A.sm{t}" if t < len(QT) else f"A.oT{o - 1}", u))
                    pe.wait_ge(*at(f"A.prob{o}", u))
                    for h in range(AH):
                        m = pe.transpose(ps[u][0:kn, h // 4, P * (h % 4):P * (h % 4) + qn], z.s[o % 2][0:qn, h, 0:kn], ident[0:qn, 0:qn])
                    m.then_inc(*done("tensor", f"A.pT_p{o}", u))
                for u in LANES:
                    z = SA[u]
                    pe.wait_ge(*at(f"A.pT{o}", u))
                    for h in range(AH):
                        pe.matmul(ps[u][0:qn, 0, 9 * h:9 * h + 9], z.pT[0:kn, h, 0:qn], z.v[0:kn, o, h, :], start=True, stop=True)
                    pe.matmul(ps[u][0:qn, 0, 160:192], z.qT[:, qs:qs + qn], a_gates[:, :], start=True, stop=True)
                    pe.matmul(ps[u][0:qn, 0, 256:384], z.remT[0:64, qs:qs + qn], a_ro[:, :], start=True, stop=True)\
                        .then_inc(*done("tensor", f"A.o_p{o}", u))
                for u in LANES:
                    z = SA[u]
                    pe.wait_ge(*at(f"A.o{o}", u))
                    pe.transpose(ps[u][:, 1, 0:qn], z.o[0:qn, :, :], ident[0:qn, 0:qn])\
                        .then_inc(*done("tensor", f"A.oT_p{o}", u))
            for u in LANES:
                pe.wait_ge(*at(f"A.oT{len(QT) - 1}", u))
            for u in LANES:
                z = SA[u]
                for i in range(TT):
                    m = pe.matmul(ps[u][:, 0, P * i:P * i + P], z.oT[:, P * i:P * i + P], a_wo[:, :], start=True, stop=True)
                m.then_inc(*done("tensor", "A.y_p", u))

        def a_maxima(v, u, t):
            z = SA[u]
            qs, qn, ks, kn = QT[t]
            v.wait_ge(*at(f"A.s_p{t}", u))
            if t >= 2:
                v.wait_ge(*at(f"A.pT_p{t - 2}", u))
            sc = ps[u][0:qn, :, :].rearrange("p g (r k) -> p (g r) k", k=P)[:, :, 0:kn]
            step(v, "vector", v.tensor_tensor(z.s[t % 2][0:qn, :, 0:kn], sc, over(a_mask[t][0:qn, 0:kn].unsqueeze(1), [qn, AH, kn]), ALU.add), f"A.sm{t}", u)
            mark(v, "vector", v.tensor_reduce(z.mx[t % 2][0:qn, :], z.s[t % 2][0:qn, :, 0:kn], AX.X, ALU.max), f"A.mx{t}", u)

        def a_heads(v, u, o):
            z = SA[u]
            qs, qn, ks, kn = QT[o]
            v.wait_ge(*at(f"A.o_p{o}", u))
            v.wait_ge(*at(f"A.gsig{o}", u))
            q = ps[u][0:qn, 0, 0:144].rearrange("p (h d) -> p h d", d=9)
            mark(v, "vector", v.tensor_tensor(z.o[0:qn, :, :], ps[u][0:qn, 0, 256:384].rearrange("p (h d) -> p h d", d=8),
                                              over(z.g[0:qn, 16:32].unsqueeze(2), [qn, AH, 8]), ALU.mult), f"A.orem{o}", u)
            step(v, "vector", v.reciprocal(z.rs[0:qn, 0:16].unsqueeze(2), q[:, :, 8:9]), f"A.rs{o}", u)
            step(v, "vector", v.tensor_tensor(z.rs[0:qn, 0:16], z.rs[0:qn, 0:16], z.g[0:qn, 0:16], ALU.mult), f"A.grs{o}", u)
            step(v, "vector", v.tensor_tensor(z.loc[0:qn, :, :], q[:, :, 0:8], over(z.rs[0:qn, 0:16].unsqueeze(2), [qn, AH, 8]), ALU.mult), f"A.loc{o}", u)
            mark(v, "vector", v.tensor_tensor(z.o[0:qn, :, :], z.o[0:qn, :, :], z.loc[0:qn, :, :], ALU.add), f"A.o{o}", u)

        def a_vector(v):
            for u in LANES:
                z = SA[u]
                v.wait_ge(*at("A.xT_p", u))
                step(v, "vector", v.tensor_copy(XT[u][:, :], ps[u][:, 0, 0:S]), "A.xT", u)
                step(v, "vector", v.tensor_reduce(z.xp[:, 0, :], XT[u][:, :].rearrange("p (n c) -> p n c", c=POOL), AX.X, ALU.add), "A.xp0", u)
                step(v, "vector", v.tensor_scalar(z.xp[:, 0, :], z.xp[:, 0, :], 1.0 / POOL, None, ALU.mult), "A.xp1", u)
                step(v, "vector", v.tensor_copy(z.xp[:, 1, :], z.xp[:, 0, :]), "A.xp", u)
            for u in LANES:
                z = SA[u]
                v.wait_ge(*at("A.proj_p", u))
                step(v, "vector", v.tensor_tensor(z.kT, over(ps[u][:, 1, S:2 * S].unsqueeze(1), [P, 4, S]),
                                                  over(head_mod[:, :].unsqueeze(2), [P, 4, S]), ALU.mult), "A.kT", u)
                mark(v, "vector", v.tensor_tensor(z.qg, over(ps[u][:, 1, 0:S].unsqueeze(1), [P, 4, S]),
                                                  over(quarter_of[:, :].unsqueeze(2), [P, 4, S]), ALU.mult), "A.qg", u)
                step(v, "vector", v.tensor_tensor(z.gkT[0:64, :, :], over(ps[u][0:64, 2, 256:256 + LN].unsqueeze(1), [64, 4, LN]),
                                                  over(head_mod[0:64, :].unsqueeze(2), [64, 4, LN]), ALU.mult), "A.gkT", u)
                for k in range(2):
                    src = ps[u][64 * k:64 * k + 64, 2, 320:384].rearrange("p (c e d) -> p c e d", c=4, e=2)
                    step(v, "vector", v.tensor_copy(z.gv[64 * k:64 * k + 64, :, k, 0:8], src[:, :, k, :]), f"A.gv{k}", u)
                    step(v, "vector", v.memset(z.gv[64 * k:64 * k + 64, :, k, 8:9], 1.0), f"A.gvone{k}", u)
                    step(v, "vector", v.memset(z.gv[64 * k:64 * k + 64, :, 1 - k, :], 0.0), f"A.gvnil{k}", u)
                step(v, "vector", v.memset(z.v[:, :, :, 8:9], 1.0), "A.vone", u)
                for t, (qs, qn, ks, kn) in enumerate(QT):
                    step(v, "vector", v.tensor_copy(z.v[0:kn, t, :, 0:8], ps[u][0:kn, 3, P * t:P * t + P].rearrange("p (h d) -> p h d", d=AHD)),
                         f"A.v{t}" if t < 2 else "A.proj", u)
            for u in LANES:
                a_maxima(v, u, 0)
            for u in LANES:
                z = SA[u]
                v.wait_ge(*at("A.ls_p", u))
                for i in range(TT):
                    step(v, "vector", v.tensor_tensor(
                        z.ls[:, i, :, :].rearrange("p (g r) n -> p g r n", g=2),
                        ps[u][:, 0:2, 256 * i:256 * i + 256].rearrange("p g (r n) -> p g r n", r=4),
                        over(a_lmask[:, i:i + 1, :].unsqueeze(1), [P, 2, 4, LN]), ALU.add), f"A.lsm{i}", u)
                step(v, "vector", v.tensor_reduce(z.lmx, z.ls, AX.X, ALU.max), "A.lmx", u)
                step(v, "vector", v.tensor_tensor(z.ls, z.ls, over(z.lmx.rearrange("p (i h) -> p i h", i=TT).unsqueeze(3), [P, TT, LH, LN]), ALU.subtract), "A.lsub", u)
            for u in LANES:
                z = SA[u]
                v.wait_ge(*at("A.rem_p", u))
                o = ps[u][:, 0, 0:2 * P].rearrange("p (i c) -> p i c", i=TT)[:, :, 0:72].rearrange("p i (h d) -> p i h d", d=9)
                rs = z.rs[:, 0:16].rearrange("p (i h) -> p i h", i=TT)
                step(v, "vector", v.reciprocal(rs.unsqueeze(3), o[:, :, :, 8:9]), "A.rrs", u)
                step(v, "vector", v.tensor_tensor(z.rem.rearrange("p i (h d) -> p i h d", d=8), o[:, :, :, 0:8],
                                                  over(rs.unsqueeze(3), [P, TT, LH, 8]), ALU.mult), "A.rem", u)
            for u in LANES:
                z = SA[u]
                v.wait_ge(*at("A.remT_p", u))
                step(v, "vector", v.tensor_copy(z.remT[0:64, 0:P], ps[u][0:64, 1, 0:P]), "A.remT0", u)
                step(v, "vector", v.tensor_copy(z.remT[0:64, P:S], ps[u][64:P, 1, 0:P]), "A.remT", u)
            for t in range(1, len(QT) + 1):
                if t < len(QT):
                    for u in LANES:
                        a_maxima(v, u, t)
                    b_statistics(v, t - 1)
                o = t - 1
                for u in LANES:
                    a_heads(v, u, o)
                qs, qn, ks, kn = QT[o]
                for u in LANES:
                    z = SA[u]
                    v.wait_ge(*at(f"A.oT_p{o}", u))
                    mark(v, "vector", v.tensor_copy(z.oT[:, qs:qs + qn], ps[u][:, 1, 0:qn]), f"A.oT{o}", u)
            for u in LANES:
                b_normed(v, u)
            for u in LANES:
                v.wait_ge(*at("A.y_p", u))
                norm_vector_1(v, "A", u, ps[u][:, 0, 0:S].rearrange("p (i d) -> p i d", i=TT))
            for u in LANES:
                norm_vector_2(v, "A", u)

        def a_exponentials(a, u, t):
            s = SA[u].s[t % 2][0:QT[t][1], :, 0:QT[t][3]]
            a.wait_ge(*at(f"A.ssub{t}", u))
            mark(a, "scalar", a.activation(s, s, ACT.Exp, scale=A_SCALE), f"A.prob{t}", u)

        def a_transposed(a, u, o):
            z = SA[u]
            qs, qn, ks, kn = QT[o]
            a.wait_ge(*at(f"A.pT_p{o}", u))
            src = ps[u][0:kn, :, :].rearrange("p g (r k) -> p (g r) k", k=P)[:, :, 0:qn]
            mark(a, "scalar", a.activation(z.pT[0:kn, :, 0:qn], src, ACT.Copy), f"A.pT{o}", u)

        def a_scalar(a):
            for u in LANES:
                z = SA[u]
                a.wait_ge(*at("A.proj_p", u))
                a.wait_ge(*at("A.qg", u))
                step(a, "scalar", a.activation(z.qT, ps[u][:, 1, 0:S], ACT.Copy), "A.qT", u)
                a.wait_ge(*at("A.proj", u))
                step(a, "scalar", a.activation(z.gqT[0:64, :], ps[u][0:64, 2, 0:S], ACT.Copy), "A.proj_a", u)
            for u in LANES:
                a_exponentials(a, u, 0)
            for u in LANES:
                z = SA[u]
                a.wait_ge(*at("A.lsub", u))
                step(a, "scalar", a.activation(z.ls, z.ls, ACT.Exp, scale=A_SCALE), "A.lprob", u)
            for u in LANES:
                z = SA[u]
                a.wait_ge(*at("A.lpT_p", u))
                step(a, "scalar", a.activation(z.lpT, ps[u][:, 2:4, :].rearrange("p b (c q) -> p (b c) q", c=4), ACT.Copy), "A.lpT", u)
            for t in range(1, len(QT) + 1):
                for u in LANES:
                    a_transposed(a, u, t - 1)
                    if t < len(QT):
                        a_exponentials(a, u, t)
                for u in LANES:
                    z = SA[u]
                    qn = QT[t - 1][1]
                    a.wait_ge(*at(f"A.o_p{t - 1}", u))
                    step(a, "scalar", a.activation(z.g[0:qn, :], ps[u][0:qn, 0, 160:192], ACT.Exp, scale=-1.0), f"A.gexp{t - 1}", u)
                    step(a, "scalar", a.activation(z.g[0:qn, :], z.g[0:qn, :], ACT.Ln, bias=one_col[0:qn, 0:1]), f"A.gln{t - 1}", u)
                    mark(a, "scalar", a.activation(z.g[0:qn, :], z.g[0:qn, :], ACT.Exp, scale=-1.0), f"A.gsig{t - 1}", u)
                if t < len(QT):
                    b_powers(a, t - 1)
            for u in LANES:
                norm_scalar(a, "A", u)

        def a_pool(g):
            for t, (qs, qn, ks, kn) in enumerate(QT):
                for u in LANES:
                    z = SA[u]
                    g.wait_ge(*at(f"A.mx{t}", u))
                    mark(g, "pool", g.tensor_tensor(z.s[t % 2][0:qn, :, 0:kn], z.s[t % 2][0:qn, :, 0:kn],
                                                    over(z.mx[t % 2][0:qn, :].unsqueeze(2), [qn, AH, kn]), ALU.subtract), f"A.ssub{t}", u)

        MT = (SC + P - 1) // P
        ML = SC - (MT - 1) * P
        MP = (MT + 1) // 2
        ITERS = 3
        b_w = [XT[0][:, 0:P], XT[0][:, P:S], XT[1][:, 0:P]]
        b_gw = [[X[0][:, 0, :], X[0][:, 1, :], X[1][:, 0, :]],
                [X[1][:, 1, :], res[0][:, 0, :], res[0][:, 1, :]]]
        b_hhT = sb("b_hhT", [P, 3 * P])
        c_wqT = sb("c_wqT", [P, 1024])
        b_ihT = c_wqT[:, 0:3 * P]
        b_A = sb("b_A", [P, P])
        b_C = sb("b_C", [P, 3 * P])
        b_bias = sb("b_bias", [P, 2, 3])
        b_nw = sb("b_nw", [P, 2])
        b_small = sb("b_small", [P, 8])
        b_mean = sb("b_mean", [P, P])
        e_ln = sb("e_ln", [P, 4])
        KV = SC + S
        kvT = [sb(f"kvT{u}", [P, KV]) for u in LANES]

        class StageB:
            def __init__(self, u):
                c = Carve(u, AREA - MT * P)
                self.ctx = c(MT, P)
                c = Carve(u, B_KEPT)
                self.p = c(MT, P + 1)
                self.st = c(MT, 6)
                self.vv = c(2, MT)
                self.rr = c(2, MT)
                self.t1 = c(2, MT)
                self.mean = c(MT)
                self.df = c(MT)
                assert c.at <= AREA - MT * P
                c = Carve(u)
                self.pT = c(SC)
                self.att = c(MT, S)
                self.xn = c(MT, P)
                self.pw = c(MT, P + 1)
                self.sl = c(S)
                self.sq = c(S)
                self.qk = c(S)
                self.mx = c(2 * MP)
                self.rs = c(2 * MP)
                self.rd = c(2)
                self.un = c(2, P)
                self.uT = c(S)
                self.rz = c(2 * S)
                self.n = c(S)
                self.t = c(S)
                assert c.at <= B_KEPT

        SB = [StageB(u) for u in LANES]

        def col(name):
            return w[name].rearrange("(g p) -> p g", p=P)

        def b_load(sp):
            for i, n in enumerate(("Wq", "Wk", "Wv")):
                sp.dma_start(b_w[i], w[f"L0_xattn_{n}"]).then_inc(s_weights, 16)
            for i, n in enumerate(("gru_wih", "gru_whh")):
                for g in range(3):
                    sp.dma_start(b_gw[i][g], w[f"L0_xattn_{n}"][P * g:P * g + P, :]).then_inc(s_weights, 16)
            for i, n in enumerate(("gru_bih", "gru_bhh")):
                sp.dma_start(b_bias[:, i, :], col(f"L0_xattn_{n}"), allow_slow_non_contiguous=True).then_inc(s_weights, 16)
            for i, n in enumerate(("slot_norm_w", "input_norm_w")):
                sp.dma_start(b_nw[:, i:i + 1], col(f"L0_xattn_{n}"), allow_slow_non_contiguous=True).then_inc(s_weights, 16)
            for i, n in enumerate(("g_x", "b_x", "g_l", "b_l")):
                sp.dma_start(e_ln[:, i:i + 1], col(f"L1_xattn_{n}"), allow_slow_non_contiguous=True).then_inc(s_weights, 16)

        def b_setup_pool(g):
            for u in LANES:
                g.memset(area[u][:, :], 0.0).then_inc(s_pool, 1)
            g.memset(b_mean[:, :], 1.0 / P).then_inc(s_pool, 1)

        def b_setup_tensor(pe):
            pe.matmul(ps[0][:, 0, 0:P], b_w[0], b_w[1], start=True, stop=True)
            for i in range(3):
                pe.transpose(ps[0][:, 1, P * i:P * i + P], b_gw[0][i], ident[:, :])
            for i in range(3):
                m = pe.transpose(ps[0][:, 2, P * i:P * i + P], b_gw[1][i], ident[:, :])
            m.then_inc(*done("tensor", "setup.b1_p"))
            pe.wait_ge(*at("setup.b_ihT"))
            pe.matmul(ps[0][:, 3, 0:3 * P], b_w[2], b_ihT, start=True, stop=True).then_inc(*done("tensor", "setup.b2_p"))

        def b_setup_vector(v):
            v.wait_ge(*at("setup.b1_p"))
            step(v, "vector", v.tensor_scalar(b_A[:, :], ps[0][:, 0, 0:P], b_nw[:, 0:1], None, ALU.mult), "setup.b_A")
            step(v, "vector", v.tensor_copy(b_hhT[:, :], ps[0][:, 2, 0:3 * P]), "setup.b_hhT")
            step(v, "vector", v.tensor_copy(b_ihT, ps[0][:, 1, 0:3 * P]), "setup.b_ihT")
            v.wait_ge(*at("setup.b2_p"))
            step(v, "vector", v.tensor_scalar(b_C[:, :], ps[0][:, 3, 0:3 * P], b_nw[:, 1:2], None, ALU.mult), "setup.b_C")
            step(v, "vector", v.tensor_tensor(b_small[:, 0:2], b_bias[:, 0, 0:2], b_bias[:, 1, 0:2], ALU.add), "setup.b_s0")
            step(v, "vector", v.tensor_scalar(b_small[:, 0:2], b_small[:, 0:2], -1.0, None, ALU.mult), "setup.b_s1")
            step(v, "vector", v.tensor_scalar(b_small[:, 2:3], b_bias[:, 0, 2:3], 2.0, None, ALU.mult), "setup.b_s2")
            step(v, "vector", v.tensor_scalar(b_small[:, 3:4], b_nw[:, 1:2], float(D) ** -0.5, None, ALU.mult), "setup.b_s3")

        def b_sync(sp, it):
            for u in LANES:
                src = w["ctx_1024"][it * 2 + u]
                sp.dma_start(SB[u].ctx[:, 0:MT - 1, :], src[0:P * (MT - 1), :].rearrange("(t p) d -> p t d", p=P)).then_inc(s_ctx[u], 16)
                sp.dma_start(SB[u].ctx[0:ML, MT - 1, :], src[P * (MT - 1):SC, :]).then_inc(s_ctx[u], 16)

        def rows(m):
            return ML if m == MT - 1 else P

        B_HALVES = [(r, u) for r in range(ITERS) for u in LANES] + [(ITERS, 0)]

        def b_before(r, u):
            return (r, 0) if u else (r - 1, 1)

        def b_query_tensor(pe, u, r):
            pe.wait_ge(*at("B.sl" if r == 0 else f"B.{r - 1}.sl", u))
            pe.matmul(ps[u][:, 3, S:2 * S], b_A[:, :], SB[u].sl, start=True, stop=True)
            pe.wait_ge(*at(f"B.{r}.sq", u))
            pe.matmul(ps[u][:, 3, 0:S], b_mean[:, :], SB[u].sq, start=True, stop=True).then_inc(*done("tensor", f"B.{r}.ms_p", u))

        def b_scores_tensor(pe, k, u, g):
            z = SB[u]
            if g == 0:
                pe.wait_ge(*at(f"{k}.qk", u))
            if 2 <= g < MP:
                pe.wait_ge(*at(f"{k}.att{2 * g - 3}", u))
            for m in range(2 * g, min(2 * g + 2, MT)):
                o = pe.matmul(ps[u][0:rows(m), g % 2, S * (m % 2):S * (m % 2) + S], z.pT[:, P * m:P * m + rows(m)], z.qk, start=True, stop=True)
                if m % 2 or m == MT - 1:
                    o.then_inc(*done("tensor", f"{k}.s_p{g}", u))

        def b_products_tensor(pe, k, u, g):
            z = SB[u]
            if g == MP + 1:
                pe.wait_ge(*at(f"{k}.att{MT - 1}", u))
                for j in range(2):
                    pe.matmul(ps[u][:, j, 0:S], b_hhT[:, P * j:P * j + P], z.sl, start=True, stop=False)
            if g >= 2:
                pe.wait_ge(*at(f"{k}.pw{g - 2}", u))
            for m in range(max(2 * g - 4, 0), min(2 * g - 2, MT)):
                for j in range(2):
                    o = pe.matmul(ps[u][:, 2 + j, 0:P + 1], z.att[0:rows(m), m, P * j:P * j + P], z.pw[0:rows(m), m, :],
                                  start=m == 0, stop=m == MT - 1)
            if g == MP + 1:
                o.then_inc(*done("tensor", f"{k}.u_p", u))

        def b_update_tensor(pe, r, u, g):
            if r < 0:
                return
            z = SB[u]
            k = f"B.{r}"
            if g == 0:
                pe.wait_ge(*at(f"{k}.un", u))
                for j in range(2):
                    o = pe.transpose(ps[u][:, 2, P * j:P * j + P], z.un[:, j, :], ident[:, :])
                o.then_inc(*done("tensor", f"{k}.uT_p", u))
                pe.matmul(ps[u][:, 3, S:2 * S], b_hhT[:, 2 * P:3 * P], z.sl, start=True, stop=True)
            if g == 1:
                pe.wait_ge(*at(f"{k}.uT", u))
                for j in range(2):
                    pe.matmul(ps[u][:, j, 0:S], b_C[:, P * j:P * j + P], z.uT, start=False, stop=True)
                pe.matmul(ps[u][:, 3, 0:S], b_C[:, 2 * P:3 * P], z.uT, start=True, stop=True).then_inc(*done("tensor", f"{k}.gru_p", u))
            if g == 6 and r + 1 < ITERS:
                b_query_tensor(pe, u, r + 1)

        def b_tensor(pe):
            for u in LANES:
                pe.wait_ge(*at("B.p", u))
                pe.wait_ge(*at("A.res", u))
                for m in range(MT):
                    o = pe.transpose(ps[u][:, m // 4, P * (m % 4):P * (m % 4) + rows(m)], SB[u].p[0:rows(m), m, 0:P], ident[0:rows(m), 0:rows(m)])
                o.then_inc(*done("tensor", "B.pT_p", u))
            for u in LANES:
                pe.wait_ge(*at("B.pT", u))
                pe.wait_ge(*at("A.x1", u))
                for i in range(TT):
                    o = pe.transpose(ps[u][:, 0, P * i:P * i + P], X[u][:, i, :], ident[:, :])
                o.then_inc(*done("tensor", "B.slT_p", u))
            for u in LANES:
                b_query_tensor(pe, u, 0)
            for r, u in B_HALVES:
                for g in range(MP + 2):
                    if r < ITERS:
                        b_scores_tensor(pe, f"B.{r}", u, g)
                    b_update_tensor(pe, *b_before(r, u), g)
                    if r < ITERS:
                        b_products_tensor(pe, f"B.{r}", u, g)
            for u in LANES:
                pe.wait_ge(*at(f"B.{ITERS - 1}.sl", u))
                for i in range(TT):
                    o = pe.transpose(ps[u][:, 0, P * i:P * i + P], SB[u].sl[:, P * i:P * i + P], ident[:, :])
                o.then_inc(*done("tensor", "B.y_p", u))
            for u in LANES:
                pe.wait_ge(*at("B.xn", u))
                pe.wait_ge(*at("B.res", u))
                for m in range(MT):
                    o = pe.transpose(ps[u][:, m // 4, P * (m % 4):P * (m % 4) + rows(m)], SB[u].xn[0:rows(m), m, :], ident[0:rows(m), 0:rows(m)])
                o.then_inc(*done("tensor", "B.xnT_p", u))

        def b_statistics(v, u):
            z = SB[u]
            v.wait_ge(s_ctx[u], 32)
            for m in range(MT):
                mark(v, "vector", v.bn_stats(z.st[:, m, :], z.ctx[:, m, :]), f"B.cst{m}", u)
            v.wait_ge(*at(f"B.cst{MT - 1}", u))
            me, mo, ce, co = (z.st[:, :, i] for i in (1, 4, 2, 5))
            step(v, "vector", v.tensor_tensor(z.mean, me, mo, ALU.add), "B.cmean0", u)
            step(v, "vector", v.tensor_tensor(z.df, me, mo, ALU.subtract), "B.df", u)
            step(v, "vector", v.tensor_scalar(z.mean, z.mean, 0.5, None, ALU.mult), "B.cmean", u)
            step(v, "vector", v.tensor_tensor(z.df, z.df, z.df, ALU.mult), "B.df2", u)
            step(v, "vector", v.tensor_tensor(z.vv[:, 0, :], ce, co, ALU.add), "B.cv", u)
            step(v, "vector", v.tensor_scalar(z.vv[:, 0, :], z.vv[:, 0, :], 1.0 / D, None, ALU.mult), "B.cvd", u)
            step(v, "vector", v.scalar_tensor_tensor(out=z.vv[:, 0, :], in0=z.df, scalar=0.25, in1=z.vv[:, 0, :], op0=ALU.mult, op1=ALU.add), "B.cvar", u)
            step(v, "vector", v.tensor_tensor(z.vv[:, 1, :], z.mean, z.mean, ALU.mult), "B.msq", u)
            step(v, "vector", v.tensor_tensor(z.vv[:, 1, :], z.vv[:, 1, :], z.vv[:, 0, :], ALU.add), "B.ms", u)
            step(v, "vector", v.tensor_scalar(z.vv[:, 0, :], z.vv[:, 0, :], 1e-5, None, ALU.add), "B.vare", u)
            step(v, "vector", v.tensor_scalar(z.vv[:, 1, :], z.vv[:, 1, :], 1e-6, None, ALU.add), "B.vv", u)

        def b_normed(v, u):
            z = SB[u]
            v.wait_ge(*at("B.cpower", u))
            rsqrt_newton(v, "B.c", u, z.rr, z.vv, z.t1)
            step(v, "vector", v.tensor_tensor(z.p[:, :, 0:P], z.ctx, over(z.rr[:, 1, :].unsqueeze(2), [P, MT, P]), ALU.mult), "B.p0", u)
            step(v, "vector", v.memset(z.p[:, :, P:P + 1], 1.0), "B.p", u)

        def b_vector(v):
            for u in LANES:
                v.wait_ge(*at("B.slT_p", u))
                step(v, "vector", v.tensor_copy(SB[u].sl, ps[u][:, 0, 0:S]), "B.sl", u)
            for u in LANES:
                mark(v, "vector", v.tensor_tensor(SB[u].sq, SB[u].sl, SB[u].sl, ALU.mult), "B.0.sq", u)
            for u in LANES:
                b_query_vector(v, u, 0)
            for r, u in B_HALVES:
                for g in range(MP + 2):
                    if g == 0:
                        b_update_vector(v, *b_before(r, u), 0)
                    if r < ITERS and g < MP:
                        b_maxima(v, f"B.{r}", u, g)
                    if g:
                        b_update_vector(v, *b_before(r, u), g)
                    if r < ITERS and 1 <= g <= MP:
                        b_weigh(v, f"B.{r}", u, g - 1)
            for u in LANES:
                v.wait_ge(*at("B.y_p", u))
                norm_vector_1(v, "B", u, ps[u][:, 0, 0:S].rearrange("p (i d) -> p i d", i=TT))
            for u in LANES:
                norm_vector_2(v, "B", u)

        def b_weigh(v, k, u, g):
            n = min(2, MT - 2 * g)
            q = rows(2 * g + n - 1)
            z = SB[u]
            v.wait_ge(*at(f"{k}.att{2 * g + n - 1}", u))
            step(v, "vector", v.reciprocal(z.rs[0:q, 2 * g:2 * g + n], z.rs[0:q, 2 * g:2 * g + n]), f"{k}.rs{g}", u)
            mark(v, "vector", v.tensor_tensor(z.pw[0:q, 2 * g:2 * g + n, :], z.p[0:q, 2 * g:2 * g + n, :],
                                              over(z.rs[0:q, 2 * g:2 * g + n].unsqueeze(2), [q, n, P + 1]), ALU.mult), f"{k}.pw{g}", u)

        def b_maxima(v, k, u, g):
            n = min(2, MT - 2 * g)
            q = rows(2 * g + n - 1)
            v.wait_ge(*at(f"{k}.s_p{g}", u))
            mark(v, "vector", v.tensor_reduce(SB[u].mx[0:q, 2 * g:2 * g + n], ps[u][0:q, g % 2, 0:S * n].rearrange("p (m k) -> p m k", m=n), AX.X, ALU.max, negate=True),
                 f"{k}.nmx{g}", u)

        def b_query_vector(v, u, r):
            z = SB[u]
            v.wait_ge(*at(f"B.{r}.power", u))
            mark(v, "vector", v.scalar_tensor_tensor(out=z.qk, in0=ps[u][:, 3, S:2 * S], scalar=b_small[:, 3:4], in1=z.t, op0=ALU.mult, op1=ALU.mult), f"B.{r}.qk", u)

        def b_update_vector(v, r, u, g):
            if r < 0:
                return
            z = SB[u]
            k = f"B.{r}"
            if g == 0:
                v.wait_ge(*at(f"{k}.u_p", u))
                step(v, "vector", v.tensor_scalar(z.rd, ps[u][:, 2:4, P], 1e-6, None, ALU.add), f"{k}.rd0", u)
                step(v, "vector", v.reciprocal(z.rd, z.rd), f"{k}.rd", u)
                mark(v, "vector", v.tensor_tensor(z.un, ps[u][:, 2:4, 0:P], over(z.rd.unsqueeze(2), [P, 2, P]), ALU.mult), f"{k}.un", u)
            if g == 2:
                v.wait_ge(*at(f"{k}.r", u))
                step(v, "vector", v.scalar_tensor_tensor(out=z.t, in0=ps[u][:, 3, S:2 * S], scalar=b_bias[:, 1, 2:3], in1=z.rz[:, 0:S], op0=ALU.add, op1=ALU.mult), f"{k}.t0", u)
                mark(v, "vector", v.tensor_tensor(z.t, ps[u][:, 3, 0:S], z.t, ALU.add), f"{k}.t1", u)
            if g == 4:
                v.wait_ge(*at(f"{k}.en", u))
                step(v, "vector", v.tensor_scalar(z.n, z.n, -2.0, 1.0, ALU.mult, ALU.add), f"{k}.n", u)
                step(v, "vector", v.tensor_tensor(z.t, z.sl, z.n, ALU.subtract), f"{k}.d0", u)
                v.wait_ge(*at(f"{k}.z", u))
                step(v, "vector", v.tensor_tensor(z.t, z.rz[:, S:2 * S], z.t, ALU.mult), f"{k}.d1", u)
                step(v, "vector", v.tensor_tensor(z.sl, z.n, z.t, ALU.add), f"{k}.sl", u)
                if r + 1 < ITERS:
                    mark(v, "vector", v.tensor_tensor(z.sq, z.sl, z.sl, ALU.mult), f"B.{r + 1}.sq", u)
            if g == MP + 1 and r + 1 < ITERS:
                b_query_vector(v, u, r + 1)

        def b_powers(a, u):
            z = SB[u]
            a.wait_ge(*at("B.vv", u))
            step(a, "scalar", a.activation(z.t1, z.vv, ACT.Ln), "B.cln", u)
            mark(a, "scalar", a.activation(z.rr, z.t1, ACT.Exp, scale=-0.5), "B.cpower", u)

        def b_sigmoid(a, k, u, j):
            z = SB[u]
            g = z.rz[:, S * j:S * j + S]
            name = "rz"[j]
            a.wait_ge(*at(f"{k}.gru_p", u))
            step(a, "scalar", a.activation(g, ps[u][:, j, 0:S], ACT.Exp, scale=-1.0, bias=b_small[:, j:j + 1]), f"{k}.e{name}", u)
            step(a, "scalar", a.activation(g, g, ACT.Ln, bias=one_col[:, 0:1]), f"{k}.l{name}", u)
            mark(a, "scalar", a.activation(g, g, ACT.Exp, scale=-1.0), f"{k}.{name}", u)

        def b_tanh(a, k, u):
            z = SB[u]
            a.wait_ge(*at(f"{k}.t1", u))
            step(a, "scalar", a.activation(z.n, z.t, ACT.Exp, scale=2.0, bias=b_small[:, 2:3]), f"{k}.en0", u)
            step(a, "scalar", a.activation(z.n, z.n, ACT.Ln, bias=one_col[:, 0:1]), f"{k}.ln1", u)
            mark(a, "scalar", a.activation(z.n, z.n, ACT.Exp, scale=-1.0), f"{k}.en", u)

        def b_exponentials(a, k, u, g):
            z = SB[u]
            a.wait_ge(*at(f"{k}.nmx{g}", u))
            for m in range(2 * g, min(2 * g + 2, MT)):
                q = rows(m)
                mark(a, "scalar", a.activation(z.att[0:q, m, :], ps[u][0:q, g % 2, S * (m % 2):S * (m % 2) + S], ACT.Exp,
                                               bias=z.mx[0:q, m:m + 1], accum_out=z.rs[0:q, m:m + 1]), f"{k}.att{m}", u)

        def b_query_scalar(a, u, r):
            z = SB[u]
            k = f"B.{r}"
            a.wait_ge(*at(f"{k}.ms_p", u))
            step(a, "scalar", a.activation(z.t, ps[u][:, 3, 0:S], ACT.Ln, bias=eps6[:, 0:1]), f"{k}.ln", u)
            mark(a, "scalar", a.activation(z.t, z.t, ACT.Exp, scale=-0.5), f"{k}.power", u)

        def b_update_scalar(a, r, u, g):
            if r < 0:
                return
            k = f"B.{r}"
            if g == 0:
                a.wait_ge(*at(f"{k}.uT_p", u))
                mark(a, "scalar", a.activation(SB[u].uT, ps[u][:, 2, 0:S], ACT.Copy), f"{k}.uT", u)
            if g == 1:
                b_sigmoid(a, k, u, 0)
            if g == 2:
                b_tanh(a, k, u)
            if g == 3:
                b_sigmoid(a, k, u, 1)
            if g == MP - 1 and r + 1 < ITERS:
                b_query_scalar(a, u, r + 1)

        def b_scalar(a):
            for u in LANES:
                a.wait_ge(*at("B.pT_p", u))
                mark(a, "scalar", a.activation(SB[u].pT, ps[u][:, :, :].rearrange("p b c -> p (b c)")[:, 0:SC], ACT.Copy), "B.pT", u)
            for u in LANES:
                b_query_scalar(a, u, 0)
            for r, u in B_HALVES:
                for g in range(MP):
                    if g == 0:
                        b_update_scalar(a, *b_before(r, u), 0)
                    if r < ITERS:
                        b_exponentials(a, f"B.{r}", u, g)
                    if g:
                        b_update_scalar(a, *b_before(r, u), g)
            for u in LANES:
                norm_scalar(a, "B", u)
            for u in LANES:
                a.wait_ge(*at("B.xnT_p", u))
                mark(a, "scalar", a.activation(kvT[u][:, 0:SC], ps[u][:, :, :].rearrange("p b c -> p (b c)")[:, 0:SC], ACT.Identity,
                                               scale=e_ln[:, 0:1], bias=e_ln[:, 1:2]), "B.xnT", u)

        def b_pool(g):
            for u in LANES:
                z = SB[u]
                g.wait_ge(*at("B.c.rstd", u))
                g.wait_ge(*at("A.x1", u))
                step(g, "pool", g.tensor_tensor(z.xn, z.ctx, over(z.mean.unsqueeze(2), [P, MT, P]), ALU.subtract), "B.xn0", u)
                step(g, "pool", g.tensor_tensor(z.xn, z.xn, over(z.rr[:, 0, :].unsqueeze(2), [P, MT, P]), ALU.mult), "B.xn", u)

        CH, CD, CE = 16, 64, 8
        CP = CH // 2
        c_wkT = sb("c_wkT", [P, CH * CD])
        c_wvT = sb("c_wvT", [P, CE * CD])
        c_wgT = sb("c_wgT", [P, 2 * CH * CE])
        c_woT = sb("c_woT", [P, 4, P])
        c_order = sb("c_order", [P, CE])
        cp_ = [sb(f"c_prob{i}", [P, TT, S]) for i in range(2)]
        ct_ = [sb(f"c_probT{i}", [P, TT, S]) for i in range(2)]

        class StageC:
            def __init__(self, u):
                c = Carve(u)
                self.gT = c(TT, 4, P)
                c(CP * S - TT * 4 * P)
                self.k = c(CP, S)
                self.pv = c(TT, CE, CD)
                self.v = c(TT, CH, CD)
                self.att = c(TT, CH, CD)
                self.e1 = c(2048)
                self.gate = c(TT, 2, CH, CE)
                self.k1 = c(TT, 2, CH, CE)
                self.k2 = c(TT, 2, CH, CE)
                self.ix = c(TT, 2, CH, CE)
                self.m = c(TT * 2 * CH)
                self.mix = c(TT, CH, CE)
                self.mx = c(CH, TT)
                self.rs = c(CH, TT)
                self.e2 = c(2048)
                self.prod = [self.e1, self.e2]
                self.g = self.pv

        SC_ = [StageC(u) for u in LANES]
        c_q = [area[1][:, 1024 * i:1024 * i + 1024].rearrange("p (h q) -> p h q", h=4) for i in range(2)]
        C_UNITS = [(u, h) for u in LANES for h in range(CH)]

        def c_load(sp):
            def rows_of(t):
                return t.rearrange("a b c -> (a b) c").rearrange("(g p) c -> p g c", p=P)
            def part(u, a, g):
                return kvT[u][:, a:a + g * P].rearrange("p (g c) -> p g c", g=g)
            sp.dma_start(part(0, 0, 8), rows_of(w["L0_ffn_Wq"])).then_inc(s_weights, 16)
            sp.dma_start(part(1, 0, 8), rows_of(w["L0_ffn_Wk"])).then_inc(s_weights, 16)
            sp.dma_start(part(0, 1024, 4), rows_of(w["L0_ffn_Wv"])).then_inc(s_weights, 16)
            sp.dma_start(part(0, 1536, 1), rows_of(w["L0_ffn_Ws"])).then_inc(s_weights, 16)
            sp.dma_start(part(1, 1536, 1), rows_of(w["L0_ffn_Wd"])).then_inc(s_weights, 16)
            sp.dma_start(kvT[1][:, 1024:1536].rearrange("p (e d) -> p e d", e=CE), w["L0_ffn_Wo"].rearrange("e f d -> f e d")).then_inc(s_weights, 16)

        def c_setup_pool(g):
            for e in range(CE):
                g.memset(c_order[:, e:e + 1], float(CE - e)).then_inc(s_pool, 1)

        def c_setup_tensor(pe):
            for i in range(8):
                for u in LANES:
                    m = pe.transpose(ps[1][:, 2 * u + i // 4, P * (i % 4):P * (i % 4) + P], kvT[u][:, P * i:P * i + P], ident[:, :])
            m.then_inc(*done("tensor", "setup.c1_p"))
            pe.wait_ge(*at("setup.c_wk"))
            for i in range(4):
                pe.transpose(ps[1][:, 0, P * i:P * i + P], kvT[0][:, 1024 + P * i:1024 + P * i + P], ident[:, :])
                pe.transpose(ps[1][:, 1, P * i:P * i + P], kvT[1][:, 1024 + P * i:1024 + P * i + P], ident[:, :])
            for u in LANES:
                m = pe.transpose(ps[1][:, 2, P * u:P * u + P], kvT[u][:, 1536:1536 + P], ident[:, :])
            m.then_inc(*done("tensor", "setup.c2_p"))

        def c_setup_vector(v):
            v.wait_ge(*at("setup.c1_p"))
            step(v, "vector", v.tensor_scalar(c_wqT[:, :], ps[1][:, 0:2, :].rearrange("p a b -> p (a b)"), float(CD) ** -0.5, None, ALU.mult), "setup.c_wq")
            step(v, "vector", v.tensor_copy(c_wkT[:, :], ps[1][:, 2:4, :].rearrange("p a b -> p (a b)")), "setup.c_wk")
            v.wait_ge(*at("setup.c2_p"))
            step(v, "vector", v.tensor_copy(c_wvT[:, :], ps[1][:, 0, :]), "setup.c_wv")
            step(v, "vector", v.tensor_copy(c_woT[:, :, :], ps[1][:, 1, :].rearrange("p (a b) -> p a b", a=4)), "setup.c_wo")
            step(v, "vector", v.tensor_copy(c_wgT[:, :], ps[1][:, 2, 0:2 * P]), "setup.c_wg")

        def copy_xT(v, tag):
            for u in LANES:
                v.wait_ge(*at(f"{tag}.xT_p", u))
                step(v, "vector", v.tensor_copy(XT[u][:, :], ps[u][:, 0, 0:S]), f"{tag}.xT", u)

        C_GROUPS = len(LANES) * 2 * (CH // 4)
        C_QK_AT = {4 * (m // 2 - 1) + m % 2: m for m in range(2, C_GROUPS)}

        def c_qk_tensor(pe, m):
            u, j = m // 8, m % 8 // 2
            weights = c_wqT if m % 2 == 0 else c_wkT
            if m >= 2:
                pe.wait_ge(*at(f"C.qk{m - 2}"))
            for c in range(2):
                q = pe.matmul(ps[1][:, 2 + m % 2, S * c:S * c + S], weights[:, P * (2 * j + c):P * (2 * j + c) + P], XT[u][:, :], start=True, stop=True)
            q.then_inc(*done("tensor", f"C.qk_p{m}"))

        def c_qk_scalar(a, m):
            u, j = m // 8, m % 8 // 2
            if m == 0:
                a.wait_ge(*at("C.zero"))
            a.wait_ge(*at(f"C.qk_p{m}"))
            if m % 2 == 0:
                if m >= 4:
                    a.wait_ge(*at(f"C.s_p{4 * (m // 2 - 2) + 3}"))
                for half in range(2):
                    r = CD * half
                    mark(a, "scalar", a.activation(c_q[m // 2 % 2][r:r + CD, half:4:2, :], ps[1][r:r + CD, 2, :].rearrange("p (c q) -> p c q", c=2), ACT.Copy),
                         f"C.qk{m}" if half else f"C.qka{m}")
            else:
                mark(a, "scalar", a.activation(SC_[u].k[:, 2 * j:2 * j + 2, :].rearrange("p a b -> p (a b)"), ps[1][:, 3, :], ACT.Copy), f"C.qk{m}")

        def c_pv_banks(u):
            return ps[0][:, 2:4, :] if u == 0 else ps[1][:, 0:2, :]

        def c_tensor(pe):
            for u in LANES:
                pe.wait_ge(*at("B.x1", u))
                pe.wait_ge(*at("B.xnT", u))
                for i in range(TT):
                    m = pe.transpose(ps[u][:, 0, P * i:P * i + P], X[u][:, i, :], ident[:, :])
                m.then_inc(*done("tensor", "C.xT_p", u))
            for u in LANES:
                pe.wait_ge(*at("C.xT", u))
                for i in range(TT):
                    m = pe.matmul(ps[0][:, u, S * i:S * i + S], XT[u][:, P * i:P * i + P], c_wgT[:, :], start=True, stop=True)
                m.then_inc(*done("tensor", "C.gate_p", u))
            for m in range(2):
                c_qk_tensor(pe, m)
            for u in LANES:
                for i in range(TT):
                    m = pe.matmul(c_pv_banks(u)[:, i, :], XT[u][:, P * i:P * i + P], c_wvT[:, :], start=True, stop=True)
                m.then_inc(*done("tensor", "C.pv_p", u))
            last = len(C_UNITS)
            for n in range(last + 2):
                if n < last:
                    u, h = C_UNITS[n]
                    z = SC_[u]
                    if n < 2:
                        pe.wait_ge(*at("C.gate", n))
                    if n >= 2:
                        pe.wait_ge(*at(f"C.exp{n - 2}"))
                    if h % 4 == 0:
                        pe.wait_ge(*at(f"C.qk{CH // 2 * u + 2 * (h // 4) + 1}"))
                    for i in range(TT):
                        m = pe.matmul(ps[0][:, n % 2, S * i:S * i + S], c_q[n // 4 % 2][:, h % 4, P * i:P * i + P], z.k[:, h // 2, :], start=True, stop=True)
                    m.then_inc(*done("tensor", f"C.s_p{n}"))
                if n in C_QK_AT:
                    c_qk_tensor(pe, C_QK_AT[n])
                if 1 <= n < last + 1:
                    o = n - 1
                    pe.wait_ge(*at(f"C.exp{o}"))
                    if o == 0:
                        pe.wait_ge(*at("C.pv", 0))
                    if o >= 2:
                        pe.wait_ge(*at(f"C.pT{o - 2}"))
                    for j in range(TT):
                        for i in range(TT):
                            m = pe.transpose(ps[0][:, 2 + o % 2, S * j + P * i:S * j + P * i + P], cp_[o % 2][:, i, P * j:P * j + P], ident[:, :])
                    m.then_inc(*done("tensor", f"C.pT_p{o}"))
                if n >= 2:
                    o = n - 2
                    u, h = C_UNITS[o]
                    z = SC_[u]
                    if o == 0:
                        pe.wait_ge(*at("C.pv", 1))
                    if h % 4 == 0:
                        pe.wait_ge(*at(f"C.v{2 * (h // 4) + 1}", u))
                    pe.wait_ge(*at(f"C.pT{o}"))
                    if o >= 2:
                        pe.wait_ge(*at(f"C.att{o - 2}"))
                    for i in range(TT):
                        for j in range(TT):
                            m = pe.matmul(ps[1][:, o % 2, CD * i:CD * i + CD], ct_[o % 2][:, j, P * i:P * i + P], z.v[:, j, h, :], start=j == 0, stop=j == TT - 1)
                    m.then_inc(*done("tensor", f"C.o_p{o}"))
            pe.wait_ge(*at(f"C.att{last - 1}"))
            for u in LANES:
                z = SC_[u]
                for i in range(TT):
                    pe.wait_ge(*at(f"C.g{4 * i + 3}", u))
                    for c in range(4):
                        m = pe.transpose(ps[1][:, 2 + i, P * c:P * c + P], z.g[:, i, 2 * c:2 * c + 2, :], ident[:, :])
                    m.then_inc(*done("tensor", f"C.gT_p{i}", u))
                    pe.wait_ge(*at(f"C.gT{i}", u))
                    for c in range(4):
                        m = pe.matmul(ps[1][:, u, P * i:P * i + P], z.gT[:, i, c, :], c_woT[:, c, :], start=c == 0, stop=c == 3)
                m.then_inc(*done("tensor", "C.y_p", u))

        C_PICK = 12

        def c_pick(v, u, k, i):
            z = SC_[u]
            gate, k1, k2, ix = (t[:, :, k, :, :] for t in (z.gate, z.k1, z.k2, z.ix))
            m = z.m.rearrange("p (i k h) -> p i k h", i=TT, k=2)[:, :, k, :]
            mb = over(m.unsqueeze(3), [P, TT, CH, CE])
            order = over(c_order[:, :].unsqueeze(1).unsqueeze(1), [P, TT, CH, CE])
            if i:
                v.wait_ge(*at(f"C.pick{k}{i - 1}", u))
            src, dst = (gate, k1) if i < 5 else (k2, k2)
            if i == 5:
                o = v.scalar_tensor_tensor(out=k2, in0=k1, scalar=NEG, in1=gate, op0=ALU.mult, op1=ALU.add)
            elif i == 11:
                o = v.tensor_tensor(k1, k1, k2, ALU.add)
            elif i in (0, 6):
                o = v.tensor_reduce(m, src, AX.X, ALU.max)
            elif i in (1, 7):
                o = v.tensor_tensor(ix, src, mb, ALU.is_equal)
            elif i in (2, 8):
                o = v.tensor_tensor(ix, ix, order, ALU.mult)
            elif i in (3, 9):
                o = v.tensor_reduce(m, ix, AX.X, ALU.max)
            else:
                o = v.tensor_tensor(dst, ix, mb, ALU.is_equal)
            mark(v, "vector", o, f"C.pick{k}{i}", u)

        def c_mix(v, u):
            z = SC_[u]
            v.wait_ge(*at(f"C.pick0{C_PICK - 1}", u))
            v.wait_ge(*at("C.sig", u))
            mark(v, "vector", v.tensor_tensor(z.mix, z.mix, z.k1[:, :, 0, :, :], ALU.mult), "C.mix", u)

        def c_v_vector(v, m):
            u, j, i = m // 8, m % 8 // 2, m % 2
            z = SC_[u]
            v.wait_ge(*at(f"C.prodv{m % 8}", u))
            mark(v, "vector", v.tensor_reduce(z.v[:, i, 4 * j:4 * j + 4, :], z.prod[m % 2].rearrange("p (h e d) -> p h d e", h=4, e=CE), AX.X, ALU.add),
                 f"C.v{m % 8}", u)

        C_PROD_VECTOR = (0, 4)

        def c_prod_o(u, n):
            z = SC_[u]
            if u == 1 and n in C_PROD_VECTOR:
                return z.v.rearrange("p i h d -> p (i h d)")
            if u == 1:
                n -= sum(m < n for m in C_PROD_VECTOR)
            return z.prod[n % 2]

        def c_g_vector(v, u, n):
            i, c = n // 4, n % 4
            z = SC_[u]
            v.wait_ge(*at(f"C.prodo{n}", u))
            mark(v, "vector", v.tensor_reduce(z.g[:, i, 2 * c:2 * c + 2, :], c_prod_o(u, n).rearrange("p (e h d) -> p e d h", e=2, h=CH), AX.X, ALU.add),
                 f"C.g{n}", u)

        C_V_AT = {4 * m // 3: m + 2 for m in range(C_GROUPS - 2)}
        C_G_AT = {20 + 3 * n // 2: n for n in range(8)}

        def c_prod_vector(v, u, n):
            z = SC_[u]
            i, c = n // 4, n % 4
            step(v, "vector", v.tensor_tensor(c_prod_o(u, n).rearrange("p (e h d) -> p e h d", e=2, h=CH),
                                              over(z.k1[:, i, 1, :, 2 * c:2 * c + 2].rearrange("p h e -> p e h").unsqueeze(3), [P, 2, CH, CD]),
                                              over(z.att[:, i:i + 1, :, :], [P, 2, CH, CD]), ALU.mult), f"C.prodo{n}", u)

        def c_vector(v):
            for u in LANES:
                v.wait_ge(*at("C.xT_p", u))
                mark(v, "vector", v.tensor_copy(XT[u][:, :], ps[u][:, 0, 0:S]), "C.xT", u)
            for u in LANES:
                v.wait_ge(*at("C.gate_p", u))
                step(v, "vector", v.tensor_copy(SC_[u].gate.rearrange("p i k h e -> p (i k h e)"), ps[0][:, u, :]), "C.gate", u)
            for u in LANES:
                for i in range(C_PICK):
                    c_pick(v, u, 0, i)
                c_mix(v, u)
            for m in range(2):
                c_v_vector(v, m)
            last = len(C_UNITS)
            for n in range(last + 2):
                if n < last:
                    u, h = C_UNITS[n]
                    z = SC_[u]
                    v.wait_ge(*at(f"C.s_p{n}"))
                    mark(v, "vector", v.tensor_reduce(z.mx[:, h, :], ps[0][:, n % 2, :].rearrange("p (i k) -> p i k", i=TT), AX.X, ALU.max, negate=True), f"C.nmx{n}")
                if n in C_V_AT:
                    c_v_vector(v, C_V_AT[n])
                if n < 2 * C_PICK:
                    c_pick(v, n // C_PICK, 1, n % C_PICK)
                if n in C_G_AT:
                    c_g_vector(v, 0, C_G_AT[n])
                if n >= 2:
                    o = n - 2
                    u, h = C_UNITS[o]
                    z = SC_[u]
                    v.wait_ge(*at(f"C.exp{o}"))
                    step(v, "vector", v.reciprocal(z.rs[:, h, :], z.rs[:, h, :]), f"C.rs{o}", 0)
                    v.wait_ge(*at(f"C.o_p{o}"))
                    mark(v, "vector", v.tensor_tensor(z.att[:, :, h, :], ps[1][:, o % 2, 0:TT * CD].rearrange("p (i d) -> p i d", i=TT),
                                                      over(z.rs[:, h, :].unsqueeze(2), [P, TT, CD]), ALU.mult), f"C.att{o}")
            v.wait_ge(*at(f"C.att{last - 1}"))
            for n in range(3):
                if n in C_PROD_VECTOR:
                    c_prod_vector(v, 1, n)
                c_g_vector(v, 1, n)
            v.wait_ge(*at("C.y_p", 0))
            norm_vector_1(v, "C", 0, ps[1][:, 0, 0:S].rearrange("p (i d) -> p i d", i=TT))
            for n in range(3, 6):
                if n in C_PROD_VECTOR:
                    c_prod_vector(v, 1, n)
                c_g_vector(v, 1, n)
            norm_vector_2(v, "C", 0)
            for n in range(6, 8):
                c_g_vector(v, 1, n)
            v.wait_ge(*at("C.y_p", 1))
            norm_vector_1(v, "C", 1, ps[1][:, 1, 0:S].rearrange("p (i d) -> p i d", i=TT))
            norm_vector_2(v, "C", 1)

        def c_scalar(a):
            for u in LANES:
                z = SC_[u]
                a.wait_ge(*at("C.gate", u))
                step(a, "scalar", a.activation(z.mix, z.gate[:, :, 0, :, :], ACT.Exp, scale=-1.0), "C.gexp", u)
                step(a, "scalar", a.activation(z.mix, z.mix, ACT.Ln, bias=one_col[:, 0:1]), "C.gln", u)
                mark(a, "scalar", a.activation(z.mix, z.mix, ACT.Exp, scale=-1.0), "C.sig", u)
            for m in range(2):
                c_qk_scalar(a, m)
            for u in LANES:
                a.wait_ge(*at("C.pv_p", u))
                mark(a, "scalar", a.activation(SC_[u].pv.rearrange("p i e d -> p (i e d)"), c_pv_banks(u).rearrange("p a b -> p (a b)"), ACT.Copy), "C.pv", u)
            last = len(C_UNITS)
            for n in range(last + 1):
                if n < last:
                    u, h = C_UNITS[n]
                    z = SC_[u]
                    a.wait_ge(*at(f"C.nmx{n}"))
                    if n >= 2:
                        a.wait_ge(*at(f"C.pT_p{n - 2}"))
                    for i in range(TT):
                        m = a.activation(cp_[n % 2][:, i, :], ps[0][:, n % 2, S * i:S * i + S], ACT.Exp, bias=z.mx[:, h, i:i + 1], accum_out=z.rs[:, h, i:i + 1])
                        mark(a, "scalar", m, f"C.exp{n}" if i == TT - 1 else f"C.expa{n}")
                if n in C_QK_AT:
                    c_qk_scalar(a, C_QK_AT[n])
                if n >= 1:
                    o = n - 1
                    a.wait_ge(*at(f"C.pT_p{o}"))
                    if o >= 2:
                        a.wait_ge(*at(f"C.o_p{o - 2}"))
                    mark(a, "scalar", a.activation(ct_[o % 2][:, :, :].rearrange("p j i -> p (j i)"), ps[0][:, 2 + o % 2, :], ACT.Copy), f"C.pT{o}")
            for u in LANES:
                for i in range(TT):
                    a.wait_ge(*at(f"C.gT_p{i}", u))
                    mark(a, "scalar", a.activation(SC_[u].gT[:, i, :, :].rearrange("p c q -> p (c q)"), ps[1][:, 2 + i, :], ACT.Copy), f"C.gT{i}", u)
                norm_scalar(a, "C", u)

        def c_pool(g):
            g.wait_ge(*at("B.x1", 1))
            mark(g, "pool", g.memset(area[1][:, 0:2048], 0.0), "C.zero")
            for u in LANES:
                z = SC_[u]
                g.wait_ge(*at("C.mix", u))
                g.wait_ge(*at("C.pv", u))
                for n in range(8):
                    j, i = n // 2, n % 2
                    if n >= 2:
                        g.wait_ge(*at(f"C.v{n - 2}", u))
                    mark(g, "pool", g.tensor_tensor(z.prod[n % 2].rearrange("p (h e d) -> p h e d", h=4, e=CE),
                                                    over(z.mix[:, i, 4 * j:4 * j + 4, :].unsqueeze(3), [P, 4, CE, CD]),
                                                    over(z.pv[:, i:i + 1, :, :], [P, 4, CE, CD]), ALU.mult), f"C.prodv{n}", u)
            for u in LANES:
                z = SC_[u]
                g.wait_ge(*at(f"C.att{CH * u + CH - 1}"))
                g.wait_ge(*at(f"C.pick1{C_PICK - 1}", u))
                groups = [n for n in range(8) if u == 0 or n not in C_PROD_VECTOR]
                for k, n in enumerate(groups):
                    i, c = n // 4, n % 4
                    if k >= 2:
                        g.wait_ge(*at(f"C.g{groups[k - 2]}", u))
                    mark(g, "pool", g.tensor_tensor(c_prod_o(u, n).rearrange("p (e h d) -> p e h d", e=2, h=CH),
                                                    over(z.k1[:, i, 1, :, 2 * c:2 * c + 2].rearrange("p h e -> p e h").unsqueeze(3), [P, 2, CH, CD]),
                                                    over(z.att[:, i:i + 1, :, :], [P, 2, CH, CD]), ALU.mult), f"C.prodo{n}", u)

        DI, DS, DJ = 256, 16, 2
        NC_ = 4
        SELU_L, SELU_A = 1.0507009873554805, 1.6732632423543772
        d_win = sb("d_win", [P, DI])
        d_bin = sb("d_bin", [P, DJ])
        d_A = sb("d_A", [P, DJ, DS])
        d_wbc = sb("d_wbc", [P, DJ, 2 * DS])
        d_bbc = sb("d_bbc", [2 * DS, 1])
        d_wd = sb("d_wd", [P, DJ, DI])
        d_bd = sb("d_bd", [P, DJ])
        d_D = sb("d_D", [P, DJ])
        d_wo = sb("d_wo", [P, DJ, P])
        d_bo = sb("d_bo", [1, P])
        d_pick = sb("d_pick", [96, 2 * DS])
        d_sel = sb("d_sel", [96, 2 * DS, P], BF16)
        d_bc3 = [sb(f"d_bc3{u}", [96, S], BF16) for u in LANES]

        class StageD:
            def __init__(self, u):
                c = Carve(u)
                self.h = c(DJ, S)
                self.lo = c(DJ, S)
                self.hi = c(DJ, S)
                self.a = c(DJ, S)
                self.dt = c(DJ, S)
                self.dh = c(DJ, S)
                self.bc = c(S)
                self.part = c(S)
                self.dA = [c(NC_, S) for _ in range(2)]
                self.B = [c(NC_, S) for _ in range(2)]
                self.dBu = [c(NC_, S) for _ in range(2)]
                self.s = [c(NC_, S) for _ in range(DJ)]
                self.yc = c(DJ, NC_, S)
                self.y = c(DJ, S)

        SD = [StageD(u) for u in LANES]

        def d_load(sp):
            def jp(t):
                return t.rearrange("(j p) c -> p j c", p=P)
            n = "L1_attn_"
            sp.dma_start(d_win[:, :], w[n + "W_in"]).then_inc(s_weights, 16)
            sp.dma_start(d_bin[:, :], col(n + "b_in"), allow_slow_non_contiguous=True).then_inc(s_weights, 16)
            sp.dma_start(d_A[:, :, :], jp(w[n + "A_log"])).then_inc(s_weights, 16)
            sp.dma_start(d_wbc[:, :, 0:DS], jp(w[n + "W_B"])).then_inc(s_weights, 16)
            sp.dma_start(d_wbc[:, :, DS:2 * DS], jp(w[n + "W_C"])).then_inc(s_weights, 16)
            sp.dma_start(d_bbc[0:DS, :], w[n + "b_B"].rearrange("(p a) -> p a", a=1)).then_inc(s_weights, 16)
            sp.dma_start(d_bbc[DS:2 * DS, :], w[n + "b_C"].rearrange("(p a) -> p a", a=1)).then_inc(s_weights, 16)
            sp.dma_start(d_wd[:, :, :], jp(w[n + "W_delta"])).then_inc(s_weights, 16)
            sp.dma_start(d_bd[:, :], col(n + "b_delta"), allow_slow_non_contiguous=True).then_inc(s_weights, 16)
            sp.dma_start(d_D[:, :], col(n + "D_param"), allow_slow_non_contiguous=True).then_inc(s_weights, 16)
            sp.dma_start(d_wo[:, :, :], jp(w[n + "W_out"])).then_inc(s_weights, 16)
            sp.dma_start(d_bo[:, :], w[n + "b_out"].rearrange("(a p) -> a p", a=1)).then_inc(s_weights, 16)

        def d_setup_pool(g):
            g.memset(one_col[:, :], 1.0).then_inc(s_pool, 1)

        def d_setup_scalar(a):
            a.wait_ge(s_weights, WEIGHTS_LOADED)
            step(a, "scalar", a.activation(d_A[:, :, :], d_A[:, :, :], ACT.Exp), "setup.expA")

        def d_setup_vector(v):
            v.wait_ge(*at("setup.expA"))
            step(v, "vector", v.tensor_scalar(d_A[:, :, :], d_A[:, :, :], -1.0, None, ALU.mult), "setup.A")
            step(v, "vector", v.tensor_tensor(d_pick[:, :], ident[0:96, 0:32], ident[0:96, 32:64], ALU.add), "setup.pick0")
            step(v, "vector", v.tensor_tensor(d_pick[:, :], d_pick[:, :], ident[0:96, 64:96], ALU.add), "setup.pick")
            step(v, "vector", v.tensor_copy(d_sel[:, :, :], over(d_pick[:, :].unsqueeze(2), [96, 2 * DS, P])), "setup.sel")

        def d_rows_tensor(pe, c):
            for h in range(NC_ // 2):
                for u in LANES:
                    k = NC_ // 2 * c + h
                    pe.wait_ge(*at("D.bc3" if k == 0 else f"D.B{k - 1}", u))
                    for n in range(2):
                        m = pe.matmul(ps[u][:, 0, S * n:S * n + S], d_sel[:, 2 * k + n, :], d_bc3[u][:, :], start=True, stop=True)
                    m.then_inc(*done("tensor", f"D.b_p{k}", u))

        def d_tensor(pe):
            for u in LANES:
                pe.wait_ge(*at("C.x1", u))
                for i in range(TT):
                    m = pe.transpose(ps[u][:, 0, P * i:P * i + P], X[u][:, i, :], ident[:, :])
                m.then_inc(*done("tensor", "D.xT_p", u))
            for u in LANES:
                pe.wait_ge(*at("D.xT", u))
                for j in range(DJ):
                    m = pe.matmul(ps[u][:, 1, S * j:S * j + S], d_win[:, P * j:P * j + P], XT[u][:, :], start=True, stop=True)
                m.then_inc(*done("tensor", "D.h_p", u))
            for u in LANES:
                z = SD[u]
                pe.wait_ge(*at("D.h", u))
                for k in range(DJ):
                    m = pe.matmul(ps[u][0:2 * DS, 2, 0:S], d_wbc[:, k, :], z.h[:, k, :], start=k == 0, stop=k == 1)
                m.then_inc(*done("tensor", "D.bc_p", u))
                for j in range(DJ):
                    for k in range(DJ):
                        m = pe.matmul(ps[u][:, 3, S * j:S * j + S], d_wd[:, k, P * j:P * j + P], z.h[:, k, :], start=k == 0, stop=k == 1)
                m.then_inc(*done("tensor", "D.delta_p", u))
            d_rows_tensor(pe, 0)
            for c in range(DS // NC_ + 1):
                if c + 1 < DS // NC_:
                    d_rows_tensor(pe, c + 1)
                for u in LANES:
                    pe.wait_ge(*at("D.dh" if c == 0 else f"D.yc{c - 1}1", u))
                    if c < DS // NC_:
                        for n in range(NC_):
                            m = pe.matmul(ps[u][:, 1 + n // 2, S * (n % 2):S * (n % 2) + S], d_sel[:, DS + NC_ * c + n, :], d_bc3[u][:, :], start=True, stop=True)
                        m.then_inc(*done("tensor", f"D.c_p{c}", u))
                    if c >= 1:
                        for n in range(NC_):
                            m = pe.matmul(ps[u][:, 3, :], ident[:, :], SD[u].yc[:, :, n, :], start=c == 1 and n == 0, stop=c == DS // NC_ and n == NC_ - 1)
                        m.then_inc(*done("tensor", f"D.sum_p{c - 1}", u))
            for u in LANES:
                z = SD[u]
                pe.wait_ge(*at("D.y", u))
                for i in range(TT):
                    for j in range(DJ):
                        pe.matmul(ps[u][:, 0, P * i:P * i + P], z.y[:, j, P * i:P * i + P], d_wo[:, j, :], start=j == 0, stop=False)
                    m = pe.matmul(ps[u][:, 0, P * i:P * i + P], ones_row[:, :], d_bo[:, :], start=False, stop=True)
                m.then_inc(*done("tensor", "D.y_p", u))

        def d_vector(v):
            copy_xT(v, "D")
            for u in LANES:
                z = SD[u]
                v.wait_ge(*at("D.h_p", u))
                for j in range(DJ):
                    mark(v, "vector", v.tensor_scalar(z.lo[:, j, :], ps[u][:, 1, S * j:S * j + S], d_bin[:, j:j + 1], 0.0, ALU.add, ALU.min), f"D.lo{j}", u)
                for j in range(DJ):
                    mark(v, "vector", v.tensor_scalar(z.hi[:, j, :], ps[u][:, 1, S * j:S * j + S], d_bin[:, j:j + 1], 0.0, ALU.add, ALU.max), f"D.hi{j}", u)
            for u in LANES:
                z = SD[u]
                v.wait_ge(*at("D.elo", u))
                step(v, "vector", v.tensor_scalar(z.lo, z.lo, SELU_L * SELU_A, -SELU_L * SELU_A, ALU.mult, ALU.add), "D.neg", u)
                step(v, "vector", v.scalar_tensor_tensor(out=z.h, in0=z.hi, scalar=SELU_L, in1=z.lo, op0=ALU.mult, op1=ALU.add), "D.h", u)
            for u in LANES:
                z = SD[u]
                v.wait_ge(*at("D.bc_p", u))
                r = slice(0, 2 * DS)
                step(v, "vector", v.tensor_scalar(z.bc[r, :], ps[u][r, 2, 0:S], d_bbc[:, :], None, ALU.add), "D.bc", u)
                for k in range(3):
                    step(v, "vector", v.tensor_copy(d_bc3[u][32 * k:32 * k + 32, :], z.bc[r, :]), f"D.bc3{k}" if k < 2 else "D.bc3", u)
                    if k < 2:
                        step(v, "vector", v.tensor_copy(z.part[r, :], d_bc3[u][32 * k:32 * k + 32, :]), f"D.part{k}", u)
                        step(v, "vector", v.tensor_tensor(z.bc[r, :], z.bc[r, :], z.part[r, :], ALU.subtract), f"D.rest{k}", u)
                v.wait_ge(*at("D.delta_p", u))
                for j in range(DJ):
                    mark(v, "vector", v.tensor_scalar(z.a[:, j, :], ps[u][:, 3, S * j:S * j + S], d_bd[:, j:j + 1], None, ALU.add), f"D.a{j}", u)
                v.wait_ge(*at("D.a1", u))
                mark(v, "vector", v.scalar_tensor_tensor(out=z.dt, in0=z.a, scalar=-1.0, in1=z.a, op0=ALU.mult, op1=ALU.max), "D.abs", u)
            for u in LANES:
                z = SD[u]
                v.wait_ge(*at("D.log", u))
                step(v, "vector", v.scalar_tensor_tensor(out=z.dt, in0=z.a, scalar=0.0, in1=z.dt, op0=ALU.max, op1=ALU.add), "D.dt", u)
                step(v, "vector", v.tensor_tensor(z.dh, z.dt, z.h, ALU.mult), "D.dh", u)
                for b in range(2):
                    step(v, "vector", v.memset(z.dA[b][:, :, 0:1], 0.0), f"D.start{b}", u)
            for c in range(DS // NC_):
                for u in LANES:
                    z = SD[u]
                    for j in range(DJ):
                        v.wait_ge(*at(f"D.dbu{c}{j}", u))
                        v.wait_ge(*at(f"D.dA{c}{j}", u))
                        if c >= 1:
                            v.wait_ge(*at(f"D.yc{c - 1}{j}", u))
                        mark(v, "vector", v.tensor_tensor_scan(z.s[j].rearrange("p n t -> p (n t)"), z.dA[j].rearrange("p n t -> p (n t)"),
                                                               z.dBu[j].rearrange("p n t -> p (n t)"), 0.0, ALU.mult, ALU.add), f"D.s{c}{j}", u)
                    v.wait_ge(*at(f"D.c_p{c}", u))
                    if c >= 1:
                        v.wait_ge(*at(f"D.sum_p{c - 1}", u))
                    for j in range(DJ):
                        v.wait_ge(*at(f"D.s{c}{j}", u))
                        mark(v, "vector", v.tensor_tensor(z.yc[:, j, :, :], z.s[j], ps[u][:, 1:3, :].rearrange("p b (n t) -> p (b n) t", t=S), ALU.mult), f"D.yc{c}{j}", u)
            for u in LANES:
                z = SD[u]
                v.wait_ge(*at(f"D.sum_p{DS // NC_ - 1}", u))
                for j in range(DJ):
                    mark(v, "vector", v.scalar_tensor_tensor(out=z.y[:, j, :], in0=z.h[:, j, :], scalar=d_D[:, j:j + 1], in1=ps[u][:, 3, S * j:S * j + S], op0=ALU.mult, op1=ALU.add), "D.y" if j else "D.y_", u)
            for u in LANES:
                v.wait_ge(*at("D.y_p", u))
                norm_vector_1(v, "D", u, ps[u][:, 0, 0:S].rearrange("p (i d) -> p i d", i=TT))
            for u in LANES:
                norm_vector_2(v, "D", u)

        def d_rows(a, c):
            for h in range(NC_ // 2):
                for u in LANES:
                    k = NC_ // 2 * c + h
                    a.wait_ge(*at(f"D.b_p{k}", u))
                    if c >= 2:
                        a.wait_ge(*at(f"D.dbu{c - 2}1", u))
                    mark(a, "scalar", a.activation(SD[u].B[c % 2][:, 2 * h:2 * h + 2, :].rearrange("p n t -> p (n t)"), ps[u][:, 0, :], ACT.Copy), f"D.B{k}", u)

        def d_scalar(a):
            for u in LANES:
                z = SD[u]
                a.wait_ge(*at("D.lo1", u))
                step(a, "scalar", a.activation(z.lo, z.lo, ACT.Exp), "D.elo", u)
            for u in LANES:
                z = SD[u]
                a.wait_ge(*at("D.abs", u))
                step(a, "scalar", a.activation(z.dt, z.dt, ACT.Exp, scale=-1.0), "D.eabs", u)
                step(a, "scalar", a.activation(z.dt, z.dt, ACT.Ln, bias=one_col[:, 0:1]), "D.log", u)
            d_rows(a, 0)
            for c in range(DS // NC_):
                if c + 1 < DS // NC_:
                    d_rows(a, c + 1)
                for u in LANES:
                    z = SD[u]
                    for j in range(DJ):
                        if c == 0 and j == 0:
                            a.wait_ge(*at("D.start1", u))
                        if c >= 1:
                            a.wait_ge(*at(f"D.s{c - 1}{j}", u))
                        for n in range(NC_):
                            s = NC_ * c + n
                            m = a.activation(z.dA[j][:, n, 1:S], z.dt[:, j, 1:S], ACT.Exp, scale=d_A[:, j, s:s + 1])
                            mark(a, "scalar", m, f"D.dA{c}{j}" if n == NC_ - 1 else f"D.dA{c}{j}_{n}", u)
            for u in LANES:
                norm_scalar(a, "D", u)

        def d_pool(g):
            for c in range(DS // NC_):
                for u in LANES:
                    z = SD[u]
                    g.wait_ge(*at(f"D.B{NC_ // 2 * c + NC_ // 2 - 1}", u))
                    if c == 0:
                        g.wait_ge(*at("D.dh", u))
                    for j in range(DJ):
                        if c >= 1:
                            g.wait_ge(*at(f"D.s{c - 1}{j}", u))
                        mark(g, "pool", g.tensor_tensor(z.dBu[j], over(z.dh[:, j:j + 1, :], [P, NC_, S]), z.B[c % 2], ALU.mult), f"D.dbu{c}{j}", u)

        EH, ED = 8, 64
        ET = (KV + P - 1) // P
        EL = KV - (ET - 1) * P
        CHUNKS = [(BANK * i, min(BANK, KV - BANK * i)) for i in range((KV + BANK - 1) // BANK)]
        TC = [range(4 * c, min(4 * c + 4, ET)) for c in range(4)]
        e_qk = sb("e_qk", [P, EH, P])
        e_vo = sb("e_vo", [P, EH, P])
        e_wT = kvT[0][:, 0:3 * EH * ED].rearrange("p (w n) -> p w n", w=3)
        e_wo = kvT[1][:, 0:4 * P].rearrange("p (c n) -> p c n", c=4)
        e_go = sb("e_go", [P, P])
        e_bo = sb("e_bo", [P, P])
        e_mask8 = sb("e_mask8", [P, SC], U8)

        class StageE:
            def __init__(self, u):
                c = Carve(u)
                self.kv = c(ET, P)
                self.q = c(EH, S)
                self.neg = c(KV)
                self.o = c(TT, EH, P)
                self.oT = c(TT, EH, P)
                self.mx = c(EH, TT)
                self.rs = c(EH, TT)
                if u == 0:
                    e_common.extend([c(KV), c(KV), c(ET, P)])

        e_common = []
        SE = [StageE(u) for u in LANES]
        e_s = e_common[0:2]
        e_pT = e_common[2]
        E_UNITS = [(u, h, i) for u in LANES for h in range(EH) for i in range(TT)]
        NU = len(E_UNITS)
        EC = SC // P

        def erows(t):
            return EL if t == ET - 1 else P

        def e_load(sp):
            n = "L1_xattn_"
            sp.dma_start(e_qk[:, 0:4, :], w[n + "w_q"].rearrange("p (c n) -> p c n", c=4)).then_inc(s_weights, 16)
            sp.dma_start(e_qk[:, 4:8, :], w[n + "w_kv"][:, 0:512].rearrange("p (c n) -> p c n", c=4)).then_inc(s_weights, 16)
            sp.dma_start(e_vo[:, 0:4, :], w[n + "w_kv"][:, 512:1024].rearrange("p (c n) -> p c n", c=4)).then_inc(s_weights, 16)
            sp.dma_start(e_vo[:, 4:8, :], w[n + "w_out"].rearrange("(c p) n -> p c n", p=P)).then_inc(s_weights, 16)
            sp.dma_start(e_go[:, :], w[n + "g_o"].rearrange("(a n) -> a n", a=1).to_broadcast([P, P])).then_inc(s_weights, 16)
            sp.dma_start(e_bo[:, :], w[n + "b_o"].rearrange("(a n) -> a n", a=1).to_broadcast([P, P])).then_inc(s_weights, 16)

        def e_sync(sp, it):
            for u in LANES:
                if u:
                    sp.wait_ge(*at("E.neg", 0))
                sp.dma_start(e_mask8[:, :], w["mask_BxS2_bf1"][it * 2 + u].unsqueeze(0).to_broadcast([P, SC])).then_inc(s_mask[u], 16)

        def e_setup_tensor(pe):
            pe.wait_ge(*at("setup.c_wg"))
            for c in range(4):
                pe.transpose(ps[0][:, 0, P * c:P * c + P], e_qk[:, c, :], ident[:, :])
                pe.transpose(ps[0][:, 1, P * c:P * c + P], e_qk[:, 4 + c, :], ident[:, :])
                m = pe.transpose(ps[0][:, 2, P * c:P * c + P], e_vo[:, c, :], ident[:, :])
            m.then_inc(*done("tensor", "setup.e1_p"))
            pe.wait_ge(*at("setup.e_wo"))
            for h in range(EH):
                r = slice(ED * (h % 2), ED * (h % 2) + ED)
                k = slice(P * (h // 2), P * (h // 2) + P)
                pe.matmul(ps[1][:, h % 2, k], e_wT[r, 0, k], e_wT[r, 1, k], start=True, stop=True)
                m = pe.matmul(ps[1][:, 2 + h % 2, k], e_wT[r, 2, k], e_wo[r, h // 2, :], start=True, stop=True)
            m.then_inc(*done("tensor", "setup.e2_p"))

        def e_setup_vector(v):
            v.wait_ge(*at("setup.e1_p"))
            mark(v, "vector", v.tensor_copy(e_wT, ps[0][:, 0:3, :]), "setup.e_wT")
            mark(v, "vector", v.tensor_copy(e_wo, e_vo[:, 4:8, :]), "setup.e_wo")
            v.wait_ge(*at("setup.e2_p"))
            mark(v, "vector", v.tensor_scalar(e_qk[:, :, :].rearrange("p (c r) n -> p r c n", r=2), ps[1][:, 0:2, :].rearrange("p r (c n) -> p r c n", n=P), float(ED) ** -0.5, None, ALU.mult), "setup.e_qk")
            step(v, "vector", v.tensor_copy(e_vo[:, :, :].rearrange("p (c r) n -> p r c n", r=2), ps[1][:, 2:4, :].rearrange("p r (c n) -> p r c n", n=P)), "setup.e_vo")

        def e_transposes(pe, o, c):
            g = 4 * o + c
            if g >= 3:
                pe.wait_ge(*at(f"E.pT{g - 3}"))
            for t in TC[c]:
                m = pe.transpose(ps[1][0:erows(t), g % 3, P * (t % 4):P * (t % 4) + P], e_s[o % 2][:, P * t:P * t + erows(t)], ident[:, :])
            m.then_inc(*done("tensor", f"E.pT_p{g}"))

        def e_products(pe, o, c):
            u, h, i = E_UNITS[o]
            if c == 0 and o >= 1:
                pe.wait_ge(*at(f"E.att{o - 1}"))
            pe.wait_ge(*at(f"E.pT{4 * o + c}"))
            for t in TC[c]:
                m = pe.matmul(ps[1][:, 3, 0:P], e_pT[0:erows(t), t, :], SE[u].kv[0:erows(t), t, :], start=t == 0, stop=t == ET - 1)
            m.then_inc(*done("tensor", f"E.o_p{o}" if c == 3 else f"E.o_p{o}.{c}"))

        def e_keys(pe, u, tiles):
            for t in tiles:
                b = t // 4 + 1 if t < EC else 0
                m = pe.transpose(ps[u][0:erows(t), b, P * (t % 4):P * (t % 4) + P], kvT[u][:, P * t:P * t + erows(t)], ident[:, :])
            m.then_inc(*done("tensor", f"E.kv_p{tiles[0]}", u))

        def e_tensor(pe):
            for u in LANES:
                pe.wait_ge(*at("D.res", u))
                e_keys(pe, u, range(0, EC))
            for u in LANES:
                pe.wait_ge(*at("E.l.x1", u))
                for i in range(TT):
                    m = pe.transpose(ps[u][:, 0, P * i:P * i + P], res[u][:, i, :], ident[:, :])
                m.then_inc(*done("tensor", "E.lT_p", u))
            for u in LANES:
                pe.wait_ge(*at("E.kv0", u))
                pe.wait_ge(*at("E.lT", u))
                for h in range(EH):
                    m = pe.matmul(ps[u][:, h // 2, S * (h % 2):S * (h % 2) + S], e_qk[:, h, :], kvT[u][:, SC:KV], start=True, stop=True)
                    if h == 3:
                        m.then_inc(*done("tensor", "E.q_p0", u))
                m.then_inc(*done("tensor", "E.q_p1", u))
            for u in LANES:
                pe.wait_ge(*at("E.q0", u))
                e_keys(pe, u, range(EC, ET))
            for n in range(NU + 2):
                for j, (a0, k) in enumerate(CHUNKS if n < NU else ()):
                    u, h, i = E_UNITS[n]
                    if j == 0 and n == 0:
                        pe.wait_ge(*at("E.q1", 0))
                        pe.wait_ge(*at(f"E.kv{EC}", 0))
                    if j == 0 and n >= 1:
                        pe.wait_ge(*at(f"E.max{n - 1}"))
                    m = pe.matmul(ps[0][:, j, 0:k], SE[u].q[:, h, P * i:P * i + P], kvT[u][:, a0:a0 + k], start=True, stop=True)
                    if j == len(CHUNKS) - 1:
                        m.then_inc(*done("tensor", f"E.s_p{n}"))
                    if n >= 2 and j < 2:
                        e_products(pe, n - 2, 2 + j)
                if n >= NU:
                    for c in range(2, 4):
                        e_products(pe, n - 2, c)
                if 1 <= n <= NU:
                    pe.wait_ge(*at(f"E.exp{n - 1}"))
                    if n == 1:
                        pe.wait_ge(*at("E.q1", 1))
                        pe.wait_ge(*at(f"E.kv{EC}", 1))
                    for c in range(3):
                        e_transposes(pe, n - 1, c)
                    e_products(pe, n - 1, 0)
                    e_transposes(pe, n - 1, 3)
                    e_products(pe, n - 1, 1)
            for u in LANES:
                if u == 0:
                    pe.wait_ge(*at(f"E.max{NU - 1}"))
                pe.wait_ge(*at(f"E.att{NU - 1}"))
                for i in range(TT):
                    for h in range(EH):
                        m = pe.transpose(ps[u][:, 2 * i + h // 4, P * (h % 4):P * (h % 4) + P], SE[u].o[:, i, h, :], ident[:, :])
                m.then_inc(*done("tensor", "E.oT_p", u))
            for u in LANES:
                pe.wait_ge(*at("E.oT", u))
                for i in range(TT):
                    for h in range(EH):
                        m = pe.matmul(ps[u][:, 0, P * i:P * i + P], SE[u].oT[:, i, h, :], e_vo[:, h, :], start=h == 0, stop=h == EH - 1)
                m.then_inc(*done("tensor", "E.y_p", u))

        def e_vector(v):
            for u in LANES:
                v.wait_ge(*at("D.x1", u))
                moments(v, "E.l", u, X[u], 1e-5)
            for u in LANES:
                norm_vector_2(v, "E.l", u, X[u], res[u])
            for u in LANES:
                z = SE[u]
                v.wait_ge(s_mask[u], 16)
                mark(v, "vector", v.memset(z.neg[:, SC:KV], 0.0), "E.neg0", u)
                mark(v, "vector", v.tensor_scalar(z.neg[:, 0:SC], e_mask8[:, :], -1.0, -NEG, ALU.add, ALU.mult), "E.neg", u)
                v.wait_ge(*at("E.q_p1", u))
                mark(v, "vector", v.tensor_copy(z.q[:, 4:8, :].rearrange("p h q -> p (h q)"), ps[u][:, 2:4, :].rearrange("p b c -> p (b c)")), "E.q1", u)
            for n in range(NU + 2):
                if n >= 2:
                    o = n - 2
                    u, h, i = E_UNITS[o]
                    v.wait_ge(*at(f"E.exp{o}"))
                    step(v, "vector", v.reciprocal(SE[u].rs[:, h, i:i + 1], SE[u].rs[:, h, i:i + 1]), f"E.rs{o}")
                    v.wait_ge(*at(f"E.o_p{o}"))
                    mark(v, "vector", v.tensor_scalar(SE[u].o[:, i, h, :], ps[1][:, 3, 0:P], SE[u].rs[:, h, i:i + 1], None, ALU.mult), f"E.att{o}")
                if n < NU:
                    u, h, i = E_UNITS[n]
                    z = SE[u]
                    if h == i == 0:
                        v.wait_ge(*at("E.neg", u))
                    v.wait_ge(*at(f"E.s_p{n}"))
                    if n >= 2:
                        v.wait_ge(*at(f"E.pT_p{4 * (n - 2) + 3}"))
                    step(v, "vector", v.tensor_tensor_reduce(out=e_s[n % 2], in0=ps[0][:, :, :].rearrange("p b c -> p (b c)")[:, 0:KV], in1=z.neg,
                                                             scale=1.0, scalar=-3.0e38, op0=ALU.add, op1=ALU.max, accum_out=z.mx[:, h, i:i + 1]), f"E.max{n}")
                    mark(v, "vector", v.tensor_scalar(z.mx[:, h, i:i + 1], z.mx[:, h, i:i + 1], -1.0, None, ALU.mult), f"E.nmx{n}")
            v.wait_ge(*at("E.oT_p", 1))
            mark(v, "vector", v.tensor_copy(SE[1].oT.rearrange("p i h q -> p (i h q)"), ps[1][:, :, :].rearrange("p a b -> p (a b)")), "E.oT", 1)
            for u in LANES:
                v.wait_ge(*at("E.y_p", u))
                step(v, "vector", v.tensor_copy(res[u][:, :, :], ps[u][:, 0, 0:S].rearrange("p (i d) -> p i d", i=TT)), "E.o.y", u)
                moments(v, "E.o", u, res[u], 1e-5)
            for u in LANES:
                norm_vector_2(v, "E.o", u, res[u], res[u])
                v.wait_ge(*at("E.o.x1", u))
                for name, gain, op in (("go", e_go, ALU.mult), ("bo", e_bo, ALU.add)):
                    step(v, "vector", v.tensor_tensor(res[u][:, :, :], res[u][:, :, :], over(gain[:, :].unsqueeze(1), [P, TT, P]), op), f"E.{name}", u)
                norm_vector_1(v, "E", u, res[u][:, :, :])
            for u in LANES:
                norm_vector_2(v, "E", u)

        def e_scalar(a):
            for u in LANES:
                norm_scalar(a, "E.l", u)
            for u in LANES:
                a.wait_ge(*at("E.kv_p0", u))
                mark(a, "scalar", a.activation(SE[u].kv[:, 0:EC, :], ps[u][:, 1:4, :].rearrange("p b (t n) -> p (b t) n", n=P), ACT.Copy), "E.kv0", u)
                a.wait_ge(*at("E.lT_p", u))
                mark(a, "scalar", a.activation(kvT[u][:, SC:KV], ps[u][:, 0, 0:S], ACT.Identity, scale=e_ln[:, 2:3], bias=e_ln[:, 3:4]), "E.lT", u)
            for u in LANES:
                a.wait_ge(*at("E.q_p0", u))
                mark(a, "scalar", a.activation(SE[u].q[:, 0:4, :].rearrange("p h q -> p (h q)"), ps[u][:, 0:2, :].rearrange("p b c -> p (b c)"), ACT.Copy), "E.q0", u)
            for u in LANES:
                a.wait_ge(*at(f"E.kv_p{EC}", u))
                for t in range(EC, ET):
                    mark(a, "scalar", a.activation(SE[u].kv[0:erows(t), t, :], ps[u][0:erows(t), 0, P * (t % 4):P * (t % 4) + P], ACT.Copy),
                         f"E.kv{EC}" if t == ET - 1 else f"E.kvl{t}", u)
            for n in range(NU + 1):
                if n >= 1:
                    o = n - 1
                    for c in range(4):
                        t = TC[c]
                        a.wait_ge(*at(f"E.pT_p{4 * o + c}"))
                        if o >= 1:
                            a.wait_ge(*at(f"E.o_p{o - 1}" if c == 3 else f"E.o_p{o - 1}.{c}"))
                        mark(a, "scalar", a.activation(e_pT[:, t[0]:t[0] + len(t), :], ps[1][:, (4 * o + c) % 3, 0:P * len(t)].rearrange("p (t q) -> p t q", t=len(t)), ACT.Copy),
                             f"E.pT{4 * o + c}")
                if n < NU:
                    u, h, i = E_UNITS[n]
                    z = SE[u]
                    a.wait_ge(*at(f"E.nmx{n}"))
                    mark(a, "scalar", a.activation(e_s[n % 2], e_s[n % 2], ACT.Exp, bias=z.mx[:, h, i:i + 1], accum_out=z.rs[:, h, i:i + 1]), f"E.exp{n}")
            a.wait_ge(*at("E.oT_p", 0))
            mark(a, "scalar", a.activation(SE[0].oT.rearrange("p i h q -> p (i h q)"), ps[0][:, :, :].rearrange("p a b -> p (a b)"), ACT.Copy), "E.oT", 0)
            for u in LANES:
                norm_scalar(a, "E.o", u)
                norm_scalar(a, "E", u)

        FE = 8
        f_wg = sb("f_wg", [P, P])
        f_bg = sb("f_bg", [1, P])
        f_we = sb("f_we", [P, FE, P])
        f_be = sb("f_be", [FE, P])
        f_order = sb("f_order", [P, P])

        class StageF:
            def __init__(self, u):
                c = Carve(u)
                self.l = c(TT, P)
                self.one = c(TT, P)
                self.m = c(TT)
                self.p = c(TT)
                self.f = c(TT)
                self.hot = c(TT, FE)
                self.hotT = c(TT, P)
                self.h = c(TT, FE, P)
                self.y = c(TT, P)

        SF = [StageF(u) for u in LANES]

        def f_load(sp):
            n = "L1_ffn_"
            sp.dma_start(f_wg[:, :], w[n + "Wg"]).then_inc(s_weights, 16)
            sp.dma_start(f_bg[:, :], w[n + "bg"].rearrange("(a n) -> a n", a=1)).then_inc(s_weights, 16)
            sp.dma_start(f_we[:, :, :], w[n + "We"].rearrange("e d f -> d e f")).then_inc(s_weights, 16)
            sp.dma_start(f_be[:, :], w[n + "be"]).then_inc(s_weights, 16)

        def f_setup_pool(g):
            g.iota(f_order[:, :], pattern=[[-1, P]], base=P, channel_multiplier=0, allow_small_or_imprecise_dtypes=True).then_inc(s_pool, 1)

        def f_tensor(pe):
            for u in LANES:
                pe.wait_ge(*at("E.x1", u))
                for i in range(TT):
                    m = pe.transpose(ps[u][:, 0, P * i:P * i + P], X[u][:, i, :], ident[:, :])
                m.then_inc(*done("tensor", "F.xT_p", u))
            for u in LANES:
                pe.wait_ge(*at("F.xT", u))
                for i in range(TT):
                    pe.matmul(ps[u][:, 1, P * i:P * i + P], XT[u][:, P * i:P * i + P], f_wg[:, :], start=True, stop=False)
                    m = pe.matmul(ps[u][:, 1, P * i:P * i + P], ones_row[:, :], f_bg[:, :], start=False, stop=True)
                m.then_inc(*done("tensor", "F.l_p", u))
            def experts(i):
                for u in LANES:
                    if i:
                        pe.wait_ge(*at("F.sel0", u))
                    for k in range(2):
                        m = pe.matmul(ps[u][:, 2 + k, :], XT[u][:, P * i:P * i + P], f_we[:, 4 * k:4 * k + 4, :], start=True, stop=True)
                    m.then_inc(*done("tensor", f"F.h_p{i}", u))

            experts(0)
            for u in LANES:
                z = SF[u]
                pe.wait_ge(*at("F.hot", u))
                for i in range(TT):
                    m = pe.transpose(ps[u][0:FE, 0, P * i:P * i + P], z.hot[:, i, :], ident[:, :])
                m.then_inc(*done("tensor", "F.hotT_p", u))
            for u in LANES:
                z = SF[u]
                pe.wait_ge(*at("F.hotT", u))
                for i in range(TT):
                    m = pe.matmul(ps[u][:, 1, P * i:P * i + P], z.hotT[0:FE, i, :], f_be[:, :], start=True, stop=True)
                m.then_inc(*done("tensor", "F.b_p", u))
            experts(1)

        def f_vector(v):
            copy_xT(v, "F")
            for u in LANES:
                z = SF[u]
                v.wait_ge(*at("F.l_p", u))
                l = ps[u][:, 1, 0:S].rearrange("p (i c) -> p i c", i=TT)
                step(v, "vector", v.tensor_reduce(z.m, l, AX.X, ALU.max), "F.max", u)
                step(v, "vector", v.tensor_tensor(z.l, l, over(z.m.unsqueeze(2), [P, TT, P]), ALU.subtract), "F.l", u)
                step(v, "vector", v.tensor_scalar(z.one, z.l, 0.0, None, ALU.is_equal), "F.one0", u)
                step(v, "vector", v.tensor_tensor(z.one, z.one, over(f_order[:, :].unsqueeze(1), [P, TT, P]), ALU.mult), "F.one1", u)
                step(v, "vector", v.tensor_reduce(z.f, z.one, AX.X, ALU.max), "F.first", u)
                step(v, "vector", v.tensor_tensor(z.one, z.one, over(z.f.unsqueeze(2), [P, TT, P]), ALU.is_equal), "F.one2", u)
                step(v, "vector", v.tensor_reduce(z.hot, z.one.rearrange("p i (g e) -> p i e g", e=FE), AX.X, ALU.add), "F.hot", u)
            for u in LANES:
                z = SF[u]
                v.wait_ge(*at("F.exp1", u))
                step(v, "vector", v.reciprocal(z.p, z.p), "F.p", u)
                v.wait_ge(*at("F.hotT_p", u))
                step(v, "vector", v.tensor_copy(z.hotT[0:FE, :, :].rearrange("p i q -> p (i q)"), ps[u][0:FE, 0, 0:S]), "F.hotT", u)
            for i in range(TT):
                for u in LANES:
                    z = SF[u]
                    v.wait_ge(*at(f"F.h_p{i}", u))
                    step(v, "vector", v.tensor_tensor(z.h[:, i, :, :], ps[u][:, 2:4, :].rearrange("p b (e f) -> p (b e) f", f=P),
                                                      over(z.hot[:, i, :].unsqueeze(2), [P, FE, P]), ALU.mult), f"F.sel{i}", u)
                    step(v, "vector", v.tensor_reduce(z.y[:, i, :], z.h[:, i, :, :].rearrange("p e f -> p f e"), AX.X, ALU.add), f"F.y{i}", u)
            for u in LANES:
                z = SF[u]
                v.wait_ge(*at("F.b_p", u))
                step(v, "vector", v.tensor_tensor(z.y, z.y, ps[u][:, 1, 0:S].rearrange("p (i f) -> p i f", i=TT), ALU.add), "F.yb", u)
                step(v, "vector", v.scalar_tensor_tensor(out=z.y, in0=z.y, scalar=0.0, in1=over(z.p.unsqueeze(2), [P, TT, P]), op0=ALU.max, op1=ALU.mult), "F.yp", u)
                norm_vector_1(v, "F", u, z.y)
            for u in LANES:
                norm_vector_2(v, "F", u)

        def f_scalar(a):
            for u in LANES:
                z = SF[u]
                a.wait_ge(*at("F.one2", u))
                for i in range(TT):
                    mark(a, "scalar", a.activation(z.l[:, i, :], z.l[:, i, :], ACT.Exp, accum_out=z.p[:, i:i + 1]), f"F.exp{i}", u)
            for u in LANES:
                norm_scalar(a, "F", u)

        def end_round(eng, engine):
            eng.drain().then_inc(s_round_done, 1)
            eng.wait_ge(s_open[engine], 1)
            eng.sem_clear(s_open[engine])

        block = ctx.enter_context(nc.Block())

        @block.sync
        def _(sp):
            a_load(sp)
            b_load(sp)
            c_load(sp)
            d_load(sp)
            e_load(sp)
            f_load(sp)
            sp.wait_ge(*at("setup.end"))
            with sp.Fori(0, rounds) as it:
                for u in LANES:
                    sp.dma_start(X[u][:, :, :], x_in[it * 2 + u]).then_inc(s_x[u], 16)
                b_sync(sp, it)
                e_sync(sp, it)
                for u in LANES:
                    sp.wait_ge(*at(f"F.x1", u))
                    sp.dma_start(x_out[it * 2 + u], X[u][:, :, :]).then_inc(s_out, 16)
                sp.wait_ge(s_round_done, 4)
                sp.wait_ge(s_out, 16 * len(LANES))
                sp.sem_clear(cleared)
                for engine in ENGINES:
                    sp.drain().then_inc(s_open[engine], 1)

        @block.gpsimd
        def _(g):
            g.memset(ident[:, :], 0.0).then_inc(s_id, 1)
            g.memset(ones_row[:, :], 1.0).then_inc(s_id, 1)
            g.memset(eps6[:, :], 1e-6).then_inc(s_id, 1)
            g.wait_ge(s_id, 3)
            g.affine_select(out=ident[:, :], in_=ident[:, :], compare_op=ALU.not_equal, fill=1.0, base=0,
                            pattern=[[-1, P]], channel_multiplier=1).then_inc(s_id, 1)
            a_setup_pool(g)
            b_setup_pool(g)
            c_setup_pool(g)
            d_setup_pool(g)
            f_setup_pool(g)
            with g.Fori(0, rounds):
                a_pool(g)
                b_pool(g)
                c_pool(g)
                d_pool(g)
                end_round(g, "pool")

        @block.vector
        def _(v):
            v.wait_ge(s_id, 4)
            v.wait_ge(s_weights, WEIGHTS_LOADED)
            v.wait_ge(s_pool, POSITIONS_MADE)
            step(v, "vector", v.tensor_reduce(head_of[:, :], ident[:, :].rearrange("p (h d) -> p h d", d=8), AX.X, ALU.add), "setup.head_of")
            step(v, "vector", v.tensor_reduce(head_mod[:, :], head_of[:, :].rearrange("p (g r) -> p r g", r=4), AX.X, ALU.add), "setup.head_mod")
            step(v, "vector", v.tensor_reduce(quarter_of[:, :], head_of[:, :].rearrange("p (g r) -> p g r", r=4), AX.X, ALU.add), "setup.quarter_of")
            a_setup_vector(v)
            b_setup_vector(v)
            c_setup_vector(v)
            d_setup_vector(v)
            e_setup_vector(v)
            step(v, "vector", v.memset(lnt[0][:, :], 0.0), "setup.end")
            with v.Fori(0, rounds):
                a_vector(v)
                b_vector(v)
                c_vector(v)
                d_vector(v)
                e_vector(v)
                f_vector(v)
                end_round(v, "vector")

        @block.scalar
        def _(a):
            a.preload_act_table_set("natural_log_exp_and_others")
            d_setup_scalar(a)
            a.wait_ge(*at("setup.end"))
            with a.Fori(0, rounds):
                a_scalar(a)
                b_scalar(a)
                c_scalar(a)
                d_scalar(a)
                e_scalar(a)
                f_scalar(a)
                end_round(a, "scalar")

        @block.tensor
        def _(pe):
            pe.wait_ge(s_id, 4)
            pe.wait_ge(s_weights, WEIGHTS_LOADED)
            b_setup_tensor(pe)
            c_setup_tensor(pe)
            e_setup_tensor(pe)
            pe.wait_ge(*at("setup.end"))
            with pe.Fori(0, rounds):
                a_tensor(pe)
                b_tensor(pe)
                c_tensor(pe)
                d_tensor(pe)
                e_tensor(pe)
                f_tensor(pe)
                end_round(pe, "tensor")
        return marks


_NAMES = ['x',
          'ctx_1024',
          'mask_BxS2_bf1',
          'L0_attn_wq',
          'L0_attn_wk',
          'L0_attn_wv',
          'L0_attn_wgq',
          'L0_attn_wgk',
          'L0_attn_wgv',
          'L0_attn_r_out_w',
          'L0_attn_gate_local_w',
          'L0_attn_gate_remote_w',
          'L0_attn_w_out',
          'L0_xattn_Wq',
          'L0_xattn_Wk',
          'L0_xattn_Wv',
          'L0_xattn_gru_wih',
          'L0_xattn_gru_whh',
          'L0_xattn_gru_bih',
          'L0_xattn_gru_bhh',
          'L0_xattn_slot_norm_w',
          'L0_xattn_input_norm_w',
          'L0_ffn_Wq',
          'L0_ffn_Wk',
          'L0_ffn_Wv',
          'L0_ffn_Ws',
          'L0_ffn_Wd',
          'L0_ffn_Wo',
          'L1_attn_W_in',
          'L1_attn_b_in',
          'L1_attn_A_log',
          'L1_attn_W_B',
          'L1_attn_b_B',
          'L1_attn_W_C',
          'L1_attn_b_C',
          'L1_attn_W_delta',
          'L1_attn_b_delta',
          'L1_attn_D_param',
          'L1_attn_W_out',
          'L1_attn_b_out',
          'L1_xattn_g_x',
          'L1_xattn_b_x',
          'L1_xattn_g_l',
          'L1_xattn_b_l',
          'L1_xattn_w_q',
          'L1_xattn_w_kv',
          'L1_xattn_w_out',
          'L1_xattn_g_o',
          'L1_xattn_b_o',
          'L1_ffn_Wg',
          'L1_ffn_bg',
          'L1_ffn_We',
          'L1_ffn_be']


def kernel(**inputs):
    import numpy as _np
    import concourse.bacc as _bacc
    from concourse import mybir as _mybir
    from concourse.bass_utils import run_bass_kernel_spmd as _run

    known = None
    for _ in range(2):
        nc = _bacc.Bacc("TRN2", target_bir_lowering=False, num_devices=1)
        arrays, aps = {}, {}
        for name in _NAMES:
            a = _np.ascontiguousarray(inputs[name])
            if a.dtype == _np.bool_:
                a = a.view(_np.uint8)
            arrays[f"in_{name}"] = a
            aps[name] = nc.dram_tensor(f"in_{name}", a.shape, _mybir.dt.from_np(a.dtype), kind="ExternalInput").ap()
        out = nc.dram_tensor("out_0", (B, S, D), F32, kind="ExternalOutput").ap()
        known = build(nc, aps, out, known, B // len(LANES))
    r = _run(nc, [arrays], core_ids=[0])
    return r.results[0]["out_0"]
```
